# Optimizing a Trainium2 kernel written in Bass

```python
import numpy as np
import jax
import jax.numpy as jnp

def _softmax(x, axis=-1):
    return jax.nn.softmax(x, axis=axis)

def _gelu(x):
    return jax.nn.gelu(x, approximate=True)

def _silu(x):
    return jax.nn.silu(x)

def _sigmoid(x):
    return jax.nn.sigmoid(x)

def _layernorm(x, axis=-1, eps=1e-05):
    m = jnp.mean(x, axis=axis, keepdims=True)
    v = jnp.var(x, axis=axis, keepdims=True)
    return (x - m) / jnp.sqrt(v + eps)

def _scatter_add(tgt, idx, src, axis=0):
    return tgt.at[idx].add(src)

def _segment_sum(src, seg, n):
    return jax.ops.segment_sum(src, seg, n)
kernel_name = 'mk_vit_tower_d4_tok_img768_r4_55145c'

def setup_inputs(seed: int=0):
    np.random.seed(seed)
    _w = jnp.asarray

    def _rec_inputs():
        import jax
        import jax.numpy as jnp
        _rk = jax.random.key(seed)
        x = -0.00016672 + 0.999947 * jax.random.normal(jax.random.fold_in(_rk, 1), (16, 3, 128, 128), jnp.float32)
        return x
    x = _rec_inputs()

    def _L0_tok_setup():
        import jax, jax.numpy as jnp
        import numpy as np
        PATCH = 16
        CHANNELS = 3
        EMBED = 192
        key = jax.random.key(seed)
        kx, kw, kb = jax.random.split(key, 3)
        B, C, H, W = (64, CHANNELS, 96, 96)
        x = jax.random.normal(kx, (B, C, H, W), dtype=jnp.float32)
        fan_in = C * PATCH * PATCH
        bound = 1.0 / np.sqrt(fan_in)
        weight = jax.random.uniform(kw, (EMBED, fan_in), dtype=jnp.float32, minval=-bound, maxval=bound)
        bias = jax.random.uniform(kb, (EMBED,), dtype=jnp.float32, minval=-bound, maxval=bound)
        return {'x': x, 'weight': weight, 'bias': bias}
    _L0_tok_all = _L0_tok_setup()
    _L0_tok_in = {k: v for k, v in _L0_tok_all.items() if k in ('weight', 'bias')}
    del _L0_tok_all

    def _L0_attn_setup():
        import math
        import jax, jax.numpy as jnp
        import numpy as np
        B, N, D_IN, D_OUT = (8, 512, 192, 192)
        key = jax.random.key(seed)
        k1, k2, k3 = jax.random.split(key, 3)
        x = jax.random.normal(k1, (B, N, D_IN), dtype=jnp.float32)
        W_qkv = jax.random.normal(k2, (D_IN, 3 * D_OUT), dtype=jnp.float32) * (1.0 / math.sqrt(D_IN))
        b_qkv = jax.random.normal(k3, (3 * D_OUT,), dtype=jnp.float32) * 0.02
        return {'x': x, 'W_qkv': W_qkv, 'b_qkv': b_qkv}
    _L0_attn_all = _L0_attn_setup()
    _L0_attn_in = {k: v for k, v in _L0_attn_all.items() if k in ('W_qkv', 'b_qkv')}
    del _L0_attn_all

    def _L0_ffn_setup():
        import jax, jax.numpy as jnp
        import numpy as np
        SEQ, BATCH, EMBED = (256, 2, 192)
        E = 16
        FFN_H = 384
        K_SHARED = 1
        K_ROUTE = 3
        LN_EPS = 1e-05
        NEG_INF = -1000000000.0
        key = jax.random.key(seed)
        ks = jax.random.split(key, 4)
        x = jax.random.normal(ks[0], (SEQ, BATCH, EMBED), dtype=jnp.float32)
        gate_w = jax.random.normal(ks[1], (EMBED, E), dtype=jnp.float32) * 0.02
        gate_b = jnp.zeros((E,), jnp.float32)
        fc1_w = jax.random.normal(ks[2], (E, EMBED, FFN_H), dtype=jnp.float32) * 0.02
        fc1_b = jnp.zeros((E, FFN_H), jnp.float32)
        ln_w = jnp.ones((E, FFN_H), jnp.float32)
        ln_b = jnp.zeros((E, FFN_H), jnp.float32)
        fc2_w = jax.random.normal(ks[3], (E, FFN_H, EMBED), dtype=jnp.float32) * 0.02
        fc2_b = jnp.zeros((E, EMBED), jnp.float32)
        return {'x': x, 'gate_w': gate_w, 'gate_b': gate_b, 'fc1_w': fc1_w, 'fc1_b': fc1_b, 'ln_w': ln_w, 'ln_b': ln_b, 'fc2_w': fc2_w, 'fc2_b': fc2_b}
    _L0_ffn_all = _L0_ffn_setup()
    _L0_ffn_in = {k: v for k, v in _L0_ffn_all.items() if k in ('gate_w', 'gate_b', 'fc1_w', 'fc1_b', 'ln_w', 'ln_b', 'fc2_w', 'fc2_b')}
    del _L0_ffn_all

    def _L1_attn_setup():
        import jax, jax.numpy as jnp
        import numpy as np
        N_HEADS = 12
        NEG_BIG = 10000000000.0
        key = jax.random.key(seed)
        ks = jax.random.split(key, 5)
        nb, ns, nf = (4, 512, 192)
        return {'x': jax.random.normal(ks[0], (nb, ns, nf), dtype=jnp.float32), 'Wqkv_w': jax.random.normal(ks[1], (3 * nf, nf), dtype=jnp.float32) * 0.02, 'Wqkv_b': jax.random.normal(ks[2], (3 * nf,), dtype=jnp.float32) * 0.02, 'Wproj_w': jax.random.normal(ks[3], (nf, nf), dtype=jnp.float32) * 0.02, 'Wproj_b': jax.random.normal(ks[4], (nf,), dtype=jnp.float32) * 0.02}
    _L1_attn_all = _L1_attn_setup()
    _L1_attn_in = {k: v for k, v in _L1_attn_all.items() if k in ('Wqkv_w', 'Wqkv_b', 'Wproj_w', 'Wproj_b')}
    del _L1_attn_all

    def _L1_ffn_setup():
        import jax, jax.numpy as jnp
        import numpy as np
        D_MODEL = 192
        N_EXPERTS = 16
        TOP_K = 2
        D_FF = 4 * D_MODEL
        B, L = (4, 512)
        key = jax.random.key(seed)
        ks = jax.random.split(key, 6)
        s_in = 1.0 / np.sqrt(D_MODEL)
        s_ff = 1.0 / np.sqrt(D_FF)
        x = jax.random.normal(ks[0], (B, L, D_MODEL), dtype=jnp.float32)
        Wr = jax.random.uniform(ks[1], (N_EXPERTS, D_MODEL), jnp.float32, -s_in, s_in)
        W1 = jax.random.uniform(ks[2], (N_EXPERTS, D_MODEL, D_FF), jnp.float32, -s_in, s_in)
        b1 = jax.random.uniform(ks[3], (N_EXPERTS, D_FF), jnp.float32, -s_in, s_in)
        W2 = jax.random.uniform(ks[4], (N_EXPERTS, D_FF, D_MODEL), jnp.float32, -s_ff, s_ff)
        b2 = jax.random.uniform(ks[5], (N_EXPERTS, D_MODEL), jnp.float32, -s_ff, s_ff)
        return {'x': x, 'Wr': Wr, 'W1': W1, 'b1': b1, 'W2': W2, 'b2': b2}
    _L1_ffn_all = _L1_ffn_setup()
    _L1_ffn_in = {k: v for k, v in _L1_ffn_all.items() if k in ('Wr', 'W1', 'b1', 'W2', 'b2')}
    del _L1_ffn_all

    def _L2_attn_setup():
        import jax, jax.numpy as jnp
        import numpy as np
        KERNEL = 5
        NUM_HEADS = 4

        def _window_starts(L, k):
            pad = k // 2
            return jnp.clip(jnp.arange(L) - pad, 0, L - k)

        def _neighborhood_attention_2d(xs, qkv_w, qkv_b, rpb, proj_w, proj_b):
            H, W, D = xs.shape
            nh, k = (NUM_HEADS, KERNEL)
            dh = D // nh
            qkv = xs @ qkv_w.T + qkv_b
            qkv = qkv.reshape(H, W, 3, nh, dh).transpose(2, 3, 0, 1, 4)
            q, kmat, vmat = (qkv[0], qkv[1], qkv[2])
            q = q * dh ** (-0.5)
            sh = _window_starts(H, k)
            sw = _window_starts(W, k)
            off = jnp.arange(k)
            idx_h = sh[:, None] + off[None, :]
            idx_w = sw[:, None] + off[None, :]
            kk = kmat[:, idx_h][:, :, :, idx_w]
            vv = vmat[:, idx_h][:, :, :, idx_w]
            logits = jnp.einsum('nhwd,nhawbd->nhwab', q, kk)
            bh = idx_h - jnp.arange(H)[:, None] + (k - 1)
            bw = idx_w - jnp.arange(W)[:, None] + (k - 1)
            bias = rpb[:, bh[:, None, :, None], bw[None, :, None, :]]
            logits = logits + bias
            attn = jax.nn.softmax(logits.reshape(nh, H, W, k * k), axis=-1).reshape(nh, H, W, k, k)
            out = jnp.einsum('nhwab,nhawbd->nhwd', attn, vv)
            out = out.transpose(1, 2, 0, 3).reshape(H, W, D)
            return out @ proj_w.T + proj_b
        H, W = (96, 96)
        IN_D, HID, OUT_D = (192, 96, 192)
        key = jax.random.key(seed)
        ks = jax.random.split(key, 16)
        s = 0.02
        return {'x': jax.random.normal(ks[0], (H, W, IN_D), dtype=jnp.float32), 'fc1_w': jax.random.normal(ks[1], (HID, IN_D), dtype=jnp.float32) * s, 'fc1_b': jnp.zeros((HID,), dtype=jnp.float32), 'convA_w': jax.random.normal(ks[2], (64, HID), dtype=jnp.float32) * s, 'convA_b': jnp.zeros((64,), dtype=jnp.float32), 'convB_w': jax.random.normal(ks[3], (HID, 64), dtype=jnp.float32) * s, 'convB_b': jnp.zeros((HID,), dtype=jnp.float32), 'qkv_w': jax.random.normal(ks[4], (3 * HID, HID), dtype=jnp.float32) * s, 'qkv_b': jnp.zeros((3 * HID,), dtype=jnp.float32), 'rpb': jax.random.normal(ks[5], (NUM_HEADS, 2 * KERNEL - 1, 2 * KERNEL - 1), dtype=jnp.float32) * s, 'proj_w': jax.random.normal(ks[6], (HID, HID), dtype=jnp.float32) * s, 'proj_b': jnp.zeros((HID,), dtype=jnp.float32), 'fc2_w': jax.random.normal(ks[7], (OUT_D, HID), dtype=jnp.float32) * s, 'fc2_b': jnp.zeros((OUT_D,), dtype=jnp.float32)}
    _L2_attn_all = _L2_attn_setup()
    _L2_attn_in = {k: v for k, v in _L2_attn_all.items() if k in ('fc1_w', 'fc1_b', 'convA_w', 'convA_b', 'convB_w', 'convB_b', 'qkv_w', 'qkv_b', 'rpb', 'proj_w', 'proj_b', 'fc2_w', 'fc2_b')}
    del _L2_attn_all

    def _L2_ffn_setup():
        import jax, jax.numpy as jnp
        import numpy as np
        E, TOPK = (32, 2)
        D, HID, BOT, OUT = (192, 512, 64, 192)
        B, S = (2, 128)
        key = jax.random.key(seed)
        ks = jax.random.split(key, 7)
        p = lambda k, shape: jax.random.normal(k, shape, dtype=jnp.float32) * 0.02
        return {'x': jax.random.normal(ks[0], (B, S, D), dtype=jnp.float32), 'gate_w': p(ks[1], (E, D)), 'W1': p(ks[2], (E, D, HID)), 'b1': jnp.zeros((E, HID), jnp.float32), 'W2': p(ks[3], (E, HID, HID)), 'b2': jnp.zeros((E, HID), jnp.float32), 'W3': p(ks[4], (E, HID, BOT)), 'b3': jnp.zeros((E, BOT), jnp.float32), 'Wl': p(ks[5], (E, BOT, OUT)), 'bl': jnp.zeros((E, OUT), jnp.float32)}
    _L2_ffn_all = _L2_ffn_setup()
    _L2_ffn_in = {k: v for k, v in _L2_ffn_all.items() if k in ('gate_w', 'W1', 'b1', 'W2', 'b2', 'W3', 'b3', 'Wl', 'bl')}
    del _L2_ffn_all

    def _L3_attn_setup():
        import jax, jax.numpy as jnp
        import numpy as np
        D_MODEL = 192
        D_STATE = 8
        EXPAND = 2
        D_HEAD = 64
        D_CONV = 4
        D_INNER = EXPAND * D_MODEL
        N_HEADS = D_INNER // D_HEAD
        PARAM_DIM = 2
        D_PROJ = 2 * D_INNER + N_HEADS * PARAM_DIM
        D_FF = 4 * D_MODEL
        BATCH, SEQ = (2, 512)

        def _rmsnorm(x, w, eps=1e-06):
            return x * jax.lax.rsqrt(jnp.mean(x * x, axis=-1, keepdims=True) + eps) * w

        def _l2norm(x, eps=1e-12):
            return x * jax.lax.rsqrt(jnp.sum(x * x, axis=-1, keepdims=True) + eps)

        def _mixer(x, w_in, conv_w, w_bc, D_skip, w_out):
            Bsz, T, _ = x.shape
            proj = x @ w_in
            gate, vraw, params = jnp.split(proj, [D_INNER, 2 * D_INNER], axis=-1)
            vpad = jnp.pad(vraw, ((0, 0), (D_CONV - 1, 0), (0, 0)))
            kernel = conv_w.T[:, None, :]
            conv = jax.lax.conv_general_dilated(vpad, kernel, window_strides=(1,), padding='VALID', dimension_numbers=('NWC', 'WIO', 'NWC'), feature_group_count=D_INNER)
            v = jax.nn.silu(conv)
            bc = (v @ w_bc).reshape(Bsz, T, N_HEADS, 2, D_STATE)
            Bm = _l2norm(bc[..., 0, :])
            Cm = _l2norm(bc[..., 1, :])
            p = params.reshape(Bsz, T, N_HEADS, PARAM_DIM)
            A = jax.nn.softplus(p[..., 0])
            dt = jax.nn.sigmoid(p[..., 1])
            S = 1.0 / (1.0 + dt * dt * A)
            u = v.reshape(Bsz, T, N_HEADS, D_HEAD)
            tfirst = lambda a: jnp.moveaxis(a, 1, 0)

            def step(carry, inp):
                z, xs = carry
                Bt, Ct, At, dtt, St, ut = inp
                d = dtt[..., None, None]
                a = At[..., None, None]
                s = St[..., None, None]
                bu = Bt[..., :, None] * ut[..., None, :]
                z = s * (z - d * a * xs + d * bu)
                xs = xs + d * z
                y = jnp.einsum('bhn,bhnp->bhp', Ct, xs)
                return ((z, xs), y)
            z0 = jnp.zeros((Bsz, N_HEADS, D_STATE, D_HEAD), x.dtype)
            _, ys = jax.lax.scan(step, (z0, z0), (tfirst(Bm), tfirst(Cm), tfirst(A), tfirst(dt), tfirst(S), tfirst(u)))
            y = jnp.moveaxis(ys, 0, 1)
            gated = (y + D_skip[None, None, :, None] * u) * jax.nn.silu(gate).reshape(Bsz, T, N_HEADS, D_HEAD)
            return gated.reshape(Bsz, T, D_INNER) @ w_out
        key = jax.random.key(seed)
        ks = jax.random.split(key, 8)

        def s(k, shape, scale):
            return jax.random.normal(k, shape, dtype=jnp.float32) * scale
        return {'x': s(ks[0], (BATCH, SEQ, D_MODEL), 1.0), 'norm1_w': jnp.ones((D_MODEL,), jnp.float32), 'w_in': s(ks[1], (D_MODEL, D_PROJ), D_MODEL ** (-0.5)), 'conv_w': s(ks[2], (D_INNER, D_CONV), D_CONV ** (-0.5)), 'w_bc': s(ks[3], (D_INNER, 2 * N_HEADS * D_STATE), D_INNER ** (-0.5)), 'D_skip': s(ks[4], (N_HEADS,), 1.0), 'w_out': s(ks[5], (D_INNER, D_MODEL), D_INNER ** (-0.5)), 'norm2_w': jnp.ones((D_MODEL,), jnp.float32), 'ff_w1': s(ks[6], (D_MODEL, D_FF), D_MODEL ** (-0.5)), 'ff_b1': jnp.zeros((D_FF,), jnp.float32), 'ff_w2': s(ks[7], (D_FF, D_MODEL), D_FF ** (-0.5)), 'ff_b2': jnp.zeros((D_MODEL,), jnp.float32)}
    _L3_attn_all = _L3_attn_setup()
    _L3_attn_in = {k: v for k, v in _L3_attn_all.items() if k in ('norm1_w', 'w_in', 'conv_w', 'w_bc', 'D_skip', 'w_out', 'norm2_w', 'ff_w1', 'ff_b1', 'ff_w2', 'ff_b2')}
    del _L3_attn_all

    def _L3_ffn_setup():
        import jax, jax.numpy as jnp
        import numpy as np
        D_MODEL = 192
        KAN_HIDDEN = 512
        NUM_CP = 16
        DEGREE = 3
        RMIN, RMAX = (-4.0, 4.0)

        def bspline_basis(x, num_cp=NUM_CP, degree=DEGREE, rmin=RMIN, rmax=RMAX):
            h = (rmax - rmin) / (num_cp - degree)
            knots = rmin - degree * h + jnp.arange(num_cp + degree + 1, dtype=x.dtype) * h
            xe = x[..., None]
            b = ((xe >= knots[:-1]) & (xe < knots[1:])).astype(x.dtype)
            for d in range(1, degree + 1):
                t0 = knots[:-(d + 1)]
                t1 = knots[d:-1]
                t2 = knots[d + 1:]
                t3 = knots[1:-d]
                b = (xe - t0) / (t1 - t0) * b[..., :-1] + (t2 - xe) / (t2 - t3) * b[..., 1:]
            return b

        def kan_layer(x, w):
            basis = bspline_basis(x)
            return jnp.einsum('ndk,odk->no', basis, w)
        key = jax.random.key(seed)
        kx, k1, k2 = jax.random.split(key, 3)
        x = jax.random.normal(kx, (2, 512, D_MODEL), dtype=jnp.float32)
        w1 = jax.random.normal(k1, (KAN_HIDDEN, D_MODEL, NUM_CP), dtype=jnp.float32) * (1.0 / np.sqrt(D_MODEL * NUM_CP))
        w2 = jax.random.normal(k2, (D_MODEL, KAN_HIDDEN, NUM_CP), dtype=jnp.float32) * (1.0 / np.sqrt(KAN_HIDDEN * NUM_CP))
        return {'x': x, 'w1': w1, 'w2': w2}
    _L3_ffn_all = _L3_ffn_setup()
    _L3_ffn_in = {k: v for k, v in _L3_ffn_all.items() if k in ('w1', 'w2')}
    del _L3_ffn_all
    return {'x': x, 'L0_tok_weight': _L0_tok_in['weight'], 'L0_tok_bias': _L0_tok_in['bias'], 'L0_attn_W_qkv': _L0_attn_in['W_qkv'], 'L0_attn_b_qkv': _L0_attn_in['b_qkv'], 'L0_ffn_gate_w': _L0_ffn_in['gate_w'], 'L0_ffn_gate_b': _L0_ffn_in['gate_b'], 'L0_ffn_fc1_w': _L0_ffn_in['fc1_w'], 'L0_ffn_fc1_b': _L0_ffn_in['fc1_b'], 'L0_ffn_ln_w': _L0_ffn_in['ln_w'], 'L0_ffn_ln_b': _L0_ffn_in['ln_b'], 'L0_ffn_fc2_w': _L0_ffn_in['fc2_w'], 'L0_ffn_fc2_b': _L0_ffn_in['fc2_b'], 'L1_attn_Wqkv_w': _L1_attn_in['Wqkv_w'], 'L1_attn_Wqkv_b': _L1_attn_in['Wqkv_b'], 'L1_attn_Wproj_w': _L1_attn_in['Wproj_w'], 'L1_attn_Wproj_b': _L1_attn_in['Wproj_b'], 'L1_ffn_Wr': _L1_ffn_in['Wr'], 'L1_ffn_W1': _L1_ffn_in['W1'], 'L1_ffn_b1': _L1_ffn_in['b1'], 'L1_ffn_W2': _L1_ffn_in['W2'], 'L1_ffn_b2': _L1_ffn_in['b2'], 'L2_attn_fc1_w': _L2_attn_in['fc1_w'], 'L2_attn_fc1_b': _L2_attn_in['fc1_b'], 'L2_attn_convA_w': _L2_attn_in['convA_w'], 'L2_attn_convA_b': _L2_attn_in['convA_b'], 'L2_attn_convB_w': _L2_attn_in['convB_w'], 'L2_attn_convB_b': _L2_attn_in['convB_b'], 'L2_attn_qkv_w': _L2_attn_in['qkv_w'], 'L2_attn_qkv_b': _L2_attn_in['qkv_b'], 'L2_attn_rpb': _L2_attn_in['rpb'], 'L2_attn_proj_w': _L2_attn_in['proj_w'], 'L2_attn_proj_b': _L2_attn_in['proj_b'], 'L2_attn_fc2_w': _L2_attn_in['fc2_w'], 'L2_attn_fc2_b': _L2_attn_in['fc2_b'], 'L2_ffn_gate_w': _L2_ffn_in['gate_w'], 'L2_ffn_W1': _L2_ffn_in['W1'], 'L2_ffn_b1': _L2_ffn_in['b1'], 'L2_ffn_W2': _L2_ffn_in['W2'], 'L2_ffn_b2': _L2_ffn_in['b2'], 'L2_ffn_W3': _L2_ffn_in['W3'], 'L2_ffn_b3': _L2_ffn_in['b3'], 'L2_ffn_Wl': _L2_ffn_in['Wl'], 'L2_ffn_bl': _L2_ffn_in['bl'], 'L3_attn_norm1_w': _L3_attn_in['norm1_w'], 'L3_attn_w_in': _L3_attn_in['w_in'], 'L3_attn_conv_w': _L3_attn_in['conv_w'], 'L3_attn_w_bc': _L3_attn_in['w_bc'], 'L3_attn_D_skip': _L3_attn_in['D_skip'], 'L3_attn_w_out': _L3_attn_in['w_out'], 'L3_attn_norm2_w': _L3_attn_in['norm2_w'], 'L3_attn_ff_w1': _L3_attn_in['ff_w1'], 'L3_attn_ff_b1': _L3_attn_in['ff_b1'], 'L3_attn_ff_w2': _L3_attn_in['ff_w2'], 'L3_attn_ff_b2': _L3_attn_in['ff_b2'], 'L3_ffn_w1': _L3_ffn_in['w1'], 'L3_ffn_w2': _L3_ffn_in['w2']}

def reference(x, L0_tok_weight, L0_tok_bias, L0_attn_W_qkv, L0_attn_b_qkv, L0_ffn_gate_w, L0_ffn_gate_b, L0_ffn_fc1_w, L0_ffn_fc1_b, L0_ffn_ln_w, L0_ffn_ln_b, L0_ffn_fc2_w, L0_ffn_fc2_b, L1_attn_Wqkv_w, L1_attn_Wqkv_b, L1_attn_Wproj_w, L1_attn_Wproj_b, L1_ffn_Wr, L1_ffn_W1, L1_ffn_b1, L1_ffn_W2, L1_ffn_b2, L2_attn_fc1_w, L2_attn_fc1_b, L2_attn_convA_w, L2_attn_convA_b, L2_attn_convB_w, L2_attn_convB_b, L2_attn_qkv_w, L2_attn_qkv_b, L2_attn_rpb, L2_attn_proj_w, L2_attn_proj_b, L2_attn_fc2_w, L2_attn_fc2_b, L2_ffn_gate_w, L2_ffn_W1, L2_ffn_b1, L2_ffn_W2, L2_ffn_b2, L2_ffn_W3, L2_ffn_b3, L2_ffn_Wl, L2_ffn_bl, L3_attn_norm1_w, L3_attn_w_in, L3_attn_conv_w, L3_attn_w_bc, L3_attn_D_skip, L3_attn_w_out, L3_attn_norm2_w, L3_attn_ff_w1, L3_attn_ff_b1, L3_attn_ff_w2, L3_attn_ff_b2, L3_ffn_w1, L3_ffn_w2):
    import jax
    import jax.numpy as jnp

    def _L0_tok_ref(x, weight, bias):
        import jax, jax.numpy as jnp
        import numpy as np
        PATCH = 16
        CHANNELS = 3
        EMBED = 192
        B, C, H, W = x.shape
        p = PATCH
        nh, nw = (H // p, W // p)
        patches = x.reshape(B, C, nh, p, nw, p).transpose(0, 1, 2, 4, 3, 5)
        flat = patches.reshape(B, -1, C * p * p)
        return flat @ weight.T + bias

    def _L0_attn_ref(x, W_qkv, b_qkv):
        import math
        import jax, jax.numpy as jnp
        import numpy as np
        B, N, D_IN, D_OUT = (8, 512, 192, 192)
        d_out = D_OUT
        qkv = jnp.einsum('bnd,de->bne', x, W_qkv) + b_qkv
        q = qkv[:, :, :d_out]
        k = qkv[:, :, d_out:2 * d_out]
        v = qkv[:, :, 2 * d_out:3 * d_out]
        scale = 1.0 / math.sqrt(d_out)
        scores = jnp.einsum('bqd,bkd->bqk', q, k) * scale
        attn = jax.nn.softmax(scores, axis=-1)
        context = jnp.einsum('bqk,bkd->bqd', attn, v)
        return context

    def _L0_ffn_ref(x, gate_w, gate_b, fc1_w, fc1_b, ln_w, ln_b, fc2_w, fc2_b):
        import jax, jax.numpy as jnp
        import numpy as np
        SEQ, BATCH, EMBED = (256, 2, 192)
        E = 16
        FFN_H = 384
        K_SHARED = 1
        K_ROUTE = 3
        LN_EPS = 1e-05
        NEG_INF = -1000000000.0
        S, B, D = x.shape
        T = S * B
        xf = x.reshape(T, D)
        scores = xf @ gate_w + gate_b
        scores = scores.at[:, :K_SHARED].set(NEG_INF)
        probs = jax.nn.softmax(scores, axis=-1)
        topv, topi = jax.lax.top_k(probs, K_ROUTE)
        combine = jnp.zeros((T, E), xf.dtype)
        combine = combine.at[jnp.arange(T)[:, None], topi].add(topv)
        combine = combine.at[:, :K_SHARED].add(1.0)
        h = jnp.einsum('td,edh->eth', xf, fc1_w) + fc1_b[:, None, :]
        h = jax.nn.gelu(h, approximate=False)
        mu = h.mean(-1, keepdims=True)
        var = h.var(-1, keepdims=True)
        h = (h - mu) * jax.lax.rsqrt(var + LN_EPS) * ln_w[:, None, :] + ln_b[:, None, :]
        y = jnp.einsum('eth,ehd->etd', h, fc2_w) + fc2_b[:, None, :]
        out = jnp.einsum('te,etd->td', combine, y)
        return out.reshape(S, B, D)

    def _L1_attn_ref(x, Wqkv_w, Wqkv_b, Wproj_w, Wproj_b):
        import jax, jax.numpy as jnp
        import numpy as np
        N_HEADS = 12
        NEG_BIG = 10000000000.0
        nb, ns, nf = x.shape
        hd = nf // N_HEADS
        qkv = x @ Wqkv_w.T + Wqkv_b
        q = qkv[..., :nf]
        q = q.reshape(nb, ns, N_HEADS, hd).transpose(0, 2, 1, 3)
        k = q
        v = q
        w = jnp.einsum('bhqd,bhkd->bhqk', q, k) * (1.0 / jnp.sqrt(jnp.float32(hd)))
        mask = jnp.tril(jnp.ones((ns, ns), dtype=x.dtype))
        w = jax.nn.softmax(w * mask - NEG_BIG * (1.0 - mask), axis=-1)
        a = jnp.einsum('bhqk,bhkd->bhqd', w, v)
        a = a.transpose(0, 2, 1, 3).reshape(nb, ns, nf)
        return a @ Wproj_w.T + Wproj_b

    def _L1_ffn_ref(x, Wr, W1, b1, W2, b2):
        import jax, jax.numpy as jnp
        import numpy as np
        D_MODEL = 192
        N_EXPERTS = 16
        TOP_K = 2
        D_FF = 4 * D_MODEL
        B, L = (4, 512)
        logits = jnp.einsum('bld,ed->ble', x, Wr)
        probs = jax.nn.softmax(logits, axis=-1)
        top_p, top_idx = jax.lax.top_k(probs, TOP_K)
        gating = jnp.sum(jax.nn.one_hot(top_idx, N_EXPERTS, dtype=probs.dtype) * top_p[..., None], axis=-2)
        gate_e = jnp.moveaxis(gating, -1, 0)

        def step(y, params):
            W1e, b1e, W2e, b2e, ge = params
            h = jax.nn.gelu(jnp.einsum('bld,df->blf', x, W1e) + b1e, approximate=False)
            out = jnp.einsum('blf,fd->bld', h, W2e) + b2e
            return (y + ge[..., None] * out, None)
        y0 = jnp.zeros_like(x)
        y, _ = jax.lax.scan(step, y0, (W1, b1, W2, b2, gate_e))
        return x + y

    def _L2_attn_ref(x, fc1_w, fc1_b, convA_w, convA_b, convB_w, convB_b, qkv_w, qkv_b, rpb, proj_w, proj_b, fc2_w, fc2_b):
        import jax, jax.numpy as jnp
        import numpy as np
        KERNEL = 5
        NUM_HEADS = 4

        def _window_starts(L, k):
            pad = k // 2
            return jnp.clip(jnp.arange(L) - pad, 0, L - k)

        def _neighborhood_attention_2d(xs, qkv_w, qkv_b, rpb, proj_w, proj_b):
            H, W, D = xs.shape
            nh, k = (NUM_HEADS, KERNEL)
            dh = D // nh
            qkv = xs @ qkv_w.T + qkv_b
            qkv = qkv.reshape(H, W, 3, nh, dh).transpose(2, 3, 0, 1, 4)
            q, kmat, vmat = (qkv[0], qkv[1], qkv[2])
            q = q * dh ** (-0.5)
            sh = _window_starts(H, k)
            sw = _window_starts(W, k)
            off = jnp.arange(k)
            idx_h = sh[:, None] + off[None, :]
            idx_w = sw[:, None] + off[None, :]
            kk = kmat[:, idx_h][:, :, :, idx_w]
            vv = vmat[:, idx_h][:, :, :, idx_w]
            logits = jnp.einsum('nhwd,nhawbd->nhwab', q, kk)
            bh = idx_h - jnp.arange(H)[:, None] + (k - 1)
            bw = idx_w - jnp.arange(W)[:, None] + (k - 1)
            bias = rpb[:, bh[:, None, :, None], bw[None, :, None, :]]
            logits = logits + bias
            attn = jax.nn.softmax(logits.reshape(nh, H, W, k * k), axis=-1).reshape(nh, H, W, k, k)
            out = jnp.einsum('nhwab,nhawbd->nhwd', attn, vv)
            out = out.transpose(1, 2, 0, 3).reshape(H, W, D)
            return out @ proj_w.T + proj_b
        xs = x @ fc1_w.T + fc1_b
        a = xs @ convA_w.T + convA_b
        b = a @ convB_w.T + convB_b
        xs = b * 1.0 + xs
        xs = jax.nn.gelu(xs, approximate=False)
        xs = _neighborhood_attention_2d(xs, qkv_w, qkv_b, rpb, proj_w, proj_b)
        xs = xs @ fc2_w.T + fc2_b
        return x + xs

    def _L2_ffn_ref(x, gate_w, W1, b1, W2, b2, W3, b3, Wl, bl):
        import jax, jax.numpy as jnp
        import numpy as np
        E, TOPK = (32, 2)
        D, HID, BOT, OUT = (192, 512, 64, 192)
        B, S = (2, 128)
        Bz, Sl, d = x.shape
        xt = x.reshape(-1, d)
        scores = jax.nn.softmax(xt @ gate_w.T, axis=-1)
        topk_w, topk_idx = jax.lax.top_k(scores, TOPK)
        topk_w = topk_w / (topk_w.sum(-1, keepdims=True) + 1e-20)
        gelu = lambda v: jax.nn.gelu(v, approximate=False)
        h = gelu(jnp.einsum('nd,edh->enh', xt, W1) + b1[:, None, :])
        h = gelu(jnp.einsum('enh,ehg->eng', h, W2) + b2[:, None, :])
        z = jnp.einsum('eng,egb->enb', h, W3) + b3[:, None, :]
        out_all = jnp.einsum('enb,ebo->eno', z, Wl) + bl[:, None, :]
        sel = jnp.take_along_axis(out_all.transpose(1, 0, 2), topk_idx[:, :, None], axis=1)
        y = (sel * topk_w[:, :, None]).sum(axis=1)
        return y.reshape(Bz, Sl, OUT)

    def _L3_attn_ref(x, norm1_w, w_in, conv_w, w_bc, D_skip, w_out, norm2_w, ff_w1, ff_b1, ff_w2, ff_b2):
        import jax, jax.numpy as jnp
        import numpy as np
        D_MODEL = 192
        D_STATE = 8
        EXPAND = 2
        D_HEAD = 64
        D_CONV = 4
        D_INNER = EXPAND * D_MODEL
        N_HEADS = D_INNER // D_HEAD
        PARAM_DIM = 2
        D_PROJ = 2 * D_INNER + N_HEADS * PARAM_DIM
        D_FF = 4 * D_MODEL
        BATCH, SEQ = (2, 512)

        def _rmsnorm(x, w, eps=1e-06):
            return x * jax.lax.rsqrt(jnp.mean(x * x, axis=-1, keepdims=True) + eps) * w

        def _l2norm(x, eps=1e-12):
            return x * jax.lax.rsqrt(jnp.sum(x * x, axis=-1, keepdims=True) + eps)

        def _mixer(x, w_in, conv_w, w_bc, D_skip, w_out):
            Bsz, T, _ = x.shape
            proj = x @ w_in
            gate, vraw, params = jnp.split(proj, [D_INNER, 2 * D_INNER], axis=-1)
            vpad = jnp.pad(vraw, ((0, 0), (D_CONV - 1, 0), (0, 0)))
            kernel = conv_w.T[:, None, :]
            conv = jax.lax.conv_general_dilated(vpad, kernel, window_strides=(1,), padding='VALID', dimension_numbers=('NWC', 'WIO', 'NWC'), feature_group_count=D_INNER)
            v = jax.nn.silu(conv)
            bc = (v @ w_bc).reshape(Bsz, T, N_HEADS, 2, D_STATE)
            Bm = _l2norm(bc[..., 0, :])
            Cm = _l2norm(bc[..., 1, :])
            p = params.reshape(Bsz, T, N_HEADS, PARAM_DIM)
            A = jax.nn.softplus(p[..., 0])
            dt = jax.nn.sigmoid(p[..., 1])
            S = 1.0 / (1.0 + dt * dt * A)
            u = v.reshape(Bsz, T, N_HEADS, D_HEAD)
            tfirst = lambda a: jnp.moveaxis(a, 1, 0)

            def step(carry, inp):
                z, xs = carry
                Bt, Ct, At, dtt, St, ut = inp
                d = dtt[..., None, None]
                a = At[..., None, None]
                s = St[..., None, None]
                bu = Bt[..., :, None] * ut[..., None, :]
                z = s * (z - d * a * xs + d * bu)
                xs = xs + d * z
                y = jnp.einsum('bhn,bhnp->bhp', Ct, xs)
                return ((z, xs), y)
            z0 = jnp.zeros((Bsz, N_HEADS, D_STATE, D_HEAD), x.dtype)
            _, ys = jax.lax.scan(step, (z0, z0), (tfirst(Bm), tfirst(Cm), tfirst(A), tfirst(dt), tfirst(S), tfirst(u)))
            y = jnp.moveaxis(ys, 0, 1)
            gated = (y + D_skip[None, None, :, None] * u) * jax.nn.silu(gate).reshape(Bsz, T, N_HEADS, D_HEAD)
            return gated.reshape(Bsz, T, D_INNER) @ w_out
        x = x + _mixer(_rmsnorm(x, norm1_w), w_in, conv_w, w_bc, D_skip, w_out)
        h = _rmsnorm(x, norm2_w)
        return x + (jax.nn.gelu(h @ ff_w1 + ff_b1) @ ff_w2 + ff_b2)

    def _L3_ffn_ref(x, w1, w2):
        import jax, jax.numpy as jnp
        import numpy as np
        D_MODEL = 192
        KAN_HIDDEN = 512
        NUM_CP = 16
        DEGREE = 3
        RMIN, RMAX = (-4.0, 4.0)

        def bspline_basis(x, num_cp=NUM_CP, degree=DEGREE, rmin=RMIN, rmax=RMAX):
            h = (rmax - rmin) / (num_cp - degree)
            knots = rmin - degree * h + jnp.arange(num_cp + degree + 1, dtype=x.dtype) * h
            xe = x[..., None]
            b = ((xe >= knots[:-1]) & (xe < knots[1:])).astype(x.dtype)
            for d in range(1, degree + 1):
                t0 = knots[:-(d + 1)]
                t1 = knots[d:-1]
                t2 = knots[d + 1:]
                t3 = knots[1:-d]
                b = (xe - t0) / (t1 - t0) * b[..., :-1] + (t2 - xe) / (t2 - t3) * b[..., 1:]
            return b

        def kan_layer(x, w):
            basis = bspline_basis(x)
            return jnp.einsum('ndk,odk->no', basis, w)
        B, T, D = x.shape
        input_dtype = x.dtype
        h = x.reshape(B * T, D).astype(jnp.float32)
        h = kan_layer(h, w1)
        h = kan_layer(h, w2)
        h = h.astype(input_dtype)
        return h.reshape(B, T, -1)
    h = _L0_tok_ref(x, L0_tok_weight, L0_tok_bias)
    h = h + _L0_attn_ref(_layernorm(h, axis=-1), L0_attn_W_qkv, L0_attn_b_qkv)
    h = h + _L0_ffn_ref(_layernorm(h, axis=-1), L0_ffn_gate_w, L0_ffn_gate_b, L0_ffn_fc1_w, L0_ffn_fc1_b, L0_ffn_ln_w, L0_ffn_ln_b, L0_ffn_fc2_w, L0_ffn_fc2_b)
    h = h + _L1_attn_ref(_layernorm(h, axis=-1), L1_attn_Wqkv_w, L1_attn_Wqkv_b, L1_attn_Wproj_w, L1_attn_Wproj_b)
    h = h + _L1_ffn_ref(_layernorm(h, axis=-1), L1_ffn_Wr, L1_ffn_W1, L1_ffn_b1, L1_ffn_W2, L1_ffn_b2)
    h = h + _L2_attn_ref(_layernorm(h, axis=-1), L2_attn_fc1_w, L2_attn_fc1_b, L2_attn_convA_w, L2_attn_convA_b, L2_attn_convB_w, L2_attn_convB_b, L2_attn_qkv_w, L2_attn_qkv_b, L2_attn_rpb, L2_attn_proj_w, L2_attn_proj_b, L2_attn_fc2_w, L2_attn_fc2_b)
    h = h + _L2_ffn_ref(_layernorm(h, axis=-1), L2_ffn_gate_w, L2_ffn_W1, L2_ffn_b1, L2_ffn_W2, L2_ffn_b2, L2_ffn_W3, L2_ffn_b3, L2_ffn_Wl, L2_ffn_bl)
    h = h + _L3_attn_ref(_layernorm(h, axis=-1), L3_attn_norm1_w, L3_attn_w_in, L3_attn_conv_w, L3_attn_w_bc, L3_attn_D_skip, L3_attn_w_out, L3_attn_norm2_w, L3_attn_ff_w1, L3_attn_ff_b1, L3_attn_ff_w2, L3_attn_ff_b2)
    h = h + _L3_ffn_ref(_layernorm(h, axis=-1), L3_ffn_w1, L3_ffn_w2)
    return h

_drawn_inputs = setup_inputs


def setup_inputs(seed=0):
    import zlib

    import numpy as np

    out = dict(_drawn_inputs(seed))
    spreads = {'L0_ffn_gate_b': (0.0, 0.1),
     'L0_ffn_fc1_b': (0.0, 0.1),
     'L0_ffn_ln_w': (1.0, 0.2),
     'L0_ffn_ln_b': (0.0, 0.1),
     'L0_ffn_fc2_b': (0.0, 0.1),
     'L2_attn_fc1_b': (0.0, 0.8),
     'L2_attn_convA_b': (0.0, 0.8),
     'L2_attn_convB_b': (0.0, 0.8),
     'L2_attn_qkv_b': (0.0, 0.8),
     'L2_attn_proj_b': (0.0, 0.8),
     'L2_attn_fc2_b': (0.0, 0.1),
     'L2_ffn_b1': (0.0, 0.8),
     'L2_ffn_b2': (0.0, 0.8),
     'L2_ffn_b3': (0.0, 0.8),
     'L2_ffn_bl': (0.0, 2.0),
     'L3_attn_norm1_w': (1.0, 0.6),
     'L3_attn_norm2_w': (1.0, 0.6),
     'L3_attn_ff_b1': (0.0, 2.0),
     'L3_attn_ff_b2': (0.0, 1.788)}
    factors = {'L1_attn_Wqkv_b': 6.245,
     'L1_ffn_b1': 8.0,
     'L1_ffn_b2': 8.0,
     'L2_attn_fc1_w': 8.0,
     'L2_attn_convA_w': 8.0,
     'L2_attn_convB_w': 8.0,
     'L2_attn_qkv_w': 8.0,
     'L2_attn_rpb': 8.0,
     'L2_attn_proj_w': 8.0,
     'L2_attn_fc2_w': 7.93,
     'L2_ffn_W1': 8.0,
     'L2_ffn_W2': 8.0,
     'L2_ffn_W3': 8.0,
     'L2_ffn_Wl': 8.0,
     'L3_ffn_w1': 30.488,
     'L3_attn_w_bc': 2.781,
     'L3_attn_D_skip': 3.174,
     'L3_ffn_w2': 7.896}
    for name, (base, spread) in spreads.items():
        noise = np.random.default_rng([zlib.crc32(name.encode()), seed]).standard_normal(out[name].shape)
        drawn = base * np.exp(spread * noise) if base else spread * noise
        out[name] = jnp.asarray(drawn.astype(out[name].dtype))
    for name, factor in factors.items():
        out[name] = (out[name] * factor).astype(out[name].dtype)
    return out
```

```python
from contextlib import ExitStack

import concourse.bass as bass
from concourse import mybir

F32 = mybir.dt.float32
I32 = mybir.dt.int32
U32 = mybir.dt.uint32
ALU = mybir.AluOpType
ACT = mybir.ActivationFunctionType
AX_X = mybir.AxisListType.X

P = 128
D = 192
DC = 96
N_TOK = 1024
NT = N_TOK // P
HALF = 512
SEQ = 64
NEG = -1.0e30

C_ID = 0
C_M16 = C_ID + P
C_M24 = C_M16 + 6
C_M8 = C_M24 + 4
C_BLK = C_M8 + 6
C_CAU = C_BLK + P
C_LT = C_CAU + 3 * P
C_IOTA = C_LT + P
C_K1 = C_IOTA + P
C_K2 = C_K1 + 8
C_N = C_K2 + 16


class Chain:

    def __init__(self, eng, sem):
        self.eng, self.sem, self.n, self.base = eng, sem, 0, 0

    def __call__(self, ins):
        ins.then_inc(self.sem, 1)
        self.n += 1
        self.eng.wait_ge(self.sem, self.base + self.n)


class Tower:
    pass


def sems(nc, ctx, prefix, *names):
    handles = [ctx.enter_context(nc.semaphore(f"{prefix}_{n}")) for n in names]

    def clear():
        for handle in handles:
            nc.gpsimd.sem_clear(handle)

    if prefix not in ("m0", "m1", "m2"):
        ctx.callback(clear)
    return handles


def wait_alone(eng, sem, value, waited):
    eng.wait_ge(sem, value)
    eng.sem_inc(waited, 1)


def tokens_stage(nc, T, patches, loads, mixtures):
    with ExitStack() as ctx:
        xs = ctx.enter_context(nc.sbuf_tensor("tok_x", [P, 6, N_TOK], F32))
        s_x = sems(nc, ctx, "tok", *[f"patches{k}" for k in range(6)])
        s_mm, s_h, s_z = sems(nc, ctx, "tok", "products", "h", "zeros")
        with nc.Block() as block:
            @block.sync
            def _(sp):
                sp.dma_start(T.w["tok_w"][:, :, :], loads["tok_w"][1]).then_inc(T.loaded["tok_w"], 16)
                for k in range(1, 6, 2):
                    sp.dma_start(xs[:, k, :], patches[:, k, :]).then_inc(s_x[k], 16)
                for name, (dst, src) in loads.items():
                    if name != "tok_w":
                        sp.dma_start(dst, src).then_inc(T.loaded[name], 16)

            @block.scalar
            def _(act):
                for k in range(0, 6, 2):
                    act.dma_start(xs[:, k, :], patches[:, k, :]).then_inc(s_x[k], 16)
                act.wait_ge(s_z, 1)
                for m in mixtures:
                    for slots in (m.slots_x, m.slots_y):
                        act.dma_start(slots.rearrange("(n p) d -> p n d", p=P),
                                      T.zeros[:, :].unsqueeze(1).to_broadcast([P, m.tiles, D])
                                      ).then_inc(T.s_cleared, 16)

            @block.tensor
            def _(pe):
                pe.wait_ge(T.loaded["tok_w"], 16)
                for k in range(6):
                    pe.wait_ge(s_x[k], 16)
                    for t in range(NT):
                        mm = pe.matmul(T.ps[:, t, 0:D], xs[:, k, t * P:(t + 1) * P], T.w["tok_w"][:, k, :],
                                       start=(k == 0), stop=(k == 5))
                        if k == 5:
                            mm.then_inc(s_mm, 1)

            @block.vector
            def _(dve):
                dve.memset(T.zeros[:, :], 0.0).then_inc(s_z, 1)
                dve.memset(T.ones[:, :], 1.0)
                dve.memset(T.power[:, :], -0.5)
                dve.memset(T.xT[DC:DC + 1, 0, :], 1.0)
                dve.memset(T.aT[DC:DC + 1, 0, :], 1.0)
                dve.wait_ge(T.loaded["tok_b"], 16)
                for t in range(NT):
                    dve.wait_ge(s_mm, t + 1)
                    dve.tensor_tensor(T.h[:, t, :], T.ps[:, t, 0:D], T.w["tok_b"][:, :], ALU.add).then_inc(s_h, 1)
                dve.wait_ge(s_h, NT)


def norm_stage(nc, T, name):
    with ExitStack() as ctx:
        stats = ctx.enter_context(nc.sbuf_tensor(f"{name}_stats", [P, NT, 6], F32))
        mv = ctx.enter_context(nc.sbuf_tensor(f"{name}_mv", [P, NT, 2], F32))
        var = ctx.enter_context(nc.sbuf_tensor(f"{name}_var", [P, NT], F32))
        rstd = ctx.enter_context(nc.sbuf_tensor(f"{name}_rstd", [P, NT], F32))
        s_c, s_var, s_rstd, s_xn, s_tp, s_cp = sems(
            nc, ctx, name, "chain", "variance", "rstd", "xn", "transposed", "copied")
        with nc.Block() as block:
            @block.vector
            def _(dve):
                chain = Chain(dve, s_c)
                for t in range(NT):
                    ins = dve.bn_stats(stats[:, t, :], T.h[:, t, :])
                chain(ins)
                for t in range(NT):
                    ins = dve.bn_aggr(mv[:, t, :], stats[:, t, :])
                chain(ins)
                dve.tensor_scalar(var[:, :], mv[:, :, 1], 1e-5, None, ALU.add).then_inc(s_var, 1)
                dve.wait_ge(s_rstd, 1)
                for t in range(NT):
                    dve.tensor_scalar(T.xn[:, t, :], T.h[:, t, :], mv[:, t, 0:1], rstd[:, t:t + 1],
                                      ALU.subtract, ALU.mult).then_inc(s_xn, 1)
                for t in range(0, NT, 2):
                    dve.wait_ge(s_tp, t + 1)
                    dve.tensor_copy(T.xT[0:DC, :, t * P:(t + 1) * P],
                                    T.ps[0:DC, t, 0:2 * P].rearrange("p (c n) -> p c n", c=2)).then_inc(s_cp, 1)
                dve.wait_ge(s_cp, NT)

            @block.gpsimd
            def _(pool):
                pool.wait_ge(s_var, 1)
                pool.tensor_tensor(rstd[:, :], var[:, :], T.power[:, :], ALU.pow).then_inc(s_rstd, 1)

            @block.scalar
            def _(act):
                for t in range(1, NT, 2):
                    act.wait_ge(s_tp, t + 1)
                    act.activation(T.xT[0:DC, :, t * P:(t + 1) * P],
                                   T.ps[0:DC, t, 0:2 * P].rearrange("p (c n) -> p c n", c=2),
                                   ACT.Copy).then_inc(s_cp, 1)

            @block.tensor
            def _(pe):
                if name == "n0":
                    pe.wait_ge(T.loaded["consts"], 16)
                for t in range(NT):
                    pe.wait_ge(s_xn, t + 1)
                    for c in range(2):
                        mm = pe.transpose(T.ps[0:DC, t, c * P:(c + 1) * P],
                                          T.xn[:, t, c * DC:(c + 1) * DC], T.ident)
                    mm.then_inc(s_tp, 1)


def attention0_stage(nc, T):
    scale = float(D) ** -0.5
    with ExitStack() as ctx:
        sb = lambda n, s: ctx.enter_context(nc.sbuf_tensor(f"a0_{n}", s, F32))
        qk = sb("qk", [DC, 4, N_TOK])
        v = sb("v", [P, NT, D])
        logit = sb("logit", [P, NT, P])
        prob = sb("prob", [P, NT, P])
        probT = sb("probT", [P, NT, P])
        top = sb("top", [P, NT])
        total = sb("total", [P, NT])
        inv = sb("inv", [P, NT])
        s_c, s_qkmm, s_qk, s_vmm, s_v, s_smm, s_l, s_e, s_t, s_pT, s_o, s_h = sems(
            nc, ctx, "a0", "chain", "qk_products", "qk", "v_products", "v", "scores", "logits", "exps",
            "transposed", "probT", "contexts", "h")
        with nc.Block() as block:
            @block.tensor
            def _(pe):
                pe.wait_ge(T.loaded["a0_w"], 16)
                for o in range(4):
                    for half in range(2):
                        cols = slice(half * HALF, (half + 1) * HALF)
                        pe.matmul(T.ps[0:DC, 2 * o + half, :], T.w["a0_w"][:, 0, o * DC:(o + 1) * DC],
                                  T.xT[:, 0, cols], start=True, stop=False)
                        pe.matmul(T.ps[0:DC, 2 * o + half, :], T.w["a0_w"][0:DC, 1, o * DC:(o + 1) * DC],
                                  T.xT[0:DC, 1, cols], start=False, stop=True).then_inc(s_qkmm, 1)
                for t in range(NT):
                    pe.wait_ge(s_qk, t + 1)
                    pe.matmul(T.ps[:, t, 0:D], T.xT[:, 0, t * P:(t + 1) * P], T.w["a0_w"][:, 0, 2 * D:3 * D],
                              start=True, stop=False)
                    pe.matmul(T.ps[:, t, 0:D], T.xT[0:DC, 1, t * P:(t + 1) * P], T.w["a0_w"][0:DC, 1, 2 * D:3 * D],
                              start=False, stop=True).then_inc(s_vmm, 1)
                for t in range(NT):
                    pe.wait_ge(s_v, t + 1)
                    for c in range(2):
                        mm = pe.matmul(T.ps[:, t, 0:P], qk[:, c, t * P:(t + 1) * P],
                                       qk[:, 2 + c, t * P:(t + 1) * P], start=(c == 0), stop=(c == 1))
                    mm.then_inc(s_smm, 1)
                for t in range(NT):
                    pe.wait_ge(s_e, t + 1)
                    pe.transpose(T.ps[:, t, P:2 * P], prob[:, t, :], T.ident).then_inc(s_t, 1)
                for t in range(NT):
                    pe.wait_ge(s_pT, t + 1)
                    pe.matmul(T.ps[:, t, 2 * P:2 * P + D], probT[:, t, :], v[:, t, :],
                              start=True, stop=True).then_inc(s_o, 1)

            @block.scalar
            def _(act):
                for b in range(8):
                    act.wait_ge(s_qkmm, b + 1)
                    act.activation(qk[:, b // 2, (b % 2) * HALF:(b % 2 + 1) * HALF], T.ps[0:DC, b, :],
                                   ACT.Copy).then_inc(s_qk, 1)
                for t in range(NT):
                    act.wait_ge(s_l, t + 1)
                    act.activation(prob[:, t, :], logit[:, t, :], ACT.Exp, bias=top[:, t:t + 1],
                                   accum_out=total[:, t:t + 1]).then_inc(s_e, 1)
                for t in range(NT):
                    act.wait_ge(s_t, t + 1)
                    act.activation(probT[:, t, :], T.ps[:, t, P:2 * P], ACT.Copy).then_inc(s_pT, 1)

            @block.vector
            def _(dve):
                chain = Chain(dve, s_c)
                for t in range(NT):
                    dve.wait_ge(s_vmm, t + 1)
                    dve.tensor_copy(v[:, t, :], T.ps[:, t, 0:D]).then_inc(s_v, 1)
                for t in range(NT):
                    dve.wait_ge(s_smm, t + 1)
                    chain(dve.scalar_tensor_tensor(logit[:, t, :], T.ps[:, t, 0:P], scale, T.block_mask,
                                                   ALU.mult, ALU.add))
                    dve.tensor_reduce(top[:, t:t + 1], logit[:, t, :], AX_X, ALU.max,
                                      negate=True).then_inc(s_l, 1)
                dve.wait_ge(s_e, NT)
                chain(dve.reciprocal(inv[:, :], total[:, :]))
                for t in range(NT):
                    dve.wait_ge(s_o, t + 1)
                    dve.scalar_tensor_tensor(T.h[:, t, :], T.ps[:, t, 2 * P:2 * P + D], inv[:, t:t + 1],
                                             T.h[:, t, :], ALU.mult, ALU.add).then_inc(s_h, 1)
                dve.wait_ge(s_h, NT)
def windowed_attention(nc, T, name, scores, scale, bias, heads, width, v, first_key_tile, ctxs):
    blocks = 12 // heads
    W = 384
    with ExitStack() as ctx:
        sb = lambda n, s: ctx.enter_context(nc.sbuf_tensor(f"{name}_{n}", s, F32))
        logit = sb("logit", [P, 2, 4, W])
        shifted = sb("shifted", [P, 2, 4 * W])
        prob = sb("prob", [P, 2, 12, P])
        probT = sb("probT", [P, 2, 12 * P])
        top = sb("top", [P, NT, heads])
        inv = sb("inv", [P, NT, heads])
        s_c, s_s, s_l, s_m, s_sh, s_e, s_t, s_pT, s_o, s_a = sems(
            nc, ctx, name, "chain", "scores", "logits", "maxima", "shifted", "exps", "transposed", "probT",
            "products", "contexts")
        with nc.Block() as block:
            @block.tensor
            def _(pe):
                def score(t):
                    if t:
                        pe.wait_ge(s_l, t)
                    for g in range(4):
                        lhsT, rhs = scores(t, g)
                        mm = pe.matmul(T.ps[:, g, 0:W], lhsT, rhs, start=True, stop=True)
                    mm.then_inc(s_s, 1)

                score(0)
                for t in range(NT):
                    if t + 1 < NT:
                        score(t + 1)
                    pe.wait_ge(s_e, t + 1)
                    if t:
                        pe.wait_ge(s_pT, 3 * t)
                    for b in range(12):
                        mm = pe.transpose(T.ps[:, 4 + b // 4, (b % 4) * P:(b % 4 + 1) * P],
                                          prob[:, t % 2, b, :], T.ident)
                        if b % 4 == 3:
                            mm.then_inc(s_t, 1)
                    if t:
                        pe.wait_ge(s_a, t)
                    pe.wait_ge(s_pT, 3 * (t + 1))
                    for n in range(heads):
                        for i in range(blocks):
                            b = n * blocks + i
                            mm = pe.matmul(T.ps[:, 7, n * (width + 1):(n + 1) * (width + 1)],
                                           probT[:, t % 2, b * P:(b + 1) * P],
                                           v[:, first_key_tile(t) + i, n, :],
                                           start=(i == 0), stop=(i == blocks - 1))
                    mm.then_inc(s_o, 1)

            @block.vector
            def _(dve):
                chain = Chain(dve, s_c)

                def context(t):
                    dve.wait_ge(s_o, t + 1)
                    o = T.ps[:, 7, 0:heads * (width + 1)].rearrange("p (h d) -> p h d", h=heads)
                    chain(dve.reciprocal(inv[:, t, :], o[:, :, width]))
                    dve.tensor_tensor(ctxs[:, t, :].rearrange("p (h d) -> p h d", h=heads), o[:, :, 0:width],
                                      inv[:, t, :].unsqueeze(2).to_broadcast([P, heads, width]),
                                      ALU.mult).then_inc(s_a, 1)

                for t in range(NT):
                    dve.wait_ge(s_s, t + 1)
                    if t >= 2:
                        dve.wait_ge(s_sh, t - 1)
                    dve.scalar_tensor_tensor(logit[:, t % 2, :, :], T.ps[:, 0:4, 0:W], scale, bias(t),
                                             ALU.mult, ALU.add).then_inc(s_l, 1)
                    dve.wait_ge(s_l, t + 1)
                    dve.tensor_reduce(top[:, t, :],
                                      logit[:, t % 2, :, :].rearrange("p g k -> p (g k)")
                                      .rearrange("p (h k) -> p h k", h=heads), AX_X, ALU.max).then_inc(s_m, 1)
                    if t:
                        context(t - 1)
                context(NT - 1)
                dve.wait_ge(s_a, NT)

            @block.gpsimd
            def _(pool):
                for t in range(NT):
                    pool.wait_ge(s_m, t + 1)
                    if t >= 2:
                        pool.wait_ge(s_e, t - 1)
                    pool.tensor_tensor(shifted[:, t % 2, :].rearrange("p (h k) -> p h k", h=heads),
                                       logit[:, t % 2, :, :].rearrange("p g k -> p (g k)")
                                       .rearrange("p (h k) -> p h k", h=heads),
                                       top[:, t, :].unsqueeze(2).to_broadcast([P, heads, 4 * W // heads]),
                                       ALU.subtract).then_inc(s_sh, 1)

            @block.scalar
            def _(act):
                for t in range(NT):
                    act.wait_ge(s_sh, t + 1)
                    if t >= 2:
                        act.wait_ge(s_t, 3 * (t - 1))
                    act.activation(prob[:, t % 2, :, :].rearrange("p b k -> p (b k)"), shifted[:, t % 2, :],
                                   ACT.Exp).then_inc(s_e, 1)
                    if t >= 2:
                        act.wait_ge(s_o, t - 1)
                    for q in range(3):
                        act.wait_ge(s_t, 3 * t + q + 1)
                        act.activation(probT[:, t % 2, q * HALF:(q + 1) * HALF], T.ps[:, 4 + q, :],
                                       ACT.Copy).then_inc(s_pT, 1)


def attention1_stage(nc, T):
    H, W = 12, 16
    with ExitStack() as ctx:
        sb = lambda n, s: ctx.enter_context(nc.sbuf_tensor(f"a1_{n}", s, F32))
        qT = sb("qT", [DC, 2, N_TOK])
        q_head = sb("q_head", [DC, 2, 6, N_TOK])
        v = sb("v", [P, NT, H, W + 1])
        ctxs = sb("ctxs", [P, NT, D])
        s_qmm, s_q, s_vmm, s_v, s_one, s_qh = sems(nc, ctx, "a1p", "q_products", "q", "v_products", "v", "ones",
                                                   "q_heads")
        with nc.Block() as block:
            @block.tensor
            def _(pe):
                pe.wait_ge(T.loaded["a1_w"], 16)
                pe.wait_ge(T.loaded["a1_proj"], 16)
                for c in range(2):
                    for half in range(2):
                        cols = slice(half * HALF, (half + 1) * HALF)
                        pe.matmul(T.ps[0:DC, 2 * c + half, :], T.w["a1_w"][:, 0, c * DC:(c + 1) * DC],
                                  T.xT[:, 0, cols], start=True, stop=False)
                        pe.matmul(T.ps[0:DC, 2 * c + half, :], T.w["a1_w"][0:DC, 1, c * DC:(c + 1) * DC],
                                  T.xT[0:DC, 1, cols], start=False, stop=True).then_inc(s_qmm, 1)
                for t in range(NT):
                    if t >= 4:
                        pe.wait_ge(s_v, t - 3)
                    pe.matmul(T.ps[:, 4 + t % 4, 0:D], T.xT[:, 0, t * P:(t + 1) * P], T.w["a1_w"][:, 0, :],
                              start=True, stop=False)
                    pe.matmul(T.ps[:, 4 + t % 4, 0:D], T.xT[0:DC, 1, t * P:(t + 1) * P], T.w["a1_w"][0:DC, 1, :],
                              start=False, stop=True).then_inc(s_vmm, 1)

            @block.scalar
            def _(act):
                for b in range(4):
                    act.wait_ge(s_qmm, b + 1)
                    act.activation(qT[:, b // 2, (b % 2) * HALF:(b % 2 + 1) * HALF], T.ps[0:DC, b, :],
                                   ACT.Copy).then_inc(s_q, 1)
                for t in range(NT):
                    act.wait_ge(s_vmm, t + 1)
                    act.activation(v[:, t, :, 0:W], T.ps[:, 4 + t % 4, 0:D].rearrange("p (h d) -> p h d", h=H),
                                   ACT.Copy).then_inc(s_v, 1)
                act.wait_ge(s_v, NT)

            @block.vector
            def _(dve):
                dve.memset(v[:, :, :, W:W + 1], 1.0).then_inc(s_one, 1)
                for c in range(2):
                    dve.wait_ge(s_q, 2 * c + 2)
                    for j in range(6):
                        dve.tensor_scalar(q_head[:, c, j, :], qT[:, c, :], T.consts[0:DC, C_M16 + j:C_M16 + j + 1],
                                          None, ALU.mult).then_inc(s_qh, 1)
                dve.wait_ge(s_one, 1)
                dve.wait_ge(s_qh, 12)

        def scores(t, g):
            c, j = g // 2, 3 * (g % 2)
            return qT[:, c, t * P:(t + 1) * P], q_head[:, c, j:j + 3, t * P:(t + 1) * P]

        windowed_attention(nc, T, "a1", scores, float(W) ** -0.5,
                           lambda t: T.causal3.unsqueeze(1).to_broadcast([P, 4, 384]),
                           H, W, v, lambda t: t, ctxs)

        s_tp, s_aT, s_mm, s_h = sems(nc, ctx, "a1o", "transposed", "aT", "products", "h")
        with nc.Block() as block:
            @block.tensor
            def _(pe):
                for t in range(NT):
                    for c in range(2):
                        mm = pe.transpose(T.ps[0:DC, t, c * P:(c + 1) * P], ctxs[:, t, c * DC:(c + 1) * DC], T.ident)
                    mm.then_inc(s_tp, 1)
                for t in range(NT):
                    pe.wait_ge(s_aT, t + 1)
                    pe.matmul(T.ps[:, t, 2 * P:2 * P + D], T.aT[:, 0, t * P:(t + 1) * P], T.w["a1_proj"][:, 0, :],
                              start=True, stop=False)
                    pe.matmul(T.ps[:, t, 2 * P:2 * P + D], T.aT[0:DC, 1, t * P:(t + 1) * P],
                              T.w["a1_proj"][0:DC, 1, :], start=False, stop=True).then_inc(s_mm, 1)

            @block.scalar
            def _(act):
                for t in range(NT):
                    act.wait_ge(s_tp, t + 1)
                    act.activation(T.aT[0:DC, :, t * P:(t + 1) * P],
                                   T.ps[0:DC, t, 0:2 * P].rearrange("p (c n) -> p c n", c=2),
                                   ACT.Copy).then_inc(s_aT, 1)

            @block.vector
            def _(dve):
                for t in range(NT):
                    dve.wait_ge(s_mm, t + 1)
                    dve.tensor_tensor(T.h[:, t, :], T.ps[:, t, 2 * P:2 * P + D], T.h[:, t, :],
                                      ALU.add).then_inc(s_h, 1)
                dve.wait_ge(s_h, NT)


def attention2_stage(nc, T, a):
    H, W, M = 4, 24, 64
    first_key_tile = lambda t: min(max(t - 1, 0), NT - 3)
    kind = lambda t: 0 if t == 0 else 2 if t == NT - 1 else 1
    with ExitStack() as ctx:
        sb = lambda n, s: ctx.enter_context(nc.sbuf_tensor(f"a2_{n}", s, F32))
        bias = sb("bias", [P, 3, 4, 384])
        xs = sb("xs", [DC, N_TOK])
        mid = sb("mid", [M, N_TOK])
        pre = sb("pre", [DC, N_TOK])
        qT = sb("qT", [DC, N_TOK])
        k_head = sb("k_head", [DC, H, N_TOK])
        v = sb("v", [P, NT, H, W + 1])
        ctxs = sb("ctxs", [P, NT, DC])
        ctxT = sb("ctxT", [DC, N_TOK])
        gT = T.aT[:, 0, :]
        s_b, s_f, s_xs, s_am, s_a, s_bm, s_p, s_g, s_qm, s_q, s_km, s_k, s_vm, s_v, s_one = sems(
            nc, ctx, "a2p", "bias", "fc1_products", "fc1", "convA_products", "convA", "convB_products",
            "pre", "gelu", "q_products", "q", "k_products", "k_heads", "v_products", "v", "ones")
        with nc.Block() as block:
            @block.sync
            def _(sp):
                sp.dma_start(bias[:, :, :, :].rearrange("p a b c -> p (a b c)"), a["a2_bias"]).then_inc(s_b, 16)
                sp.wait_ge(s_b, 16)

            @block.tensor
            def _(pe):
                for n in ("a2_fc1", "a2_convA", "a2_convB", "a2_qkv", "a2_proj", "a2_fc2", "a2_cols"):
                    pe.wait_ge(T.loaded[n], 16)
                cols = [slice(0, HALF), slice(HALF, N_TOK)]
                for i in range(2):
                    pe.matmul(T.ps[0:DC, i, :], T.w["a2_fc1"][:, 0, :], T.xT[:, 0, cols[i]], start=True, stop=False)
                    pe.matmul(T.ps[0:DC, i, :], T.w["a2_fc1"][0:DC, 1, :], T.xT[0:DC, 1, cols[i]],
                              start=False, stop=True).then_inc(s_f, 1)
                for i in range(2):
                    pe.wait_ge(s_xs, i + 1)
                    pe.matmul(T.ps[0:M, 2 + i, :], T.w["a2_convA"][:, :], xs[:, cols[i]],
                              start=True, stop=True).then_inc(s_am, 1)
                for i in range(2):
                    pe.wait_ge(s_a, i + 1)
                    pe.matmul(T.ps[0:DC, 4 + i, :], T.w["a2_convB"][:, :], mid[:, cols[i]],
                              start=True, stop=True).then_inc(s_bm, 1)
                for i in range(2):
                    pe.wait_ge(s_g, i + 1)
                    pe.matmul(T.ps[0:DC, i, :], T.w["a2_qkv"][:, 0:DC], gT[:, cols[i]],
                              start=True, stop=True).then_inc(s_qm, 1)
                    pe.matmul(T.ps[0:DC, 2 + i, :], T.w["a2_qkv"][:, DC:2 * DC], gT[:, cols[i]],
                              start=True, stop=True).then_inc(s_km, 1)
                for t in range(NT):
                    if t >= 2:
                        pe.wait_ge(s_v, t - 1)
                    pe.matmul(T.ps[:, 6 + t % 2, 0:DC], gT[:, t * P:(t + 1) * P], T.w["a2_qkv"][:, 2 * DC:3 * DC],
                              start=True, stop=True).then_inc(s_vm, 1)

            @block.scalar
            def _(act):
                for i in range(2):
                    act.wait_ge(s_f, i + 1)
                    act.activation(xs[:, i * HALF:(i + 1) * HALF], T.ps[0:DC, i, :], ACT.Copy).then_inc(s_xs, 1)
                for i in range(2):
                    act.wait_ge(s_am, i + 1)
                    act.activation(mid[:, i * HALF:(i + 1) * HALF], T.ps[0:M, 2 + i, :], ACT.Identity,
                                   bias=T.w["a2_cols"][0:M, 0:1]).then_inc(s_a, 1)
                for i in range(2):
                    act.wait_ge(s_p, i + 1)
                    act.activation(T.aT[0:DC, 0, i * HALF:(i + 1) * HALF], pre[:, i * HALF:(i + 1) * HALF],
                                   ACT.Gelu).then_inc(s_g, 1)
                for i in range(2):
                    act.wait_ge(s_qm, i + 1)
                    act.activation(qT[:, i * HALF:(i + 1) * HALF], T.ps[0:DC, i, :], ACT.Copy).then_inc(s_q, 1)
                for t in range(NT):
                    act.wait_ge(s_vm, t + 1)
                    act.activation(v[:, t, :, 0:W], T.ps[:, 6 + t % 2, 0:DC].rearrange("p (h d) -> p h d", h=H),
                                   ACT.Copy).then_inc(s_v, 1)
                act.wait_ge(s_v, NT)

            @block.vector
            def _(dve):
                dve.memset(v[:, :, :, W:W + 1], 1.0).then_inc(s_one, 1)
                for i in range(2):
                    cols = slice(i * HALF, (i + 1) * HALF)
                    dve.wait_ge(s_bm, i + 1)
                    dve.wait_ge(s_xs, i + 1)
                    dve.scalar_tensor_tensor(pre[:, cols], T.ps[0:DC, 4 + i, :], T.w["a2_cols"][:, 1:2], xs[:, cols],
                                             ALU.add, ALU.add).then_inc(s_p, 1)
                for i in range(2):
                    dve.wait_ge(s_km, i + 1)
                    for n in range(H):
                        dve.tensor_scalar(k_head[:, n, i * HALF:(i + 1) * HALF], T.ps[0:DC, 2 + i, :],
                                          T.consts[0:DC, C_M24 + n:C_M24 + n + 1], None, ALU.mult).then_inc(s_k, 1)
                dve.wait_ge(s_k, 2 * H)
                dve.wait_ge(s_one, 1)

        def scores(t, g):
            k0 = first_key_tile(t) * P
            return qT[:, t * P:(t + 1) * P], k_head[:, g, k0:k0 + 384]

        windowed_attention(nc, T, "a2", scores, float(W) ** -0.5, lambda t: bias[:, kind(t), :, :],
                           H, W, v, first_key_tile, ctxs)

        s_tp, s_cT, s_pm, s_pT, s_mm, s_hx, s_h = sems(nc, ctx, "a2o", "transposed", "ctxT", "proj_products",
                                                       "proj", "products", "h_x", "h")
        with nc.Block() as block:
            @block.tensor
            def _(pe):
                for t in range(NT):
                    mm = pe.transpose(T.ps[0:DC, t // 4, (t % 4) * P:(t % 4 + 1) * P], ctxs[:, t, :], T.ident)
                    if t % 4 == 3:
                        mm.then_inc(s_tp, 1)
                for i in range(2):
                    pe.wait_ge(s_cT, i + 1)
                    pe.matmul(T.ps[0:DC, 2 + i, :], T.w["a2_proj"][:, :], ctxT[:, i * HALF:(i + 1) * HALF],
                              start=True, stop=True).then_inc(s_pm, 1)
                for t in range(NT):
                    pe.wait_ge(s_pT, t // 4 + 1)
                    if t >= 4:
                        pe.wait_ge(s_h, t - 3)
                    pe.matmul(T.ps[:, 4 + t % 4, 0:D], gT[:, t * P:(t + 1) * P], T.w["a2_fc2"][:, :],
                              start=True, stop=True).then_inc(s_mm, 1)

            @block.scalar
            def _(act):
                for i in range(2):
                    act.wait_ge(s_tp, i + 1)
                    act.activation(ctxT[:, i * HALF:(i + 1) * HALF], T.ps[0:DC, i, :], ACT.Copy).then_inc(s_cT, 1)
                for i in range(2):
                    act.wait_ge(s_pm, i + 1)
                    act.activation(T.aT[0:DC, 0, i * HALF:(i + 1) * HALF], T.ps[0:DC, 2 + i, :], ACT.Identity,
                                   bias=T.w["a2_cols"][:, 2:3]).then_inc(s_pT, 1)

            @block.vector
            def _(dve):
                dve.tensor_tensor(T.h[:, :, :], T.h[:, :, :], T.xn[:, :, :], ALU.add).then_inc(s_hx, 1)
                dve.wait_ge(s_hx, 1)
                for t in range(NT):
                    dve.wait_ge(s_mm, t + 1)
                    dve.tensor_tensor(T.h[:, t, :], T.ps[:, 4 + t % 4, 0:D], T.h[:, t, :],
                                      ALU.add).then_inc(s_h, 1)
                dve.wait_ge(s_h, NT)


class Moe:

    def __init__(self, name, experts, picks, shared=False, renormalise=False):
        self.name, self.E, self.K, self.shared, self.renormalise = name, experts, picks, shared, renormalise
        self.C = picks + shared
        most = (N_TOK * self.C + experts * (P - 1)) // P
        self.tiles = -(-most // 4) * 4


def route_stage(nc, T, m, gate_w):
    E, K, C, name = m.E, m.K, m.C, m.name
    with ExitStack() as ctx:
        sb = lambda n, s, dt=F32: ctx.enter_context(nc.sbuf_tensor(f"{name}r_{n}", s, dt))
        logit = sb("logit", [P, NT, E])
        prob = sb("prob", [P, NT, E])
        small = sb("small", [P, 3, NT])
        best = sb("best", [P, NT, 8])
        best_at = sb("best_at", [P, NT, 8], U32)
        best_f = sb("best_f", [P, NT, 8])
        pick = sb("pick", [P, C, NT, E])
        taken = sb("taken", [P, NT, E])
        totals = sb("totals", [P, NT, E])
        before = sb("before", [P, NT + 1, E])
        n_tiles = sb("n_tiles", [P, E])
        ends = sb("ends", [P, E])
        zeros = sb("zeros", [P, E])
        start = sb("start", [P, E])
        slot = sb("slot", [P, NT, E])
        slot_of = sb("slot_of", [P, C, NT, E])
        slot_f = sb("slot_f", [P, C, NT])
        past = sb("past", [1, m.tiles, E])
        map_f = sb("map_f", [1, m.tiles + 1])
        round_used = sb("round_used", [1, m.tiles // U])
        s_c, s_mm, s_sh, s_e, s_tk, s_rk, s_sl = sems(
            nc, ctx, f"{name}r", "chain", "logits", "shifted", "exps", "taken", "ranks", "slots")
        iota = T.consts[:, C_IOTA:C_IOTA + E]
        over_tiles = lambda x: x.unsqueeze(1).to_broadcast([P, NT, E])
        over_experts = lambda x: x.unsqueeze(2).to_broadcast([P, NT, E])
        with nc.Block() as block:
            @block.tensor
            def _(pe):
                pe.wait_ge(T.loaded[gate_w], 16)
                w = T.w[gate_w]
                for t in range(NT):
                    pe.matmul(T.ps[:, 0, t * E:(t + 1) * E], T.xT[:, 0, t * P:(t + 1) * P], w[:, 0, :],
                              start=True, stop=False)
                    mm = pe.matmul(T.ps[:, 0, t * E:(t + 1) * E], T.xT[0:DC, 1, t * P:(t + 1) * P],
                                   w[0:DC, 1, :], start=False, stop=True)
                mm.then_inc(s_mm, 1)
                pe.wait_ge(s_tk, 1)
                both = taken[:, :, :].rearrange("p t e -> p (t e)")
                pe.matmul(T.ps[:, 1, 0:NT * E], T.consts[:, C_LT:C_LT + P], both, start=True, stop=True)
                pe.matmul(T.ps[:, 2, 0:NT * E], T.ones[:, :], both, start=True, stop=True).then_inc(s_rk, 1)

            @block.scalar
            def _(act):
                act.wait_ge(s_sh, 1)
                act.activation(prob[:, :, :], logit[:, :, :], ACT.Exp).then_inc(s_e, 1)

            @block.vector
            def _(dve):
                chain = Chain(dve, s_c)
                dve.wait_ge(s_mm, 1)
                chain(dve.tensor_copy(logit[:, :, :], T.ps[:, 0, 0:NT * E].rearrange("p (t e) -> p t e", e=E)))
                if m.shared:
                    chain(dve.memset(logit[:, :, 0:1], -1.0e9))
                chain(dve.tensor_reduce(small[:, 0, :], logit[:, :, :], AX_X, ALU.max))
                dve.tensor_tensor(logit[:, :, :], logit[:, :, :], over_experts(small[:, 0, :]),
                                  ALU.subtract).then_inc(s_sh, 1)
                dve.wait_ge(s_e, 1)
                chain(dve.tensor_reduce(small[:, 1, :], prob[:, :, :], AX_X, ALU.add))
                chain(dve.reciprocal(small[:, 2, :], small[:, 1, :]))
                chain(dve.tensor_tensor(prob[:, :, :], prob[:, :, :], over_experts(small[:, 2, :]), ALU.mult))
                for t in range(NT):
                    ins = dve.max(best[:, t, :], prob[:, t, :])
                chain(ins)
                for t in range(NT):
                    ins = dve.max_index(best_at[:, t, :], best[:, t, :], prob[:, t, :])
                chain(ins)
                chain(dve.tensor_copy(best_f[:, :, :], best_at[:, :, :]))
                for k in range(K):
                    chain(dve.tensor_tensor(pick[:, k, :, :], over_tiles(iota), over_experts(best_f[:, :, k]),
                                            ALU.is_equal))
                    dve_w = dve.tensor_copy(m.gate[:, k, :], best[:, :, k])
                    chain(dve_w)
                if m.shared:
                    chain(dve.memset(pick[:, K, :, :], 0.0))
                    chain(dve.memset(pick[:, K, :, 0:1], 1.0))
                    chain(dve.memset(m.gate[:, K, :], 1.0))
                if m.renormalise:
                    chain(dve.tensor_tensor(small[:, 0, :], m.gate[:, 0, :], m.gate[:, 1, :], ALU.add))
                    chain(dve.tensor_scalar(small[:, 0, :], small[:, 0, :], 1.0e-20, None, ALU.add))
                    chain(dve.reciprocal(small[:, 1, :], small[:, 0, :]))
                    for k in range(K):
                        chain(dve.tensor_tensor(m.gate[:, k, :], m.gate[:, k, :], small[:, 1, :], ALU.mult))
                chain(dve.tensor_tensor(taken[:, :, :], pick[:, 0, :, :], pick[:, 1, :, :], ALU.add))
                for k in range(2, C):
                    chain(dve.tensor_tensor(taken[:, :, :], taken[:, :, :], pick[:, k, :, :], ALU.add))
                dve.sem_inc(s_tk, 1)
                dve.wait_ge(s_rk, 1)
                chain(dve.memset(before[:, 0, :], 0.0))
                chain(dve.memset(zeros[:, :], 0.0))
                chain(dve.tensor_copy(totals[:, :, :], T.ps[:, 2, 0:NT * E].rearrange("p (t e) -> p t e", e=E)))
                for t in range(NT):
                    chain(dve.tensor_tensor(before[:, t + 1, :], before[:, t, :], totals[:, t, :], ALU.add))
                chain(dve.tensor_scalar(n_tiles[:, :], before[:, NT, :], 0.0, None, ALU.is_gt))
                for j in range(1, NT * (1 + m.shared)):
                    chain(dve.scalar_tensor_tensor(n_tiles[:, :], before[:, NT, :], float(P * j), n_tiles[:, :],
                                                   ALU.is_gt, ALU.add))
                chain(dve.tensor_tensor_scan(ends[:, :], n_tiles[:, :], zeros[:, :], 0.0, ALU.add, ALU.add))
                chain(dve.tensor_tensor(start[:, :], ends[:, :], n_tiles[:, :], ALU.subtract))
                chain(dve.tensor_scalar(start[:, :], start[:, :], float(P), None, ALU.mult))
                chain(dve.tensor_tensor(slot[:, :, :], T.ps[:, 1, 0:NT * E].rearrange("p (t e) -> p t e", e=E),
                                        before[:, 0:NT, :], ALU.add))
                chain(dve.tensor_tensor(slot[:, :, :], slot[:, :, :], over_tiles(start[:, :]), ALU.add))
                for k in range(C):
                    chain(dve.tensor_tensor(slot_of[:, k, :, :], pick[:, k, :, :], slot[:, :, :], ALU.mult))
                chain(dve.tensor_reduce(slot_f[:, :, :].rearrange("p c t -> p (c t)"),
                                        slot_of[:, :, :, :].rearrange("p c t e -> p (c t) e"), AX_X, ALU.add))
                dve.tensor_copy(m.slots[:, :, :], slot_f[:, :, :]).then_inc(s_sl, 1)
                chain(dve.tensor_tensor(past[:, :, :],
                                        T.consts[0:1, C_IOTA:C_IOTA + m.tiles].unsqueeze(2)
                                        .to_broadcast([1, m.tiles, E]),
                                        ends[0:1, :].unsqueeze(1).to_broadcast([1, m.tiles, E]), ALU.is_ge))
                chain(dve.tensor_reduce(map_f[:, 0:m.tiles], past[:, :, :], AX_X, ALU.add))
                chain(dve.tensor_scalar(map_f[:, 0:m.tiles], map_f[:, 0:m.tiles], float(E - 1), None, ALU.min))
                chain(dve.tensor_scalar(round_used[:, :], T.consts[0:1, C_IOTA:C_IOTA + m.tiles // U], float(U),
                                        ends[0:1, E - 1:E], ALU.mult, ALU.is_lt))
                chain(dve.tensor_reduce(map_f[:, m.tiles:m.tiles + 1], round_used[:, :], AX_X, ALU.add))
                chain(dve.tensor_copy(m.expert_of[:, :], map_f[:, :]))

            @block.gpsimd
            def _(pool):
                pool.wait_ge(s_sl, 1)
                pool.wait_ge(T.s_cleared, 96)
                for t in range(NT):
                    for k in range(C):
                        pool.indirect_dma_start(
                            m.slots_x, bass.IndirectOffsetOnAxis(m.slots[:, k, t:t + 1], 0),
                            T.xn[:, t, :], None).then_inc(m.s_scattered, 16)
                pool.wait_ge(m.s_scattered, 16 * NT * C)


def combine_stage(nc, T, m, plus_x):
    with ExitStack() as ctx:
        y = ctx.enter_context(nc.sbuf_tensor(f"{m.name}c_y", [P, NT, m.C, D], F32))
        s_c, s_h = sems(nc, ctx, f"{m.name}c", "chain", "h")
        with nc.Block() as block:
            @block.gpsimd
            def _(pool):
                for t in range(NT):
                    for k in range(m.C):
                        pool.indirect_dma_start(
                            y[:, t, k, :], None, m.slots_y,
                            bass.IndirectOffsetOnAxis(m.slots[:, k, t:t + 1], 0)).then_inc(m.s_gathered[t], 16)

            @block.vector
            def _(dve):
                chain = Chain(dve, s_c)
                if plus_x:
                    chain(dve.tensor_tensor(T.h[:, :, :], T.h[:, :, :], T.xn[:, :, :], ALU.add))
                for t in range(NT):
                    dve.wait_ge(m.s_gathered[t], 16 * m.C)
                    for k in range(m.C):
                        chain(dve.scalar_tensor_tensor(T.h[:, t, :], y[:, t, k, :], m.gate[:, k, t:t + 1],
                                                       T.h[:, t, :], ALU.mult, ALU.add))


U = 4


def every_round(eng, m, body):
    rounds = m.tiles // U
    used = eng.value_load(m.expert_of[0:1, m.tiles:m.tiles + 1], min_val=1, max_val=rounds)
    body(Loop(0, True))
    with eng.Fori(1, rounds) as i:
        with eng.If(i < used):
            body(Loop(i, False))
    return used


class Loop:

    def __init__(self, i, first):
        self.i, self.first = i, first

    def after(self, u, times=1, back=0):
        return self.i * (U * times) + (u + 1 - back) * times


def expert_loop(nc, T, m, weights, layers):
    name = m.name
    with ExitStack() as ctx:
        sb = lambda n, s, dt=F32: ctx.enter_context(nc.sbuf_tensor(f"{name}e_{n}", s, dt))
        x = sb("x", [P, U, D])
        xsT = sb("xsT", [DC + 1, U, 2, P])
        y = sb("y", [P, U, D])
        bufs = [sb(f"w{n}", [w.shape[1], U, w.shape[2]]) for n, w in enumerate(weights)]
        s_x = sems(nc, ctx, f"{name}e", *[f"x{u}" for u in range(U)])
        s_w = [sems(nc, ctx, f"{name}e_w{n}", *[f"in{u}" for u in range(U)]) for n in range(len(weights))]
        s_out = m.s_stored
        s_tp, s_xs, s_ymm, s_y, s_one = sems(
            nc, ctx, f"{name}e", "transposed", "xsT", "y_products", "y", "ones")
        S = dict(xsT=xsT, y=y, bufs=bufs, s_w=s_w, s_xs=s_xs, s_ymm=s_ymm, s_y=s_y, ctx=ctx)
        bodies = layers(S)
        with nc.Block() as block:
            @block.sync
            def _(sp):
                def body(at):
                    for u in range(U):
                        expert = sp.value_load(m.expert_of[0:1, bass.ds(at.i * U + u, 1)], min_val=0,
                                               max_val=m.E - 1)
                        if not at.first:
                            sp.wait_ge(s_tp, at.after(u, back=U))
                        sp.dma_start(x[:, u, :], m.slots_x[bass.ds(at.i * (U * P) + u * P, P), :]
                                     ).then_inc(s_x[u], 16)
                        if not at.first:
                            sp.wait_ge(s_ymm, at.after(u, back=U))
                        for n, w in enumerate(weights):
                            sp.dma_start(bufs[n][:, u, :],
                                         w[bass.ds(expert, 1), :, :].rearrange("a p n -> p (a n)")
                                         ).then_inc(s_w[n][u], 16)
                every_round(sp, m, body)

            @block.gpsimd
            def _(pool):
                def body(at):
                    for pair in range(0, U, 2):
                        if "pool" in bodies:
                            bodies["pool"](pool, at, (pair, pair + 1))
                        for u in (pair, pair + 1):
                            pool.wait_ge(s_y, at.after(u))
                            pool.dma_start(m.slots_y[bass.ds(at.i * (U * P) + u * P, P), :], y[:, u, :]
                                           ).then_inc(s_out[u], 16)
                used = every_round(pool, m, body)
                for u in range(U):
                    pool.wait_ge(s_out[u], used * 16)

            @block.tensor
            def _(pe):
                def body(at):
                    for pair in range(0, U, 2):
                        for u in (pair, pair + 1):
                            pe.wait_ge(s_x[u], 16 * (at.i + 1))
                            for c in range(2):
                                mm = pe.transpose(T.ps[0:DC, 4 * (u % 2), c * P:(c + 1) * P],
                                                  x[:, u, c * DC:(c + 1) * DC], T.ident)
                            mm.then_inc(s_tp, 1)
                        bodies["pe"](pe, at, (pair, pair + 1))
                every_round(pe, m, body)

            @block.vector
            def _(dve):
                dve.memset(xsT[DC:DC + 1, :, 0, :], 1.0).then_inc(s_one, 1)
                dve.wait_ge(s_one, 1)
                bodies["dve_first"](dve)
                def body(at):
                    for pair in range(0, U, 2):
                        for u in (pair, pair + 1):
                            dve.wait_ge(s_tp, at.after(u))
                            dve.tensor_copy(xsT[0:DC, u, :, :],
                                            T.ps[0:DC, 4 * (u % 2), 0:2 * P].rearrange("p (c n) -> p c n", c=2)
                                            ).then_inc(s_xs, 1)
                        bodies["dve"](dve, at, (pair, pair + 1))
                        for u in (pair, pair + 1):
                            dve.wait_ge(s_ymm, at.after(u))
                            if not at.first:
                                dve.wait_ge(s_out[u], 16 * at.i)
                            dve.tensor_copy(y[:, u, :], T.ps[:, 4 * (u % 2) + 3, 0:D]).then_inc(s_y, 1)
                every_round(dve, m, body)

            @block.scalar
            def _(act):
                def body(at):
                    for pair in range(0, U, 2):
                        bodies["act"](act, at, (pair, pair + 1))
                every_round(act, m, body)


def moe1(nc, T, a):
    m = T.m1
    F, FC = 768, 6
    route_stage(nc, T, m, "e1_gate")

    def layers(S):
        xsT, (w1, w2) = S["xsT"], S["bufs"]
        h1 = S["ctx"].enter_context(nc.sbuf_tensor("m1_h1", [P, U, F], F32))
        s_1, s_g = sems(nc, S["ctx"], "m1x", "layer1", "gelu")

        def pe(pe, at, tiles):
            for u in tiles:
                pe.wait_ge(S["s_xs"], at.after(u))
                pe.wait_ge(S["s_w"][0][u], 16 * (at.i + 1))
                b = 4 * (u % 2) + 1
                flat = T.ps[:, b:b + 2, :].rearrange("p b n -> p (b n)")
                for j in range(FC):
                    out = flat[:, j * P:(j + 1) * P]
                    pe.matmul(out, w1[:, u, j * P:(j + 1) * P], xsT[:, u, 0, :], start=True, stop=False)
                    mm = pe.matmul(out, w1[0:DC, u, F + j * P:F + (j + 1) * P], xsT[0:DC, u, 1, :],
                                   start=False, stop=True)
                mm.then_inc(s_1, 1)
            for u in tiles:
                pe.wait_ge(s_g, at.after(u))
                pe.wait_ge(S["s_w"][1][u], 16 * (at.i + 1))
                if not (at.first and tiles[0] == 0):
                    pe.wait_ge(S["s_y"], at.after(tiles[0], back=1))
                out = T.ps[:, 4 * (u % 2) + 3, 0:D]
                for j in range(FC):
                    pe.matmul(out, h1[:, u, j * P:(j + 1) * P], w2[:, u, j * D:(j + 1) * D],
                              start=(j == 0), stop=False)
                pe.matmul(out, T.ones[DC:DC + 1, :], w1[DC:DC + 1, u, F:F + D],
                          start=False, stop=True).then_inc(S["s_ymm"], 1)

        def act(act, at, tiles):
            for u in tiles:
                act.wait_ge(s_1, at.after(u))
                b = 4 * (u % 2) + 1
                act.activation(h1[:, u, :], T.ps[:, b:b + 2, :].rearrange("p b n -> p (b n)")[:, 0:F],
                               ACT.Gelu).then_inc(s_g, 1)

        return {"pe": pe, "act": act, "dve": lambda dve, at, tiles: None, "dve_first": lambda dve: None}

    expert_loop(nc, T, m, [a["e1_w1"], a["e1_w2"]], layers)
    combine_stage(nc, T, m, plus_x=True)


def moe2(nc, T, a):
    m = T.m2
    F, FC, B = 512, 4, 64
    W3 = FC * F
    B2 = W3 + FC * B
    route_stage(nc, T, m, "e2_gate")

    def layers(S):
        xsT, (w1, w23, wl) = S["xsT"], S["bufs"]
        sb = lambda n, s: S["ctx"].enter_context(nc.sbuf_tensor(f"m2_{n}", s, F32))
        h1, h2, z = sb("h1", [P, U, F]), sb("h2", [P, U, F]), sb("z", [B + 1, U, P])
        s_1, s_g1, s_2, s_g2, s_3, s_z, s_one = sems(nc, S["ctx"], "m2x", "layer1", "gelu1", "layer2", "gelu2",
                                                     "layer3", "z", "ones")

        def pe(pe, at, tiles):
            for u in tiles:
                pe.wait_ge(S["s_xs"], at.after(u))
                pe.wait_ge(S["s_w"][0][u], 16 * (at.i + 1))
                for j in range(FC):
                    out = T.ps[:, 4 * (u % 2) + 1, j * P:(j + 1) * P]
                    pe.matmul(out, w1[:, u, j * P:(j + 1) * P], xsT[:, u, 0, :], start=True, stop=False)
                    mm = pe.matmul(out, w1[0:DC, u, F + j * P:F + (j + 1) * P], xsT[0:DC, u, 1, :],
                                   start=False, stop=True)
                mm.then_inc(s_1, 1)
            for u in tiles:
                pe.wait_ge(s_g1, at.after(u))
                pe.wait_ge(S["s_w"][1][u], 16 * (at.i + 1))
                for j in range(FC):
                    out = T.ps[:, 4 * (u % 2) + 2, j * P:(j + 1) * P]
                    for k in range(FC):
                        mm = pe.matmul(out, w23[:, u, k * F + j * P:k * F + (j + 1) * P],
                                       h1[:, u, k * P:(k + 1) * P], start=(k == 0), stop=(k == FC - 1))
                mm.then_inc(s_2, 1)
            for u in tiles:
                pe.wait_ge(s_g2, at.after(u, times=FC))
                if not (at.first and tiles[0] == 0):
                    pe.wait_ge(S["s_y"], at.after(tiles[0], back=1))
                for k in range(FC):
                    mm = pe.matmul(T.ps[0:B, 4 * (u % 2) + 3, 384:512], w23[:, u, W3 + k * B:W3 + (k + 1) * B],
                                   h2[:, u, k * P:(k + 1) * P], start=(k == 0), stop=(k == FC - 1))
                mm.then_inc(s_3, 1)
            for u in tiles:
                pe.wait_ge(s_z, at.after(u))
                pe.wait_ge(S["s_w"][2][u], 16 * (at.i + 1))
                pe.matmul(T.ps[:, 4 * (u % 2) + 3, 0:D], z[:, u, :], wl[:, u, 0:D],
                          start=True, stop=True).then_inc(S["s_ymm"], 1)

        def act(act, at, tiles):
            for u in tiles:
                act.wait_ge(s_1, at.after(u))
                act.activation(h1[:, u, :], T.ps[:, 4 * (u % 2) + 1, :], ACT.Gelu).then_inc(s_g1, 1)
            for u in tiles:
                act.wait_ge(s_2, at.after(u))
                for j in range(FC):
                    act.activation(h2[:, u, j * P:(j + 1) * P], T.ps[:, 4 * (u % 2) + 2, j * P:(j + 1) * P],
                                   ACT.Gelu, bias=w23[:, u, B2 + j:B2 + j + 1]).then_inc(s_g2, 1)

        def dve(dve, at, tiles):
            for u in tiles:
                dve.wait_ge(s_3, at.after(u))
                dve.wait_ge(S["s_w"][2][u], 16 * (at.i + 1))
                dve.tensor_scalar(z[0:B, u, :], T.ps[0:B, 4 * (u % 2) + 3, 384:512], wl[0:B, u, D:D + 1], None,
                                  ALU.add).then_inc(s_z, 1)

        def dve_first(dve):
            dve.memset(z[B:B + 1, :, :], 1.0).then_inc(s_one, 1)
            dve.wait_ge(s_one, 1)

        return {"pe": pe, "act": act, "dve": dve, "dve_first": dve_first}

    expert_loop(nc, T, m, [a["e2_w1"], a["e2_w23"], a["e2_wl"]], layers)
    combine_stage(nc, T, m, plus_x=False)


def moe0(nc, T, a):
    m = T.m0
    F, FC = 384, 3
    LNW = FC * D
    LNB = LNW + FC
    route_stage(nc, T, m, "e0_gate")

    def layers(S):
        xsT, (w1, w2) = S["xsT"], S["bufs"]
        sb = lambda n, s: S["ctx"].enter_context(nc.sbuf_tensor(f"m0_{n}", s, F32))
        g, gn, hT = sb("g", [P, U, F]), sb("gn", [P, U, F]), sb("hT", [P, U, F])
        stats, mv, rstd, power = sb("stats", [P, U, 6]), sb("mv", [P, U, 2]), sb("rstd", [P, U]), sb("power", [P, 1])
        s_1, s_g, s_st, s_mv, s_var, s_r, s_n, s_t, s_hT, s_pw, s_waited = sems(
            nc, S["ctx"], "m0x", "layer1", "gelu", "stats", "moments", "variance", "rstd", "normed", "transposed",
            "hT", "power", "waited")

        def pe(pe, at, tiles):
            for u in tiles:
                pe.wait_ge(S["s_xs"], at.after(u))
                pe.wait_ge(S["s_w"][0][u], 16 * (at.i + 1))
                out = T.ps[:, 4 * (u % 2) + 1, 0:F]
                pe.matmul(out, xsT[:, u, 0, :], w1[:, u, 0:F], start=True, stop=False)
                pe.matmul(out, xsT[0:DC, u, 1, :], w1[0:DC, u, F:2 * F], start=False, stop=True).then_inc(s_1, 1)
            for u in tiles:
                pe.wait_ge(s_n, at.after(u))
                for j in range(FC):
                    mm = pe.transpose(T.ps[:, 4 * (u % 2) + 2, j * P:(j + 1) * P], gn[:, u, j * P:(j + 1) * P], T.ident)
                mm.then_inc(s_t, 1)
            for u in tiles:
                pe.wait_ge(s_hT, at.after(u, times=FC))
                pe.wait_ge(S["s_w"][1][u], 16 * (at.i + 1))
                if not (at.first and tiles[0] == 0):
                    pe.wait_ge(S["s_y"], at.after(tiles[0], back=1))
                out = T.ps[:, 4 * (u % 2) + 3, 0:D]
                for j in range(FC):
                    pe.matmul(out, hT[:, u, j * P:(j + 1) * P], w2[:, u, j * D:(j + 1) * D],
                              start=(j == 0), stop=False)
                pe.matmul(out, T.ones[DC:DC + 1, :], w1[DC:DC + 1, u, F:F + D],
                          start=False, stop=True).then_inc(S["s_ymm"], 1)

        def act(act, at, tiles):
            for u in tiles:
                act.wait_ge(s_1, at.after(u))
                act.activation(g[:, u, :], T.ps[:, 4 * (u % 2) + 1, 0:F], ACT.Gelu).then_inc(s_g, 1)
            for u in tiles:
                act.wait_ge(s_t, at.after(u))
                act.wait_ge(S["s_w"][1][u], 16 * (at.i + 1))
                for j in range(FC):
                    act.activation(hT[:, u, j * P:(j + 1) * P], T.ps[:, 4 * (u % 2) + 2, j * P:(j + 1) * P],
                                   ACT.Identity, bias=w2[:, u, LNB + j:LNB + j + 1],
                                   scale=w2[:, u, LNW + j:LNW + j + 1]).then_inc(s_hT, 1)

        def dve(dve, at, tiles):
            for u in tiles:
                dve.wait_ge(s_g, at.after(u))
                dve.bn_stats(stats[:, u, :], g[:, u, :]).then_inc(s_st, 1)
            for u in tiles:
                wait_alone(dve, s_st, at.after(u), s_waited)
                dve.bn_aggr(mv[:, u, :], stats[:, u, :]).then_inc(s_mv, 1)
            for u in tiles:
                dve.wait_ge(s_mv, at.after(u))
                dve.tensor_scalar(mv[:, u, 1:2], mv[:, u, 1:2], 1e-5, None, ALU.add).then_inc(s_var, 1)
            for u in tiles:
                dve.wait_ge(s_r, at.after(u))
                dve.tensor_scalar(gn[:, u, :], g[:, u, :], mv[:, u, 0:1], rstd[:, u:u + 1],
                                  ALU.subtract, ALU.mult).then_inc(s_n, 1)

        def pool(pool, at, tiles):
            for u in tiles:
                pool.wait_ge(s_var, at.after(u))
                pool.tensor_tensor(rstd[:, u:u + 1], mv[:, u, 1:2], power[:, :], ALU.pow).then_inc(s_r, 1)

        def dve_first(dve):
            dve.memset(power[:, :], -0.5).then_inc(s_pw, 1)
            dve.wait_ge(s_pw, 1)

        return {"pe": pe, "act": act, "dve": dve, "dve_first": dve_first, "pool": pool}

    expert_loop(nc, T, m, [a["e0_w1"], a["e0_w2"]], layers)
    combine_stage(nc, T, m, plus_x=False)


def rms_stage(nc, T, name, weight):
    with ExitStack() as ctx:
        sb = lambda n, s: ctx.enter_context(nc.sbuf_tensor(f"{name}_{n}", s, F32))
        square, ms, rstd, power, xr = sb("square", [P, D]), sb("ms", [P, NT]), sb("rstd", [P, NT]), \
            sb("power", [P, NT]), sb("xr", [P, NT, D])
        s_c, s_sq, s_ms, s_r, s_xr, s_tp, s_cp = sems(nc, ctx, name, "chain", "squares", "mean_square", "rstd",
                                                      "xr", "transposed", "copied")
        with nc.Block() as block:
            @block.scalar
            def _(act):
                for t in range(NT):
                    if t:
                        act.wait_ge(s_sq, t)
                    act.activation(square[:, :], T.xn[:, t, :], ACT.Square,
                                   accum_out=ms[:, t:t + 1]).then_inc(s_sq, 1)

            @block.gpsimd
            def _(pool):
                pool.wait_ge(s_ms, 1)
                pool.tensor_tensor(rstd[:, :], ms[:, :], power[:, :], ALU.pow).then_inc(s_r, 1)

            @block.vector
            def _(dve):
                chain = Chain(dve, s_c)
                chain(dve.memset(power[:, :], -0.5))
                dve.wait_ge(s_sq, NT)
                dve.wait_ge(T.loaded["a3_norm1"], 16)
                dve.wait_ge(T.loaded["a3_norm2"], 16)
                dve.tensor_scalar(ms[:, :], ms[:, :], 1.0 / D, 1e-6, ALU.mult, ALU.add).then_inc(s_ms, 1)
                dve.wait_ge(s_r, 1)
                for t in range(NT):
                    dve.tensor_scalar(xr[:, t, :], T.xn[:, t, :], rstd[:, t:t + 1], None,
                                      ALU.mult).then_inc(s_xr, 1)
                for t in range(NT):
                    dve.wait_ge(s_tp, t + 1)
                    for c in range(2):
                        dve.tensor_scalar(T.xT[0:DC, c, t * P:(t + 1) * P], T.ps[0:DC, t, c * P:(c + 1) * P],
                                          weight[:, c:c + 1], None, ALU.mult).then_inc(s_cp, 1)
                dve.wait_ge(s_cp, 2 * NT)

            @block.tensor
            def _(pe):
                for t in range(NT):
                    pe.wait_ge(s_xr, t + 1)
                    for c in range(2):
                        mm = pe.transpose(T.ps[0:DC, t, c * P:(c + 1) * P], xr[:, t, c * DC:(c + 1) * DC], T.ident)
                    mm.then_inc(s_tp, 1)


def mixer_stage(nc, T, a):
    H, HD, DI, NS = 6, 64, 384, 8
    LANES = H * 16
    rms_stage(nc, T, "x1", T.w["a3_norm1"])
    with ExitStack() as ctx:
        sb = lambda n, s: ctx.enter_context(nc.sbuf_tensor(f"a3_{n}", s, F32))
        vT = sb("vT", [P, 3, N_TOK])
        gate = sb("gate", [P, NT, DI])
        BT = sb("BT", [H * NS, N_TOK])
        C_head = sb("C_head", [H * NS, H, N_TOK])
        u = sb("u", [P, NT, DI])
        response = sb("response", [P, NT, H, P])
        params = nc.dram_tensor("a3_params_out", (2 * H, N_TOK), F32, kind="Internal").ap()
        g_dram = nc.dram_tensor("a3_response_out", (LANES, SEQ, SEQ), F32, kind="Internal").ap()

        with ExitStack() as inner:
            sb2 = lambda n, s: inner.enter_context(nc.sbuf_tensor(f"a3p_{n}", s, F32))
            vpad = sb2("vpad", [P, 3, 16, SEQ + 3])
            conv = sb2("conv", [P, 3, 16, SEQ])
            bc = sb2("bc", [P, NT, 96])
            sq = sb2("sq", [P, NT, 96])
            norm = sb2("norm", [P, NT, 12])
            rnorm = sb2("rnorm", [P, NT, 12])
            power = sb2("power", [P, NT, 12])
            par = sb2("par", [2 * H, N_TOK])
            (s_c, s_vm, s_vp, s_pm, s_par, s_pd, s_gm, s_g, s_cv, s_v, s_bm, s_n, s_r, s_bn, s_tp, s_ev, s_zero,
             s_um, s_u) = sems(
                nc, inner, "a3p", "chain", "v_products", "v_padded", "param_products", "params", "params_out",
                "gate_products", "gate", "conv", "v", "bc_products", "norms", "rnorm", "bc", "transposed",
                "evacuated", "zeros", "u_transposed", "u")
            with nc.Block() as block:
                @block.tensor
                def _(pe):
                    pe.wait_ge(T.loaded["a3_in"], 16)
                    for half in range(2):
                        cols = slice(half * HALF, (half + 1) * HALF)
                        for c in range(2):
                            mm = pe.matmul(T.ps[0:2 * H, 6 + half, :], T.w["a3_in"][:, c, 2 * DI:], T.xT[0:DC, c, cols],
                                           start=(c == 0), stop=(c == 1))
                        mm.then_inc(s_pm, 1)
                    for j in range(3):
                        for half in range(2):
                            cols = slice(half * HALF, (half + 1) * HALF)
                            for c in range(2):
                                mm = pe.matmul(T.ps[:, 2 * j + half, :], T.w["a3_in"][:, c, DI + j * P:DI + (j + 1) * P],
                                               T.xT[0:DC, c, cols], start=(c == 0), stop=(c == 1))
                            mm.then_inc(s_vm, 1)
                    pe.wait_ge(s_par, 2)
                    for t in range(NT):
                        if t >= 2:
                            pe.wait_ge(s_g, t - 1)
                        for c in range(2):
                            mm = pe.matmul(T.ps[:, 6 + t % 2, 0:DI], T.xT[0:DC, c, t * P:(t + 1) * P],
                                           T.w["a3_in"][:, c, 0:DI], start=(c == 0), stop=(c == 1))
                        mm.then_inc(s_gm, 1)
                    pe.wait_ge(T.loaded["a3_bc"], 16)
                    for j in range(3):
                        pe.wait_ge(s_v, j + 1)
                    pe.wait_ge(s_vp, 6)
                    for t in range(NT):
                        out = T.ps[:, t // 4, (t % 4) * 96:(t % 4 + 1) * 96]
                        for j in range(3):
                            mm = pe.matmul(out, vT[:, j, t * P:(t + 1) * P], T.w["a3_bc"][:, j, :],
                                           start=(j == 0), stop=(j == 2))
                    mm.then_inc(s_bm, 1)
                    for t in range(NT):
                        if t >= 2:
                            pe.wait_ge(s_u, t - 1)
                        elif t == 0:
                            pe.wait_ge(s_g, NT)
                        for j in range(3):
                            mm = pe.transpose(T.ps[:, 6 + t % 2, j * P:(j + 1) * P], vT[:, j, t * P:(t + 1) * P],
                                              T.ident)
                        mm.then_inc(s_um, 1)
                    pe.wait_ge(s_bn, 1)
                    for t in range(NT):
                        for k in range(2):
                            mm = pe.transpose(T.ps[0:48, 2 + 2 * k + t // 4, (t % 4) * P:(t % 4 + 1) * P],
                                              bc[:, t, 48 * k:48 * k + 48], T.ident)
                    mm.then_inc(s_tp, 1)

                @block.scalar
                def _(act):
                    for half in range(2):
                        act.wait_ge(s_pm, half + 1)
                        act.activation(par[:, half * HALF:(half + 1) * HALF], T.ps[0:2 * H, 6 + half, :],
                                       ACT.Copy).then_inc(s_par, 1)
                    act.wait_ge(s_zero, 1)
                    for b in range(6):
                        act.wait_ge(s_vm, b + 1)
                        act.activation(vpad[:, b // 2, (b % 2) * 8:(b % 2 + 1) * 8, 3:],
                                       T.ps[:, b, :].rearrange("p (s n) -> p s n", n=SEQ),
                                       ACT.Copy).then_inc(s_vp, 1)
                    for t in range(NT):
                        act.wait_ge(s_gm, t + 1)
                        act.activation(gate[:, t, :], T.ps[:, 6 + t % 2, 0:DI], ACT.Silu).then_inc(s_g, 1)
                    for j in range(3):
                        act.wait_ge(s_cv, j + 1)
                        act.activation(vT[:, j, :], conv[:, j, :, :].rearrange("p s n -> p (s n)"),
                                       ACT.Silu).then_inc(s_v, 1)
                    for t in range(NT):
                        act.wait_ge(s_um, t + 1)
                        act.activation(u[:, t, :], T.ps[:, 6 + t % 2, 0:DI], ACT.Copy).then_inc(s_u, 1)
                    act.wait_ge(s_u, NT)
                    act.wait_ge(s_g, NT)

                @block.sync
                def _(sp):
                    sp.wait_ge(s_par, 2)
                    sp.dma_start(params, par[:, :]).then_inc(s_pd, 16)
                    sp.wait_ge(s_pd, 16)

                @block.gpsimd
                def _(pool):
                    pool.wait_ge(s_n, 1)
                    pool.tensor_tensor(rnorm[:, :, :], norm[:, :, :], power[:, :, :], ALU.pow).then_inc(s_r, 1)

                @block.vector
                def _(dve):
                    chain = Chain(dve, s_c)
                    dve.memset(vpad[:, :, :, 0:3], 0.0).then_inc(s_zero, 1)
                    chain(dve.memset(power[:, :, :], -0.5))
                    chain(dve.memset(response[:, :, :, :], 0.0))
                    dve.wait_ge(T.loaded["a3_conv"], 16)
                    dve.wait_ge(s_zero, 1)
                    for j in range(3):
                        dve.wait_ge(s_vp, 2 * j + 2)
                        chain(dve.tensor_scalar(conv[:, j, :, :], vpad[:, j, :, 0:SEQ], T.w["a3_conv"][:, j, 0:1], None,
                                                ALU.mult))
                        for k in range(1, 4):
                            ins = dve.scalar_tensor_tensor(conv[:, j, :, :], vpad[:, j, :, k:k + SEQ],
                                                           T.w["a3_conv"][:, j, k:k + 1], conv[:, j, :, :],
                                                           ALU.mult, ALU.add)
                            if k < 3:
                                chain(ins)
                        ins.then_inc(s_cv, 1)
                    dve.wait_ge(s_bm, 1)
                    for i in range(2):
                        ins = dve.tensor_copy(bc[:, 4 * i:4 * i + 4, :],
                                              T.ps[:, i, 0:384].rearrange("p (t n) -> p t n", n=96))
                        chain(ins)
                    chain(dve.tensor_tensor(sq[:, :, :], bc[:, :, :], bc[:, :, :], ALU.mult))
                    chain(dve.tensor_reduce(norm[:, :, :], sq[:, :, :].rearrange("p t (g n) -> p t g n", n=NS),
                                            AX_X, ALU.add))
                    dve.tensor_scalar(norm[:, :, :], norm[:, :, :], 1e-12, None, ALU.add).then_inc(s_n, 1)
                    dve.wait_ge(s_r, 1)
                    grouped = bc[:, :, :].rearrange("p t (g n) -> p (t g) n", n=NS)
                    dve.tensor_tensor(grouped, grouped,
                                      rnorm[:, :, :].rearrange("p t g -> p (t g)").unsqueeze(2)
                                      .to_broadcast([P, NT * 12, NS]), ALU.mult).then_inc(s_bn, 1)
                    dve.wait_ge(s_tp, 1)
                    for i in range(2):
                        cols = slice(i * HALF, (i + 1) * HALF)
                        dve.tensor_copy(BT[:, cols], T.ps[0:48, 2 + i, :]).then_inc(s_ev, 1)
                        for h in range(H):
                            dve.tensor_scalar(C_head[:, h, cols], T.ps[0:48, 4 + i, :],
                                              T.consts[0:48, C_M8 + h:C_M8 + h + 1], None,
                                              ALU.mult).then_inc(s_ev, 1)
                    dve.wait_ge(s_ev, 2 * (H + 1))

        with ExitStack() as inner:
            sb2 = lambda n, s: inner.enter_context(nc.sbuf_tensor(f"a3r_{n}", s, F32))
            pa, pd = sb2("pa", [LANES, SEQ]), sb2("pd", [LANES, SEQ])
            A, d, s, nda = sb2("A", [LANES, SEQ]), sb2("d", [LANES, SEQ]), sb2("s", [LANES, SEQ]), \
                sb2("nda", [LANES, SEQ])
            t0, t1, e0, e1 = (sb2(n, [LANES, SEQ]) for n in ("t0", "t1", "e0", "e1"))
            rz = sb2("rz", [LANES, SEQ + 1, SEQ])
            G = sb2("G", [LANES, SEQ, SEQ])
            rx = sb2("rx", [LANES, SEQ])
            w = sb2("w", [LANES, SEQ])
            s_c, s_in, s_ab, s_e, s_l, s_g, s_gd, s_rd = sems(
                nc, inner, "a3r", "chain", "params", "abs", "exps", "log", "response", "response_out",
                "response_in")
            with nc.Block() as block:
                @block.sync
                def _(sp):
                    lanes = lambda k: params[k * H:(k + 1) * H, :].rearrange("h (b t) -> (h b) t", t=SEQ)
                    sp.dma_start(pa[:, :], lanes(0)).then_inc(s_in, 16)
                    sp.dma_start(pd[:, :], lanes(1)).then_inc(s_in, 16)
                    sp.wait_ge(s_g, 1)
                    sp.dma_start(g_dram, G[:, :, :]).then_inc(s_gd, 16)
                    sp.wait_ge(s_gd, 16)
                    blocks = g_dram.rearrange("(h i r) tau t -> h r tau i t", h=H, r=2)
                    for h in range(H):
                        for r in range(2):
                            half = slice(r * SEQ, (r + 1) * SEQ)
                            sp.dma_start(response[half, :, h, half], blocks[h, r]).then_inc(s_rd, 16)
                    sp.wait_ge(s_rd, 16 * 2 * H)

                @block.scalar
                def _(act):
                    act.wait_ge(s_in, 32)
                    act.activation(e1[:, :], pd[:, :], ACT.Exp, scale=-1.0).then_inc(s_e, 1)
                    act.activation(t0[:, :], pa[:, :], ACT.Abs).then_inc(s_ab, 1)
                    act.wait_ge(s_ab, 1)
                    act.activation(e0[:, :], t0[:, :], ACT.Exp, scale=-1.0).then_inc(s_e, 1)
                    act.wait_ge(s_e, 2)
                    act.activation(t1[:, :], e0[:, :], ACT.Ln, bias=1.0).then_inc(s_l, 1)

                @block.vector
                def _(dve):
                    chain = Chain(dve, s_c)
                    chain(dve.memset(rz[:, :, :], 0.0))
                    chain(dve.memset(rx[:, :], 1.0))
                    dve.wait_ge(s_in, 32)
                    dve.wait_ge(s_e, 1)
                    chain(dve.tensor_scalar(d[:, :], e1[:, :], 1.0, None, ALU.add))
                    chain(dve.reciprocal(d[:, :], d[:, :]))
                    dve.wait_ge(s_l, 1)
                    chain(dve.scalar_tensor_tensor(A[:, :], pa[:, :], 0.0, t1[:, :], ALU.max, ALU.add))
                    chain(dve.scalar_tensor_tensor(nda[:, :], A[:, :], -1.0, d[:, :], ALU.mult, ALU.mult))
                    chain(dve.scalar_tensor_tensor(s[:, :], nda[:, :], -1.0, d[:, :], ALU.mult, ALU.mult))
                    chain(dve.tensor_scalar(s[:, :], s[:, :], 1.0, None, ALU.add))
                    chain(dve.reciprocal(s[:, :], s[:, :]))
                    for tau in range(SEQ - 1, -1, -1):
                        col = lambda x: x[:, tau:tau + 1]
                        chain(dve.scalar_tensor_tensor(w[:, tau:], rx[:, tau:], col(d), rz[:, tau + 1, tau:],
                                                       ALU.mult, ALU.add))
                        chain(dve.tensor_scalar(rz[:, tau, tau:], w[:, tau:], col(s), None, ALU.mult))
                        chain(dve.scalar_tensor_tensor(rx[:, tau:], rz[:, tau, tau:], col(nda), rx[:, tau:],
                                                       ALU.mult, ALU.add))
                    dve.tensor_tensor(G[:, :, :], rz[:, 0:SEQ, :], d[:, :].unsqueeze(2)
                                      .to_broadcast([LANES, SEQ, SEQ]), ALU.mult).then_inc(s_g, 1)

        with ExitStack() as inner:
            sb2 = lambda n, s: inner.enter_context(nc.sbuf_tensor(f"a3y_{n}", s, F32))
            mixT = sb2("mixT", [P, 2, H * P])
            skip = sb2("skip", [P, NT, DI])
            gated = sb2("gated", [P, 2, DI])
            gatedT = sb2("gatedT", [P, 2, DI])
            s_c, s_b, s_m, s_y, s_sk, s_gt, s_t, s_gT, s_o, s_x = sems(
                nc, inner, "a3y", "chain", "bc_products", "mix", "y_products", "skip", "gated", "transposed",
                "gatedT", "products", "x")
            with nc.Block() as block:
                @block.tensor
                def _(pe):
                    def cb(t):
                        if t >= 1:
                            pe.wait_ge(s_m, 2 * t)
                        for q in range(2):
                            mm = pe.matmul(T.ps[:, q, 0:3 * P], BT[:, t * P:(t + 1) * P],
                                           C_head[:, 3 * q:3 * q + 3, t * P:(t + 1) * P], start=True, stop=True)
                        mm.then_inc(s_b, 1)

                    pe.wait_ge(T.loaded["a3_out"], 16)
                    cb(0)
                    for t in range(NT):
                        if t + 1 < NT:
                            cb(t + 1)
                        pe.wait_ge(s_m, 2 * (t + 1))
                        if t >= 2:
                            pe.wait_ge(s_gt, t - 1)
                        for h in range(H):
                            mm = pe.matmul(T.ps[:, 2 + t % 2, h * HD:(h + 1) * HD],
                                           mixT[:, t % 2, h * P:(h + 1) * P], u[:, t, h * HD:(h + 1) * HD],
                                           start=True, stop=True)
                        mm.then_inc(s_y, 1)
                        pe.wait_ge(s_gt, t + 1)
                        if t >= 2:
                            pe.wait_ge(s_gT, t - 1)
                        for j in range(3):
                            mm = pe.transpose(T.ps[:, 4 + t % 2, j * P:(j + 1) * P],
                                              gated[:, t % 2, j * P:(j + 1) * P], T.ident)
                        mm.then_inc(s_t, 1)
                        pe.wait_ge(s_gT, t + 1)
                        if t >= 2:
                            pe.wait_ge(s_x, t - 1)
                        for j in range(3):
                            mm = pe.matmul(T.ps[:, 6 + t % 2, 0:D], gatedT[:, t % 2, j * P:(j + 1) * P],
                                           T.w["a3_out"][:, j, :], start=(j == 0), stop=(j == 2))
                        mm.then_inc(s_o, 1)

                @block.gpsimd
                def _(pool):
                    pool.wait_ge(T.loaded["a3_skip"], 16)
                    for t in range(NT):
                        pool.tensor_tensor(skip[:, t, :], u[:, t, :], T.w["a3_skip"][:, :], ALU.mult).then_inc(s_sk, 1)

                @block.scalar
                def _(act):
                    for t in range(NT):
                        act.wait_ge(s_t, t + 1)
                        if t >= 2:
                            act.wait_ge(s_o, t - 1)
                        act.activation(gatedT[:, t % 2, :], T.ps[:, 4 + t % 2, 0:DI], ACT.Copy).then_inc(s_gT, 1)

                @block.vector
                def _(dve):
                    chain = Chain(dve, s_c)

                    def mix(t):
                        dve.wait_ge(s_b, t + 1)
                        if t >= 2:
                            dve.wait_ge(s_y, t - 1)
                        for q in range(2):
                            dve.tensor_tensor(mixT[:, t % 2, 3 * q * P:3 * (q + 1) * P], T.ps[:, q, 0:3 * P],
                                              response[:, t, 3 * q:3 * q + 3, :].rearrange("p h t -> p (h t)"),
                                              ALU.mult).then_inc(s_m, 1)

                    mix(0)
                    for t in range(NT):
                        if t + 1 < NT:
                            mix(t + 1)
                        dve.wait_ge(s_y, t + 1)
                        dve.wait_ge(s_sk, t + 1)
                        if t >= 2:
                            dve.wait_ge(s_t, t - 1)
                        chain(dve.tensor_tensor(gated[:, t % 2, :], T.ps[:, 2 + t % 2, 0:DI], skip[:, t, :], ALU.add))
                        dve.tensor_tensor(gated[:, t % 2, :], gated[:, t % 2, :], gate[:, t, :],
                                          ALU.mult).then_inc(s_gt, 1)
                        dve.wait_ge(s_o, t + 1)
                        dve.tensor_tensor(T.xn[:, t, :], T.ps[:, 6 + t % 2, 0:D], T.xn[:, t, :],
                                          ALU.add).then_inc(s_x, 1)
                    dve.wait_ge(s_x, NT)

    rms_stage(nc, T, "x2", T.w["a3_norm2"])
    with ExitStack() as ctx:
        f1 = ctx.enter_context(nc.sbuf_tensor("a3f_f1", [P, 6, N_TOK], F32))
        s_f, s_g, s_o, s_hx, s_h = sems(nc, ctx, "a3f", "ff1", "gelu", "ff2", "h_x", "h")
        with nc.Block() as block:
            @block.tensor
            def _(pe):
                pe.wait_ge(T.loaded["a3_ff1"], 16)
                pe.wait_ge(T.loaded["a3_ff2"], 16)
                for n in range(12):
                    j, half = n // 2, n % 2
                    cols = slice(half * HALF, (half + 1) * HALF)
                    if n >= 4:
                        pe.wait_ge(s_g, n - 3)
                    pe.matmul(T.ps[:, n % 4, :], T.w["a3_ff1"][:, 0, j * P:(j + 1) * P], T.xT[:, 0, cols],
                              start=True, stop=False)
                    pe.matmul(T.ps[:, n % 4, :], T.w["a3_ff1"][0:DC, 1, j * P:(j + 1) * P], T.xT[0:DC, 1, cols],
                              start=False, stop=True).then_inc(s_f, 1)
                pe.wait_ge(s_g, 12)
                for t in range(NT):
                    if t >= 4:
                        pe.wait_ge(s_h, t - 3)
                    for j in range(6):
                        mm = pe.matmul(T.ps[:, 4 + t % 4, 0:D], f1[:, j, t * P:(t + 1) * P], T.w["a3_ff2"][:, j, :],
                                       start=(j == 0), stop=(j == 5))
                    mm.then_inc(s_o, 1)

            @block.scalar
            def _(act):
                for n in range(12):
                    act.wait_ge(s_f, n + 1)
                    act.activation(f1[:, n // 2, (n % 2) * HALF:(n % 2 + 1) * HALF], T.ps[:, n % 4, :],
                                   ACT.Gelu_apprx_tanh).then_inc(s_g, 1)

            @block.vector
            def _(dve):
                dve.wait_ge(T.loaded["a3_b2"], 16)
                dve.tensor_tensor(T.h[:, :, :], T.h[:, :, :], T.xn[:, :, :], ALU.add).then_inc(s_hx, 1)
                dve.wait_ge(s_hx, 1)
                dve.tensor_tensor(T.h[:, :, :], T.h[:, :, :], T.w["a3_b2"][:, :].unsqueeze(1).to_broadcast([P, NT, D]),
                                  ALU.add).then_inc(s_hx, 1)
                dve.wait_ge(s_hx, 2)
                for t in range(NT):
                    dve.wait_ge(s_o, t + 1)
                    dve.tensor_tensor(T.h[:, t, :], T.ps[:, 4 + t % 4, 0:D], T.h[:, t, :], ALU.add).then_inc(s_h, 1)
                dve.wait_ge(s_h, NT)


KNOTS, GRID = 16, 13.0 / 8.0


def kan_layer(nc, T, name, x, rounds, centres, weights, columns, products, finish):
    U_ = x.shape[1]
    with ExitStack() as ctx:
        sb = lambda n, s: ctx.enter_context(nc.sbuf_tensor(f"{name}_{n}", s, F32))
        v, near, near3, far3, basis = (sb(n, [P, U_, N_TOK]) for n in ("v", "near", "near3", "far3", "basis"))
        w = sb("w", [P, U_, columns])
        s_w = sems(nc, ctx, name, *[f"w{u}" for u in range(U_)])
        s_v, s_cut, s_sq, s_cube, s_basis, s_used, s_waited = sems(
            nc, ctx, name, "v", "cut", "squares", "cubes", "basis", "used", "waited")

        def every_round(eng, body):
            body(0, True, False)
            with eng.Fori(1, rounds - 1) as i:
                body(i, False, False)
            body(rounds - 1, False, True)

        with nc.Block() as block:
            @block.sync
            def _(sp):
                def body(i, first, last):
                    for u in range(U_):
                        if not first:
                            sp.wait_ge(s_used, (i - 1) * U_ + u + 1)
                        sp.dma_start(w[:, u, :], weights[bass.ds(i * U_ + u, 1), :, :]
                                     .rearrange("a p n -> p (a n)")).then_inc(s_w[u], 16)
                every_round(sp, body)

            @block.scalar
            def _(act):
                def squares(n, u, first):
                    act.wait_ge(s_cut, n + 1)
                    if not first:
                        act.wait_ge(s_basis, n - U_ + 1)
                    act.activation(near3[:, u, :], near[:, u, :], ACT.Square, scale=6.0 ** -0.5)
                    act.activation(far3[:, u, :], v[:, u, :], ACT.Square, scale=(4.0 / 6.0) ** 0.5
                                   ).then_inc(s_sq, 1)

                def body(i, first, last):
                    for u in range(U_):
                        if not first:
                            wait_alone(act, s_cube, (i - 1) * U_ + u + 1, s_waited)
                        act.activation(v[:, u, :], x[:, u, :], ACT.Abs, scale=GRID,
                                       bias=centres[:, bass.ds(i, 1)]).then_inc(s_v, 1)
                        if u:
                            squares(i * U_ + u - 1, u - 1, first)
                    squares(i * U_ + U_ - 1, U_ - 1, first)
                every_round(act, body)

            @block.vector
            def _(dve):
                def body(i, first, last):
                    def cubes(u):
                        dve.wait_ge(s_sq, i * U_ + u + 1)
                        dve.tensor_tensor(near3[:, u, :], near3[:, u, :], near[:, u, :], ALU.mult)
                        dve.tensor_tensor(far3[:, u, :], far3[:, u, :], v[:, u, :], ALU.mult).then_inc(s_cube, 1)

                    for u in range(U_):
                        dve.wait_ge(s_v, i * U_ + u + 1)
                        dve.tensor_scalar(near[:, u, :], v[:, u, :], 2.0, -2.0, ALU.min, ALU.add)
                        dve.tensor_scalar(v[:, u, :], v[:, u, :], 1.0, -1.0, ALU.min, ALU.add).then_inc(s_cut, 1)
                        if u:
                            cubes(u - 1)
                    cubes(U_ - 1)
                every_round(dve, body)

            @block.gpsimd
            def _(pool):
                def body(i, first, last):
                    for u in range(U_):
                        pool.wait_ge(s_cube, i * U_ + u + 1)
                        if not first:
                            pool.wait_ge(s_used, (i - 1) * U_ + u + 1)
                        pool.tensor_tensor(basis[:, u, :], far3[:, u, :], near3[:, u, :],
                                           ALU.subtract).then_inc(s_basis, 1)
                every_round(pool, body)

            @block.tensor
            def _(pe):
                def body(i, first, last):
                    for u in range(U_):
                        pe.wait_ge(s_basis, i * U_ + u + 1)
                        pe.wait_ge(s_w[u], 16 * (i + 1))
                        products(pe, basis[:, u, :], w[:, u, :], first and u == 0, last and u == U_ - 1
                                 ).then_inc(s_used, 1)
                every_round(pe, body)

        finish()


def kan_stages(nc, T, a):
    HID, HC = 512, 4
    with ExitStack() as ctx:
        sb = lambda n, s: ctx.enter_context(nc.sbuf_tensor(f"kan_{n}", s, F32))
        hid = sb("hid", [P, HC, N_TOK])
        with ExitStack() as inner:
            x2 = inner.enter_context(nc.sbuf_tensor("kan_x2", [P, 3, N_TOK], F32))
            xd = inner.enter_context(nc.sbuf_tensor("kan_xd", [P, NT, 3, 2, 64], F32))
            s_d, s_tp, s_cp = sems(nc, inner, "kan0", "doubled", "transposed", "copied")
            with nc.Block() as block:
                @block.vector
                def _(dve):
                    for t in range(NT):
                        dve.tensor_copy(xd[:, t, :, :, :], T.xn[:, t, :].rearrange("p (c f) -> p c f", c=3)
                                        .unsqueeze(2).to_broadcast([P, 3, 2, 64])).then_inc(s_d, 1)

                @block.tensor
                def _(pe):
                    for t in range(NT):
                        pe.wait_ge(s_d, t + 1)
                        for c in range(3):
                            mm = pe.transpose(T.ps[:, t, c * P:(c + 1) * P],
                                              xd[:, t, c, :, :].rearrange("p a b -> p (a b)"), T.ident)
                        mm.then_inc(s_tp, 1)

                @block.scalar
                def _(act):
                    for t in range(NT):
                        act.wait_ge(s_tp, t + 1)
                        act.activation(x2[:, :, t * P:(t + 1) * P],
                                       T.ps[:, t, 0:3 * P].rearrange("p (c n) -> p c n", c=3),
                                       ACT.Copy).then_inc(s_cp, 1)
                    act.wait_ge(s_cp, NT)

            def products1(pe, basis, w, start, stop):
                for j in range(HC):
                    for half in range(2):
                        mm = pe.matmul(T.ps[:, 2 * j + half, :], w[:, j * P:(j + 1) * P],
                                       basis[:, half * HALF:(half + 1) * HALF], start=start, stop=stop)
                return mm

            def finish1():
                s_h, = sems(nc, inner, "kan1f", "hidden")
                with nc.Block() as block:
                    @block.scalar
                    def _(act):
                        for b in range(0, 8, 2):
                            act.activation(hid[:, b // 2, 0:HALF], T.ps[:, b, :], ACT.Copy).then_inc(s_h, 1)
                        act.wait_ge(s_h, 8)

                    @block.vector
                    def _(dve):
                        for b in range(1, 8, 2):
                            dve.tensor_copy(hid[:, b // 2, HALF:N_TOK], T.ps[:, b, :]).then_inc(s_h, 1)
                        dve.wait_ge(s_h, 8)

            kan_layer(nc, T, "kan1", x2, KNOTS // 2, T.consts[:, C_K1:C_K1 + KNOTS // 2], a["kan_w1"], HID,
                      products1, finish1)

        def products2(pe, basis, w, start, stop):
            for t in range(NT):
                mm = pe.matmul(T.ps[:, t, 0:D], basis[:, t * P:(t + 1) * P], w, start=start, stop=stop)
            return mm

        def finish2():
            s_h, = sems(nc, ctx, "kan2f", "h")
            with nc.Block() as block:
                @block.vector
                def _(dve):
                    for t in range(NT):
                        dve.tensor_tensor(T.h[:, t, :], T.ps[:, t, 0:D], T.h[:, t, :], ALU.add).then_inc(s_h, 1)
                    dve.wait_ge(s_h, NT)

        kan_layer(nc, T, "kan2", hid, KNOTS, T.consts[:, C_K2:C_K2 + KNOTS], a["kan_w2"], D, products2, finish2)


def tower(nc, a, out):
    with ExitStack() as ctx:
        T = Tower()
        T.w = {}
        sb = lambda n, s, dt=F32: ctx.enter_context(nc.sbuf_tensor(n, s, dt))
        consts = sb("consts", [P, C_N])
        T.consts = consts
        T.ident = consts[:, C_ID:C_ID + P]
        T.block_mask = consts[:, C_BLK:C_BLK + P]
        T.causal3 = consts[:, C_CAU:C_CAU + 3 * P]
        T.h = sb("h", [P, NT, D])
        T.xn = sb("xn", [P, NT, D])
        T.xT = sb("xT", [DC + 1, 2, N_TOK])
        T.aT = sb("aT", [DC + 1, 2, N_TOK])
        T.ones = sb("ones", [P, P])
        T.zeros = sb("zeros", [P, D])
        T.power = sb("power", [P, NT])
        T.ps = ctx.enter_context(nc.psum_tensor("ps", [P, 8, HALF], F32))
        loads = {"consts": (consts[:, :], a["consts"])}
        for name in WEIGHTS:
            src = a[name]
            t = sb(name, list(src.shape))
            T.w[name] = t
            full = t[:, :] if len(src.shape) == 2 else t[:, :, :] if len(src.shape) == 3 else t[:, :, :, :]
            loads[name] = (full, src)
        T.loaded = {n: ctx.enter_context(nc.semaphore(f"in_{n}")) for n in loads}
        T.s_cleared = ctx.enter_context(nc.semaphore("cleared"))
        T.m0, T.m1, T.m2 = Moe("m0", 16, 3, shared=True), Moe("m1", 16, 2), Moe("m2", 32, 2, renormalise=True)
        for m in (T.m0, T.m1, T.m2):
            m.s_scattered, = sems(nc, ctx, m.name, "scattered")
            m.s_gathered = sems(nc, ctx, m.name, *[f"gathered{t}" for t in range(NT)])
            m.s_stored = sems(nc, ctx, m.name, *[f"stored{u}" for u in range(U)])
            m.gate = sb(f"{m.name}_gate", [P, m.C, NT])
            m.slots = sb(f"{m.name}_slots", [P, m.C, NT], U32)
            m.expert_of = sb(f"{m.name}_expert_of", [1, m.tiles + 1], I32)
            m.slots_x = nc.dram_tensor(f"{m.name}_slots_x", (m.tiles * P, D), F32, kind="Internal").ap()
            m.slots_y = nc.dram_tensor(f"{m.name}_slots_y", (m.tiles * P, D), F32, kind="Internal").ap()
        stages = [
            lambda: tokens_stage(nc, T, a["patches"], loads, (T.m0, T.m1, T.m2)),
            lambda: (norm_stage(nc, T, "n0"), attention0_stage(nc, T)),
            lambda: (norm_stage(nc, T, "n1"), moe0(nc, T, a)),
            lambda: (norm_stage(nc, T, "n2"), attention1_stage(nc, T)),
            lambda: (norm_stage(nc, T, "n3"), moe1(nc, T, a)),
            lambda: (norm_stage(nc, T, "n4"), attention2_stage(nc, T, a)),
            lambda: (norm_stage(nc, T, "n5"), moe2(nc, T, a)),
            lambda: (norm_stage(nc, T, "n6"), mixer_stage(nc, T, a)),
            lambda: (norm_stage(nc, T, "n7"), kan_stages(nc, T, a)),
        ]
        for stage in stages:
            stage()
        s_out, = sems(nc, ctx, "end", "stored")
        with nc.Block() as block:
            @block.sync
            def _(sp):
                sp.dma_start(out.rearrange("(t p) d -> p t d", p=P), T.h[:, :, :]).then_inc(s_out, 16)
                sp.wait_ge(s_out, 16)
                sp.wait_ge(T.s_cleared, 96)
                for loaded in T.loaded.values():
                    sp.wait_ge(loaded, 16)


WEIGHTS = ["tok_w", "tok_b", "a0_w", "e0_gate", "e1_gate", "e2_gate", "a1_w", "a1_proj",
           "a2_fc1", "a2_convA", "a2_convB", "a2_qkv", "a2_proj", "a2_fc2", "a2_cols",
           "a3_in", "a3_conv", "a3_bc", "a3_skip", "a3_out", "a3_norm1", "a3_norm2", "a3_ff1", "a3_ff2", "a3_b2"]


def constants():
    import numpy as np
    c = np.zeros((P, C_N), np.float32)
    row = np.arange(P)
    c[:, C_ID:C_ID + P] = np.eye(P)
    for base, width, n in ((C_M16, 16, 6), (C_M24, 24, 4), (C_M8, 8, 6)):
        for j in range(n):
            c[:, base + j] = row // width == j
    same = row[:, None] // SEQ == row[None, :] // SEQ
    c[:, C_BLK:C_BLK + P] = np.where(same, 0.0, NEG)
    causal = np.where(same & (row[None, :] <= row[:, None]), 0.0, np.where(same, -1.0e10, NEG))
    c[:, C_CAU:C_CAU + 3 * P] = np.tile(causal, 3)
    c[:, C_LT:C_LT + P] = row[None, :] > row[:, None]
    c[:, C_IOTA:C_IOTA + P] = row[None, :]
    c[:, C_K1:C_K1 + 8] = 7.5 - (2 * np.arange(8)[None, :] + row[:, None] // 64)
    c[:, C_K2:C_K2 + 16] = 7.5 - np.arange(16)[None, :]
    return c


def neighbour_bias(rpb):
    import numpy as np
    rows, k = 16, 5
    start = lambda i, n: np.clip(i - k // 2, 0, n - k)
    out = np.full((P, 3, 4, 6, SEQ), NEG, np.float32)
    w = np.arange(SEQ)
    for kind, tile in enumerate((0, 1, NT - 1)):
        key_row0 = 2 * min(max(tile - 1, 0), NT - 3)
        for r in range(2):
            row = 2 * tile + r
            for key_row in range(start(row, rows), start(row, rows) + k):
                for b in range(k):
                    key = start(w, SEQ) + b
                    out[r * SEQ + w, kind, :, key_row - key_row0, key] = rpb[:, key_row - row + k - 1, key - w + k - 1].T
    return out.reshape(P, -1)


def lay_out(x):
    import numpy as np
    f = lambda n: np.asarray(x[n])

    def chunks(w, n):
        return np.ascontiguousarray(w.reshape(n, w.shape[0] // n, -1).transpose(1, 0, 2))

    def with_bias(w, b):
        out = np.zeros((DC + 1, 2, w.shape[1]), np.float32)
        out[0:DC] = chunks(w, 2)
        out[DC, 0] = b
        return out

    def rows(b):
        return np.ascontiguousarray(np.broadcast_to(b, (P, b.shape[0])))

    a = {"consts": constants()}
    p = f("x").reshape(16, 3, 8, 16, 8, 16).transpose(0, 1, 2, 4, 3, 5).reshape(N_TOK, 768)
    a["patches"] = chunks(p.T, 6)
    a["tok_w"] = chunks(f("L0_tok_weight").T, 6)
    a["tok_b"] = rows(f("L0_tok_bias"))
    a["a0_w"] = with_bias(f("L0_attn_W_qkv"), f("L0_attn_b_qkv"))
    a["a1_w"] = with_bias(f("L1_attn_Wqkv_w")[:D].T, f("L1_attn_Wqkv_b")[:D])
    a["a1_proj"] = with_bias(f("L1_attn_Wproj_w").T, f("L1_attn_Wproj_b"))
    a["a2_fc1"] = with_bias(f("L2_attn_fc1_w").T, f("L2_attn_fc1_b"))
    a["a2_convA"] = np.ascontiguousarray(f("L2_attn_convA_w").T)
    a["a2_convB"] = np.ascontiguousarray(f("L2_attn_convB_w").T)
    a["a2_qkv"] = np.concatenate([f("L2_attn_qkv_w").T, f("L2_attn_qkv_b")[None]])
    a["a2_proj"] = np.ascontiguousarray(f("L2_attn_proj_w").T)
    a["a2_fc2"] = np.concatenate([f("L2_attn_fc2_w").T, f("L2_attn_fc2_b")[None]])
    a["a2_cols"] = np.zeros((DC, 3), np.float32)
    a["a2_cols"][0:64, 0] = f("L2_attn_convA_b")
    a["a2_cols"][:, 1] = f("L2_attn_convB_b")
    a["a2_cols"][:, 2] = f("L2_attn_proj_b")
    a["a2_bias"] = neighbour_bias(f("L2_attn_rpb"))

    def experts_with_bias(w, b, b2=None):
        e, _, n = w.shape
        out = np.zeros((e, DC + 1, 2, n), np.float32)
        out[:, 0:DC] = w.reshape(e, 2, DC, n).transpose(0, 2, 1, 3)
        out[:, DC, 0] = b
        if b2 is not None:
            out[:, DC, 1, 0:D] = b2
        return out.reshape(e, DC + 1, 2 * n)

    def expert_chunks(w):
        e, k, n = w.shape
        return np.ascontiguousarray(w.reshape(e, k // P, P, n).transpose(0, 2, 1, 3).reshape(e, P, -1))

    a["e0_gate"] = with_bias(f("L0_ffn_gate_w"), f("L0_ffn_gate_b"))
    a["e1_gate"] = with_bias(f("L1_ffn_Wr").T, np.zeros(16, np.float32))
    a["e2_gate"] = with_bias(f("L2_ffn_gate_w").T, np.zeros(32, np.float32))
    a["e0_w1"] = experts_with_bias(f("L0_ffn_fc1_w"), f("L0_ffn_fc1_b"), f("L0_ffn_fc2_b"))
    a["e0_w2"] = np.concatenate([expert_chunks(f("L0_ffn_fc2_w")), expert_chunks(f("L0_ffn_ln_w")[:, :, None]),
                                 expert_chunks(f("L0_ffn_ln_b")[:, :, None])], axis=2)
    a["e1_w1"] = experts_with_bias(f("L1_ffn_W1"), f("L1_ffn_b1"), f("L1_ffn_b2"))
    a["e1_w2"] = expert_chunks(f("L1_ffn_W2"))
    a["e2_w1"] = experts_with_bias(f("L2_ffn_W1"), f("L2_ffn_b1"))
    a["e2_w23"] = np.concatenate([expert_chunks(f("L2_ffn_W2")), expert_chunks(f("L2_ffn_W3")),
                                  expert_chunks(f("L2_ffn_b2")[:, :, None])], axis=2)
    a["e2_wl"] = np.zeros((32, 65, D + 1), np.float32)
    a["e2_wl"][:, 0:64, 0:D] = f("L2_ffn_Wl")
    a["e2_wl"][:, 64, 0:D] = f("L2_ffn_bl")
    a["e2_wl"][:, 0:64, D] = f("L2_ffn_b3")
    w_in = f("L3_attn_w_in")
    w_in = np.concatenate([w_in[:, :768], w_in[:, 768::2], w_in[:, 769::2]], axis=1)
    a["a3_in"] = chunks(w_in, 2)
    a["a3_conv"] = chunks(f("L3_attn_conv_w"), 3)
    w_bc = f("L3_attn_w_bc").reshape(384, 6, 2, 8).transpose(0, 2, 1, 3).reshape(384, 96)
    a["a3_bc"] = chunks(w_bc, 3)
    a["a3_skip"] = rows(np.repeat(f("L3_attn_D_skip"), 64))
    a["a3_out"] = chunks(f("L3_attn_w_out"), 3)
    a["a3_norm1"] = np.ascontiguousarray(f("L3_attn_norm1_w").reshape(2, DC).T)
    a["a3_norm2"] = np.ascontiguousarray(f("L3_attn_norm2_w").reshape(2, DC).T)
    a["a3_ff1"] = with_bias(f("L3_attn_ff_w1"), f("L3_attn_ff_b1"))
    a["a3_ff2"] = chunks(f("L3_attn_ff_w2"), 6)
    a["a3_b2"] = rows(f("L3_attn_ff_b2"))
    a["kan_w1"] = np.ascontiguousarray(f("L3_ffn_w1").reshape(512, 3, 64, 8, 2).transpose(3, 1, 4, 2, 0)
                                       .reshape(24, P, 512))
    a["kan_w2"] = np.ascontiguousarray(f("L3_ffn_w2").reshape(D, 4, P, 16).transpose(3, 1, 2, 0).reshape(64, P, D))
    return a


def kernel(**inputs):
    import numpy as np
    import concourse.bacc as bacc
    from concourse.bass_utils import run_bass_kernel_spmd

    nc = bacc.Bacc("TRN2", target_bir_lowering=False, num_devices=1)
    arrays = {f"in_{name}": np.ascontiguousarray(x) for name, x in lay_out(inputs).items()}
    args = {name[3:]: nc.dram_tensor(name, x.shape, mybir.dt.from_np(x.dtype), kind="ExternalInput").ap()
            for name, x in arrays.items()}
    out = nc.dram_tensor("out", (N_TOK, D), F32, kind="ExternalOutput").ap()
    tower(nc, args, out)
    result = run_bass_kernel_spmd(nc, [arrays], core_ids=[0]).results[0]["out"]
    return result.reshape(16, SEQ, D)
```

```python
from contextlib import ExitStack

import concourse.bass as bass
from concourse import mybir

F32 = mybir.dt.float32
I32 = mybir.dt.int32
U32 = mybir.dt.uint32
ALU = mybir.AluOpType
ACT = mybir.ActivationFunctionType
AX_X = mybir.AxisListType.X

P = 128
D = 192
DC = 96
N_TOK = 1024
NT = N_TOK // P
HALF = 512
SEQ = 64
NEG = -1.0e30

C_ID = 0
C_M16 = C_ID + P
C_M24 = C_M16 + 6
C_M8 = C_M24 + 4
C_BLK = C_M8 + 6
C_CAU = C_BLK + P
C_LT = C_CAU + 3 * P
C_IOTA = C_LT + P
C_K1 = C_IOTA + P
C_K2 = C_K1 + 8
C_N = C_K2 + 16


class Chain:

    def __init__(self, eng, sem):
        self.eng, self.sem, self.n, self.base = eng, sem, 0, 0

    def __call__(self, ins):
        ins.then_inc(self.sem, 1)
        self.n += 1
        self.eng.wait_ge(self.sem, self.base + self.n)


class Tower:
    pass


def sems(nc, ctx, prefix, *names):
    handles = [ctx.enter_context(nc.semaphore(f"{prefix}_{n}")) for n in names]

    def clear():
        for handle in handles:
            nc.gpsimd.sem_clear(handle)

    if prefix not in ("m0", "m1", "m2"):
        ctx.callback(clear)
    return handles


def wait_alone(eng, sem, value, waited):
    eng.wait_ge(sem, value)
    eng.sem_inc(waited, 1)


def tokens_stage(nc, T, patches, loads, mixtures):
    with ExitStack() as ctx:
        xs = ctx.enter_context(nc.sbuf_tensor("tok_x", [P, 6, N_TOK], F32))
        s_x = sems(nc, ctx, "tok", *[f"patches{k}" for k in range(6)])
        s_mm, s_h, s_z = sems(nc, ctx, "tok", "products", "h", "zeros")
        with nc.Block() as block:
            @block.sync
            def _(sp):
                sp.dma_start(T.w["tok_w"][:, :, :], loads["tok_w"][1]).then_inc(T.loaded["tok_w"], 16)
                for k in range(1, 6, 2):
                    sp.dma_start(xs[:, k, :], patches[:, k, :]).then_inc(s_x[k], 16)
                for name, (dst, src) in loads.items():
                    if name != "tok_w":
                        sp.dma_start(dst, src).then_inc(T.loaded[name], 16)

            @block.scalar
            def _(act):
                for k in range(0, 6, 2):
                    act.dma_start(xs[:, k, :], patches[:, k, :]).then_inc(s_x[k], 16)
                act.wait_ge(s_z, 1)
                for m in mixtures:
                    for slots in (m.slots_x, m.slots_y):
                        act.dma_start(slots.rearrange("(n p) d -> p n d", p=P),
                                      T.zeros[:, :].unsqueeze(1).to_broadcast([P, m.tiles, D])
                                      ).then_inc(T.s_cleared, 16)

            @block.tensor
            def _(pe):
                pe.wait_ge(T.loaded["tok_w"], 16)
                for k in range(6):
                    pe.wait_ge(s_x[k], 16)
                    for t in range(NT):
                        mm = pe.matmul(T.ps[:, t, 0:D], xs[:, k, t * P:(t + 1) * P], T.w["tok_w"][:, k, :],
                                       start=(k == 0), stop=(k == 5))
                        if k == 5:
                            mm.then_inc(s_mm, 1)

            @block.vector
            def _(dve):
                dve.memset(T.zeros[:, :], 0.0).then_inc(s_z, 1)
                dve.memset(T.ones[:, :], 1.0)
                dve.memset(T.power[:, :], -0.5)
                dve.memset(T.xT[DC:DC + 1, 0, :], 1.0)
                dve.memset(T.aT[DC:DC + 1, 0, :], 1.0)
                dve.wait_ge(T.loaded["tok_b"], 16)
                for t in range(NT):
                    dve.wait_ge(s_mm, t + 1)
                    dve.tensor_tensor(T.h[:, t, :], T.ps[:, t, 0:D], T.w["tok_b"][:, :], ALU.add).then_inc(s_h, 1)
                dve.wait_ge(s_h, NT)


def norm_stage(nc, T, name, rms_weight=None):
    with ExitStack() as ctx:
        stats = ctx.enter_context(nc.sbuf_tensor(f"{name}_stats", [P, NT, 6], F32))
        mv = ctx.enter_context(nc.sbuf_tensor(f"{name}_mv", [P, NT, 2], F32))
        var = ctx.enter_context(nc.sbuf_tensor(f"{name}_var", [P, NT], F32))
        rstd = ctx.enter_context(nc.sbuf_tensor(f"{name}_rstd", [P, NT], F32))
        ms = ctx.enter_context(nc.sbuf_tensor(f"{name}_ms", [P, NT], F32))
        rrms = ctx.enter_context(nc.sbuf_tensor(f"{name}_rrms", [P, NT], F32))
        xr = ctx.enter_context(nc.sbuf_tensor(f"{name}_xr", [P, NT, D], F32)) if rms_weight is not None else T.xn
        s_c, s_var, s_rstd, s_xn, s_tp, s_cp, s_x, s_ms, s_rrms = sems(
            nc, ctx, name, "chain", "variance", "rstd", "xn", "transposed", "copied", "xn_only", "mean_square",
            "rrms")
        with nc.Block() as block:
            @block.vector
            def _(dve):
                chain = Chain(dve, s_c)
                for t in range(NT):
                    ins = dve.bn_stats(stats[:, t, :], T.h[:, t, :])
                chain(ins)
                for t in range(NT):
                    ins = dve.bn_aggr(mv[:, t, :], stats[:, t, :])
                chain(ins)
                dve.tensor_scalar(var[:, :], mv[:, :, 1], 1e-5, None, ALU.add).then_inc(s_var, 1)
                dve.wait_ge(s_rstd, 1)
                if rms_weight is not None:
                    chain(dve.tensor_tensor(ms[:, :], rstd[:, :], rstd[:, :], ALU.mult))
                    chain(dve.tensor_tensor(ms[:, :], ms[:, :], mv[:, :, 1], ALU.mult))
                    dve.tensor_scalar(ms[:, :], ms[:, :], 1e-6, None, ALU.add).then_inc(s_ms, 1)
                for t in range(NT):
                    dve.tensor_scalar(T.xn[:, t, :], T.h[:, t, :], mv[:, t, 0:1], rstd[:, t:t + 1],
                                      ALU.subtract, ALU.mult).then_inc(s_xn if rms_weight is None else s_x, 1)
                if rms_weight is not None:
                    dve.wait_ge(s_rrms, 1)
                    for t in range(NT):
                        dve.wait_ge(s_x, t + 1)
                        dve.tensor_scalar(xr[:, t, :], T.xn[:, t, :], rrms[:, t:t + 1], None,
                                          ALU.mult).then_inc(s_xn, 1)
                    dve.wait_ge(T.loaded["a3_norm1"], 16)
                    dve.wait_ge(T.loaded["a3_norm2"], 16)
                    for t in range(NT):
                        dve.wait_ge(s_tp, t + 1)
                        for c in range(2):
                            dve.tensor_scalar(T.xT[0:DC, c, t * P:(t + 1) * P], T.ps[0:DC, t, c * P:(c + 1) * P],
                                              rms_weight[:, c:c + 1], None, ALU.mult).then_inc(s_cp, 1)
                    dve.wait_ge(s_cp, 2 * NT)
                    return
                for t in range(0, NT, 2):
                    dve.wait_ge(s_tp, t + 1)
                    dve.tensor_copy(T.xT[0:DC, :, t * P:(t + 1) * P],
                                    T.ps[0:DC, t, 0:2 * P].rearrange("p (c n) -> p c n", c=2)).then_inc(s_cp, 1)
                dve.wait_ge(s_cp, NT)

            @block.gpsimd
            def _(pool):
                pool.wait_ge(s_var, 1)
                pool.tensor_tensor(rstd[:, :], var[:, :], T.power[:, :], ALU.pow).then_inc(s_rstd, 1)
                if rms_weight is not None:
                    pool.wait_ge(s_ms, 1)
                    pool.tensor_tensor(rrms[:, :], ms[:, :], T.power[:, :], ALU.pow).then_inc(s_rrms, 1)

            @block.scalar
            def _(act):
                for t in range(1, NT if rms_weight is None else 1, 2):
                    act.wait_ge(s_tp, t + 1)
                    act.activation(T.xT[0:DC, :, t * P:(t + 1) * P],
                                   T.ps[0:DC, t, 0:2 * P].rearrange("p (c n) -> p c n", c=2),
                                   ACT.Copy).then_inc(s_cp, 1)

            @block.tensor
            def _(pe):
                if name == "n0":
                    pe.wait_ge(T.loaded["consts"], 16)
                for t in range(NT):
                    pe.wait_ge(s_xn, t + 1)
                    for c in range(2):
                        mm = pe.transpose(T.ps[0:DC, t, c * P:(c + 1) * P],
                                          xr[:, t, c * DC:(c + 1) * DC], T.ident)
                    mm.then_inc(s_tp, 1)


def attention0_stage(nc, T):
    scale = float(D) ** -0.5
    with ExitStack() as ctx:
        sb = lambda n, s: ctx.enter_context(nc.sbuf_tensor(f"a0_{n}", s, F32))
        qk = sb("qk", [DC, 4, N_TOK])
        v = sb("v", [P, NT, D])
        logit = sb("logit", [P, NT, P])
        prob = sb("prob", [P, NT, P])
        probT = sb("probT", [P, NT, P])
        top = sb("top", [P, NT])
        total = sb("total", [P, NT])
        inv = sb("inv", [P, NT])
        s_c, s_qkmm, s_qk, s_vmm, s_v, s_smm, s_l, s_e, s_t, s_pT, s_o, s_h = sems(
            nc, ctx, "a0", "chain", "qk_products", "qk", "v_products", "v", "scores", "logits", "exps",
            "transposed", "probT", "contexts", "h")
        with nc.Block() as block:
            @block.tensor
            def _(pe):
                pe.wait_ge(T.loaded["a0_w"], 16)
                for o in range(4):
                    for half in range(2):
                        cols = slice(half * HALF, (half + 1) * HALF)
                        pe.matmul(T.ps[0:DC, 2 * o + half, :], T.w["a0_w"][:, 0, o * DC:(o + 1) * DC],
                                  T.xT[:, 0, cols], start=True, stop=False)
                        pe.matmul(T.ps[0:DC, 2 * o + half, :], T.w["a0_w"][0:DC, 1, o * DC:(o + 1) * DC],
                                  T.xT[0:DC, 1, cols], start=False, stop=True).then_inc(s_qkmm, 1)
                for t in range(NT):
                    pe.wait_ge(s_qk, t + 1)
                    pe.matmul(T.ps[:, t, 0:D], T.xT[:, 0, t * P:(t + 1) * P], T.w["a0_w"][:, 0, 2 * D:3 * D],
                              start=True, stop=False)
                    pe.matmul(T.ps[:, t, 0:D], T.xT[0:DC, 1, t * P:(t + 1) * P], T.w["a0_w"][0:DC, 1, 2 * D:3 * D],
                              start=False, stop=True).then_inc(s_vmm, 1)
                for t in range(NT):
                    pe.wait_ge(s_v, t + 1)
                    for c in range(2):
                        mm = pe.matmul(T.ps[:, t, 0:P], qk[:, c, t * P:(t + 1) * P],
                                       qk[:, 2 + c, t * P:(t + 1) * P], start=(c == 0), stop=(c == 1))
                    mm.then_inc(s_smm, 1)
                for t in range(NT):
                    pe.wait_ge(s_e, t + 1)
                    pe.transpose(T.ps[:, t, P:2 * P], prob[:, t, :], T.ident).then_inc(s_t, 1)
                for t in range(NT):
                    pe.wait_ge(s_pT, t + 1)
                    pe.matmul(T.ps[:, t, 2 * P:2 * P + D], probT[:, t, :], v[:, t, :],
                              start=True, stop=True).then_inc(s_o, 1)

            @block.scalar
            def _(act):
                for b in range(8):
                    act.wait_ge(s_qkmm, b + 1)
                    act.activation(qk[:, b // 2, (b % 2) * HALF:(b % 2 + 1) * HALF], T.ps[0:DC, b, :],
                                   ACT.Copy).then_inc(s_qk, 1)
                for t in range(NT):
                    act.wait_ge(s_l, t + 1)
                    act.activation(prob[:, t, :], logit[:, t, :], ACT.Exp, bias=top[:, t:t + 1],
                                   accum_out=total[:, t:t + 1]).then_inc(s_e, 1)
                for t in range(NT):
                    act.wait_ge(s_t, t + 1)
                    act.activation(probT[:, t, :], T.ps[:, t, P:2 * P], ACT.Copy).then_inc(s_pT, 1)

            @block.vector
            def _(dve):
                chain = Chain(dve, s_c)
                for t in range(NT):
                    dve.wait_ge(s_vmm, t + 1)
                    dve.tensor_copy(v[:, t, :], T.ps[:, t, 0:D]).then_inc(s_v, 1)
                for t in range(NT):
                    dve.wait_ge(s_smm, t + 1)
                    chain(dve.scalar_tensor_tensor(logit[:, t, :], T.ps[:, t, 0:P], scale, T.block_mask,
                                                   ALU.mult, ALU.add))
                    dve.tensor_reduce(top[:, t:t + 1], logit[:, t, :], AX_X, ALU.max,
                                      negate=True).then_inc(s_l, 1)
                dve.wait_ge(s_e, NT)
                chain(dve.reciprocal(inv[:, :], total[:, :]))
                for t in range(NT):
                    dve.wait_ge(s_o, t + 1)
                    dve.scalar_tensor_tensor(T.h[:, t, :], T.ps[:, t, 2 * P:2 * P + D], inv[:, t:t + 1],
                                             T.h[:, t, :], ALU.mult, ALU.add).then_inc(s_h, 1)
                dve.wait_ge(s_h, NT)
def windowed_attention(nc, T, name, scores, scale, bias, heads, width, v, first_key_tile, ctxs):
    blocks = 12 // heads
    W = 384
    with ExitStack() as ctx:
        sb = lambda n, s: ctx.enter_context(nc.sbuf_tensor(f"{name}_{n}", s, F32))
        logit = sb("logit", [P, 2, 4, W])
        shifted = sb("shifted", [P, 2, 4 * W])
        prob = sb("prob", [P, 2, 12, P])
        probT = sb("probT", [P, 2, 12 * P])
        top = sb("top", [P, NT, heads])
        inv = sb("inv", [P, NT, heads])
        s_c, s_s, s_l, s_m, s_sh, s_e, s_t, s_pT, s_o, s_a = sems(
            nc, ctx, name, "chain", "scores", "logits", "maxima", "shifted", "exps", "transposed", "probT",
            "products", "contexts")
        with nc.Block() as block:
            @block.tensor
            def _(pe):
                def score(t):
                    if t:
                        pe.wait_ge(s_l, t)
                    for g in range(4):
                        lhsT, rhs = scores(t, g)
                        mm = pe.matmul(T.ps[:, g, 0:W], lhsT, rhs, start=True, stop=True)
                    mm.then_inc(s_s, 1)

                def turn(t):
                    pe.wait_ge(s_e, t + 1)
                    if t:
                        pe.wait_ge(s_pT, 3 * t)
                    for b in range(12):
                        mm = pe.transpose(T.ps[:, 4 + b // 4, (b % 4) * P:(b % 4 + 1) * P],
                                          prob[:, t % 2, b, :], T.ident)
                        if b % 4 == 3:
                            mm.then_inc(s_t, 1)

                def product(t):
                    if t:
                        pe.wait_ge(s_a, t)
                    pe.wait_ge(s_pT, 3 * (t + 1))
                    for n in range(heads):
                        for i in range(blocks):
                            b = n * blocks + i
                            mm = pe.matmul(T.ps[:, 7, n * (width + 1):(n + 1) * (width + 1)],
                                           probT[:, t % 2, b * P:(b + 1) * P],
                                           v[:, first_key_tile(t) + i, n, :],
                                           start=(i == 0), stop=(i == blocks - 1))
                    mm.then_inc(s_o, 1)

                score(0)
                score(1)
                for t in range(NT + 1):
                    if t + 2 < NT:
                        score(t + 2)
                    if t < NT:
                        turn(t)
                    if t:
                        product(t - 1)

            @block.vector
            def _(dve):
                chain = Chain(dve, s_c)

                def context(t):
                    dve.wait_ge(s_o, t + 1)
                    o = T.ps[:, 7, 0:heads * (width + 1)].rearrange("p (h d) -> p h d", h=heads)
                    chain(dve.reciprocal(inv[:, t, :], o[:, :, width]))
                    dve.tensor_tensor(ctxs[:, t, :].rearrange("p (h d) -> p h d", h=heads), o[:, :, 0:width],
                                      inv[:, t, :].unsqueeze(2).to_broadcast([P, heads, width]),
                                      ALU.mult).then_inc(s_a, 1)

                for t in range(NT):
                    dve.wait_ge(s_s, t + 1)
                    if t >= 2:
                        dve.wait_ge(s_sh, t - 1)
                    dve.scalar_tensor_tensor(logit[:, t % 2, :, :], T.ps[:, 0:4, 0:W], scale, bias(t),
                                             ALU.mult, ALU.add).then_inc(s_l, 1)
                    dve.wait_ge(s_l, t + 1)
                    dve.tensor_reduce(top[:, t, :],
                                      logit[:, t % 2, :, :].rearrange("p g k -> p (g k)")
                                      .rearrange("p (h k) -> p h k", h=heads), AX_X, ALU.max).then_inc(s_m, 1)
                    if t >= 3:
                        context(t - 3)
                for t in range(NT - 3, NT):
                    context(t)
                dve.wait_ge(s_a, NT)

            @block.gpsimd
            def _(pool):
                for t in range(NT):
                    pool.wait_ge(s_m, t + 1)
                    if t >= 2:
                        pool.wait_ge(s_e, t - 1)
                    pool.tensor_tensor(shifted[:, t % 2, :].rearrange("p (h k) -> p h k", h=heads),
                                       logit[:, t % 2, :, :].rearrange("p g k -> p (g k)")
                                       .rearrange("p (h k) -> p h k", h=heads),
                                       top[:, t, :].unsqueeze(2).to_broadcast([P, heads, 4 * W // heads]),
                                       ALU.subtract).then_inc(s_sh, 1)

            @block.scalar
            def _(act):
                def exps(t):
                    act.wait_ge(s_sh, t + 1)
                    if t >= 2:
                        act.wait_ge(s_t, 3 * (t - 1))
                    act.activation(prob[:, t % 2, :, :].rearrange("p b k -> p (b k)"), shifted[:, t % 2, :],
                                   ACT.Exp).then_inc(s_e, 1)

                exps(0)
                for t in range(NT):
                    if t + 1 < NT:
                        exps(t + 1)
                    if t >= 2:
                        act.wait_ge(s_o, t - 1)
                    for q in range(3):
                        act.wait_ge(s_t, 3 * t + q + 1)
                        act.activation(probT[:, t % 2, q * HALF:(q + 1) * HALF], T.ps[:, 4 + q, :],
                                       ACT.Copy).then_inc(s_pT, 1)


def attention1_stage(nc, T):
    H, W = 12, 16
    with ExitStack() as ctx:
        sb = lambda n, s: ctx.enter_context(nc.sbuf_tensor(f"a1_{n}", s, F32))
        qT = sb("qT", [DC, 2, N_TOK])
        q_head = sb("q_head", [DC, 2, 6, N_TOK])
        v = sb("v", [P, NT, H, W + 1])
        ctxs = sb("ctxs", [P, NT, D])
        s_qmm, s_q, s_vmm, s_v, s_one, s_qh = sems(nc, ctx, "a1p", "q_products", "q", "v_products", "v", "ones",
                                                   "q_heads")
        with nc.Block() as block:
            @block.tensor
            def _(pe):
                pe.wait_ge(T.loaded["a1_w"], 16)
                pe.wait_ge(T.loaded["a1_proj"], 16)
                for c in range(2):
                    for half in range(2):
                        cols = slice(half * HALF, (half + 1) * HALF)
                        pe.matmul(T.ps[0:DC, 2 * c + half, :], T.w["a1_w"][:, 0, c * DC:(c + 1) * DC],
                                  T.xT[:, 0, cols], start=True, stop=False)
                        pe.matmul(T.ps[0:DC, 2 * c + half, :], T.w["a1_w"][0:DC, 1, c * DC:(c + 1) * DC],
                                  T.xT[0:DC, 1, cols], start=False, stop=True).then_inc(s_qmm, 1)
                for t in range(NT):
                    if t >= 4:
                        pe.wait_ge(s_v, t - 3)
                    pe.matmul(T.ps[:, 4 + t % 4, 0:D], T.xT[:, 0, t * P:(t + 1) * P], T.w["a1_w"][:, 0, :],
                              start=True, stop=False)
                    pe.matmul(T.ps[:, 4 + t % 4, 0:D], T.xT[0:DC, 1, t * P:(t + 1) * P], T.w["a1_w"][0:DC, 1, :],
                              start=False, stop=True).then_inc(s_vmm, 1)

            @block.scalar
            def _(act):
                for b in range(4):
                    act.wait_ge(s_qmm, b + 1)
                    act.activation(qT[:, b // 2, (b % 2) * HALF:(b % 2 + 1) * HALF], T.ps[0:DC, b, :],
                                   ACT.Copy).then_inc(s_q, 1)
                for t in range(NT):
                    act.wait_ge(s_vmm, t + 1)
                    act.activation(v[:, t, :, 0:W], T.ps[:, 4 + t % 4, 0:D].rearrange("p (h d) -> p h d", h=H),
                                   ACT.Copy).then_inc(s_v, 1)
                act.wait_ge(s_v, NT)

            @block.vector
            def _(dve):
                dve.memset(v[:, :, :, W:W + 1], 1.0).then_inc(s_one, 1)
                for c in range(2):
                    dve.wait_ge(s_q, 2 * c + 2)
                    for j in range(6):
                        dve.tensor_scalar(q_head[:, c, j, :], qT[:, c, :], T.consts[0:DC, C_M16 + j:C_M16 + j + 1],
                                          None, ALU.mult).then_inc(s_qh, 1)
                dve.wait_ge(s_one, 1)
                dve.wait_ge(s_qh, 12)

        def scores(t, g):
            c, j = g // 2, 3 * (g % 2)
            return qT[:, c, t * P:(t + 1) * P], q_head[:, c, j:j + 3, t * P:(t + 1) * P]

        windowed_attention(nc, T, "a1", scores, float(W) ** -0.5,
                           lambda t: T.causal3.unsqueeze(1).to_broadcast([P, 4, 384]),
                           H, W, v, lambda t: t, ctxs)

        s_tp, s_aT, s_mm, s_h = sems(nc, ctx, "a1o", "transposed", "aT", "products", "h")
        with nc.Block() as block:
            @block.tensor
            def _(pe):
                for t in range(NT):
                    for c in range(2):
                        mm = pe.transpose(T.ps[0:DC, t, c * P:(c + 1) * P], ctxs[:, t, c * DC:(c + 1) * DC], T.ident)
                    mm.then_inc(s_tp, 1)
                for t in range(NT):
                    pe.wait_ge(s_aT, t + 1)
                    pe.matmul(T.ps[:, t, 2 * P:2 * P + D], T.aT[:, 0, t * P:(t + 1) * P], T.w["a1_proj"][:, 0, :],
                              start=True, stop=False)
                    pe.matmul(T.ps[:, t, 2 * P:2 * P + D], T.aT[0:DC, 1, t * P:(t + 1) * P],
                              T.w["a1_proj"][0:DC, 1, :], start=False, stop=True).then_inc(s_mm, 1)

            @block.scalar
            def _(act):
                for t in range(NT):
                    act.wait_ge(s_tp, t + 1)
                    act.activation(T.aT[0:DC, :, t * P:(t + 1) * P],
                                   T.ps[0:DC, t, 0:2 * P].rearrange("p (c n) -> p c n", c=2),
                                   ACT.Copy).then_inc(s_aT, 1)

            @block.vector
            def _(dve):
                for t in range(NT):
                    dve.wait_ge(s_mm, t + 1)
                    dve.tensor_tensor(T.h[:, t, :], T.ps[:, t, 2 * P:2 * P + D], T.h[:, t, :],
                                      ALU.add).then_inc(s_h, 1)
                dve.wait_ge(s_h, NT)


def attention2_stage(nc, T, a):
    H, W, M = 4, 24, 64
    first_key_tile = lambda t: min(max(t - 1, 0), NT - 3)
    kind = lambda t: 0 if t == 0 else 2 if t == NT - 1 else 1
    with ExitStack() as ctx:
        sb = lambda n, s: ctx.enter_context(nc.sbuf_tensor(f"a2_{n}", s, F32))
        bias = sb("bias", [P, 3, 4, 384])
        xs = sb("xs", [DC, N_TOK])
        mid = sb("mid", [M, N_TOK])
        pre = sb("pre", [DC, N_TOK])
        qT = sb("qT", [DC, N_TOK])
        k_head = sb("k_head", [DC, H, N_TOK])
        v = sb("v", [P, NT, H, W + 1])
        ctxs = sb("ctxs", [P, NT, DC])
        ctxT = sb("ctxT", [DC, N_TOK])
        gT = T.aT[:, 0, :]
        s_b, s_f, s_xs, s_am, s_a, s_bm, s_p, s_g, s_qm, s_q, s_km, s_k, s_vm, s_v, s_one = sems(
            nc, ctx, "a2p", "bias", "fc1_products", "fc1", "convA_products", "convA", "convB_products",
            "pre", "gelu", "q_products", "q", "k_products", "k_heads", "v_products", "v", "ones")
        with nc.Block() as block:
            @block.sync
            def _(sp):
                sp.dma_start(bias[:, :, :, :].rearrange("p a b c -> p (a b c)"), a["a2_bias"]).then_inc(s_b, 16)
                sp.wait_ge(s_b, 16)

            @block.tensor
            def _(pe):
                for n in ("a2_fc1", "a2_convA", "a2_convB", "a2_qkv", "a2_proj", "a2_fc2", "a2_cols"):
                    pe.wait_ge(T.loaded[n], 16)
                cols = [slice(0, HALF), slice(HALF, N_TOK)]
                for i in range(2):
                    pe.matmul(T.ps[0:DC, i, :], T.w["a2_fc1"][:, 0, :], T.xT[:, 0, cols[i]], start=True, stop=False)
                    pe.matmul(T.ps[0:DC, i, :], T.w["a2_fc1"][0:DC, 1, :], T.xT[0:DC, 1, cols[i]],
                              start=False, stop=True).then_inc(s_f, 1)
                for i in range(2):
                    pe.wait_ge(s_xs, i + 1)
                    pe.matmul(T.ps[0:M, 2 + i, :], T.w["a2_convA"][:, :], xs[:, cols[i]],
                              start=True, stop=True).then_inc(s_am, 1)
                for i in range(2):
                    pe.wait_ge(s_a, i + 1)
                    pe.matmul(T.ps[0:DC, 4 + i, :], T.w["a2_convB"][:, :], mid[:, cols[i]],
                              start=True, stop=True).then_inc(s_bm, 1)
                for i in range(2):
                    pe.wait_ge(s_g, i + 1)
                    pe.matmul(T.ps[0:DC, i, :], T.w["a2_qkv"][:, 0:DC], gT[:, cols[i]],
                              start=True, stop=True).then_inc(s_qm, 1)
                    pe.matmul(T.ps[0:DC, 2 + i, :], T.w["a2_qkv"][:, DC:2 * DC], gT[:, cols[i]],
                              start=True, stop=True).then_inc(s_km, 1)
                for t in range(NT):
                    if t >= 2:
                        pe.wait_ge(s_v, t - 1)
                    pe.matmul(T.ps[:, 6 + t % 2, 0:DC], gT[:, t * P:(t + 1) * P], T.w["a2_qkv"][:, 2 * DC:3 * DC],
                              start=True, stop=True).then_inc(s_vm, 1)

            @block.scalar
            def _(act):
                for i in range(2):
                    act.wait_ge(s_f, i + 1)
                    act.activation(xs[:, i * HALF:(i + 1) * HALF], T.ps[0:DC, i, :], ACT.Copy).then_inc(s_xs, 1)
                for i in range(2):
                    act.wait_ge(s_am, i + 1)
                    act.activation(mid[:, i * HALF:(i + 1) * HALF], T.ps[0:M, 2 + i, :], ACT.Identity,
                                   bias=T.w["a2_cols"][0:M, 0:1]).then_inc(s_a, 1)
                for i in range(2):
                    act.wait_ge(s_p, i + 1)
                    act.activation(T.aT[0:DC, 0, i * HALF:(i + 1) * HALF], pre[:, i * HALF:(i + 1) * HALF],
                                   ACT.Gelu).then_inc(s_g, 1)
                for i in range(2):
                    act.wait_ge(s_qm, i + 1)
                    act.activation(qT[:, i * HALF:(i + 1) * HALF], T.ps[0:DC, i, :], ACT.Copy).then_inc(s_q, 1)
                for t in range(NT):
                    act.wait_ge(s_vm, t + 1)
                    act.activation(v[:, t, :, 0:W], T.ps[:, 6 + t % 2, 0:DC].rearrange("p (h d) -> p h d", h=H),
                                   ACT.Copy).then_inc(s_v, 1)
                act.wait_ge(s_v, NT)

            @block.vector
            def _(dve):
                dve.memset(v[:, :, :, W:W + 1], 1.0).then_inc(s_one, 1)
                for i in range(2):
                    cols = slice(i * HALF, (i + 1) * HALF)
                    dve.wait_ge(s_bm, i + 1)
                    dve.wait_ge(s_xs, i + 1)
                    dve.scalar_tensor_tensor(pre[:, cols], T.ps[0:DC, 4 + i, :], T.w["a2_cols"][:, 1:2], xs[:, cols],
                                             ALU.add, ALU.add).then_inc(s_p, 1)
                for i in range(2):
                    dve.wait_ge(s_km, i + 1)
                    for n in range(H):
                        dve.tensor_scalar(k_head[:, n, i * HALF:(i + 1) * HALF], T.ps[0:DC, 2 + i, :],
                                          T.consts[0:DC, C_M24 + n:C_M24 + n + 1], None, ALU.mult).then_inc(s_k, 1)
                dve.wait_ge(s_k, 2 * H)
                dve.wait_ge(s_one, 1)

        def scores(t, g):
            k0 = first_key_tile(t) * P
            return qT[:, t * P:(t + 1) * P], k_head[:, g, k0:k0 + 384]

        windowed_attention(nc, T, "a2", scores, float(W) ** -0.5, lambda t: bias[:, kind(t), :, :],
                           H, W, v, first_key_tile, ctxs)

        s_tp, s_cT, s_pm, s_pT, s_mm, s_hx, s_h = sems(nc, ctx, "a2o", "transposed", "ctxT", "proj_products",
                                                       "proj", "products", "h_x", "h")
        with nc.Block() as block:
            @block.tensor
            def _(pe):
                for t in range(NT):
                    mm = pe.transpose(T.ps[0:DC, t // 4, (t % 4) * P:(t % 4 + 1) * P], ctxs[:, t, :], T.ident)
                    if t % 4 == 3:
                        mm.then_inc(s_tp, 1)
                for i in range(2):
                    pe.wait_ge(s_cT, i + 1)
                    pe.matmul(T.ps[0:DC, 2 + i, :], T.w["a2_proj"][:, :], ctxT[:, i * HALF:(i + 1) * HALF],
                              start=True, stop=True).then_inc(s_pm, 1)
                for t in range(NT):
                    pe.wait_ge(s_pT, t // 4 + 1)
                    if t >= 4:
                        pe.wait_ge(s_h, t - 3)
                    pe.matmul(T.ps[:, 4 + t % 4, 0:D], gT[:, t * P:(t + 1) * P], T.w["a2_fc2"][:, :],
                              start=True, stop=True).then_inc(s_mm, 1)

            @block.scalar
            def _(act):
                for i in range(2):
                    act.wait_ge(s_tp, i + 1)
                    act.activation(ctxT[:, i * HALF:(i + 1) * HALF], T.ps[0:DC, i, :], ACT.Copy).then_inc(s_cT, 1)
                for i in range(2):
                    act.wait_ge(s_pm, i + 1)
                    act.activation(T.aT[0:DC, 0, i * HALF:(i + 1) * HALF], T.ps[0:DC, 2 + i, :], ACT.Identity,
                                   bias=T.w["a2_cols"][:, 2:3]).then_inc(s_pT, 1)

            @block.vector
            def _(dve):
                dve.tensor_tensor(T.h[:, :, :], T.h[:, :, :], T.xn[:, :, :], ALU.add).then_inc(s_hx, 1)
                dve.wait_ge(s_hx, 1)
                for t in range(NT):
                    dve.wait_ge(s_mm, t + 1)
                    dve.tensor_tensor(T.h[:, t, :], T.ps[:, 4 + t % 4, 0:D], T.h[:, t, :],
                                      ALU.add).then_inc(s_h, 1)
                dve.wait_ge(s_h, NT)


class Moe:

    def __init__(self, name, experts, picks, shared=False, renormalise=False, biased=True):
        self.name, self.E, self.K, self.shared, self.renormalise = name, experts, picks, shared, renormalise
        self.biased = biased
        self.C = picks + shared
        most = (N_TOK * self.C + experts * (P - 1)) // P
        self.tiles = -(-most // 4) * 4


def route_stage(nc, T, m, gate_w):
    E, K, C, name = m.E, m.K, m.C, m.name
    with ExitStack() as ctx:
        sb = lambda n, s, dt=F32: ctx.enter_context(nc.sbuf_tensor(f"{name}r_{n}", s, dt))
        logit = sb("logit", [P, NT, E])
        prob = sb("prob", [P, NT, E])
        small = sb("small", [P, 3, NT])
        best = sb("best", [P, NT, 8])
        best_at = sb("best_at", [P, NT, 8], U32)
        best_f = sb("best_f", [P, NT, 8])
        pick = sb("pick", [P, C, NT, E])
        taken = sb("taken", [P, NT, E])
        totals = sb("totals", [P, NT, E])
        before = sb("before", [P, NT + 1, E])
        n_tiles = sb("n_tiles", [P, E])
        ends = sb("ends", [P, E])
        zeros = sb("zeros", [P, E])
        start = sb("start", [P, E])
        slot = sb("slot", [P, NT, E])
        slot_of = sb("slot_of", [P, C, NT, E])
        slot_f = sb("slot_f", [P, C, NT])
        past = sb("past", [1, m.tiles, E])
        map_f = sb("map_f", [1, m.tiles + 1])
        round_used = sb("round_used", [1, m.tiles // U])
        s_c, s_mm, s_sh, s_e, s_tk, s_rk, s_sl = sems(
            nc, ctx, f"{name}r", "chain", "logits", "shifted", "exps", "taken", "ranks", "slots")
        iota = T.consts[:, C_IOTA:C_IOTA + E]
        over_tiles = lambda x: x.unsqueeze(1).to_broadcast([P, NT, E])
        over_experts = lambda x: x.unsqueeze(2).to_broadcast([P, NT, E])
        with nc.Block() as block:
            @block.tensor
            def _(pe):
                pe.wait_ge(T.loaded[gate_w], 16)
                w = T.w[gate_w]
                for t in range(NT):
                    pe.matmul(T.ps[:, 0, t * E:(t + 1) * E], T.xT[:, 0, t * P:(t + 1) * P], w[:, 0, :],
                              start=True, stop=False)
                    mm = pe.matmul(T.ps[:, 0, t * E:(t + 1) * E], T.xT[0:DC, 1, t * P:(t + 1) * P],
                                   w[0:DC, 1, :], start=False, stop=True)
                mm.then_inc(s_mm, 1)
                pe.wait_ge(s_tk, 1)
                both = taken[:, :, :].rearrange("p t e -> p (t e)")
                pe.matmul(T.ps[:, 1, 0:NT * E], T.consts[:, C_LT:C_LT + P], both, start=True, stop=True)
                pe.matmul(T.ps[:, 2, 0:NT * E], T.ones[:, :], both, start=True, stop=True).then_inc(s_rk, 1)

            @block.scalar
            def _(act):
                act.wait_ge(s_sh, 1)
                act.activation(prob[:, :, :], logit[:, :, :], ACT.Exp).then_inc(s_e, 1)

            @block.vector
            def _(dve):
                chain = Chain(dve, s_c)
                dve.wait_ge(s_mm, 1)
                chain(dve.tensor_copy(logit[:, :, :], T.ps[:, 0, 0:NT * E].rearrange("p (t e) -> p t e", e=E)))
                if m.shared:
                    chain(dve.memset(logit[:, :, 0:1], -1.0e9))
                chain(dve.tensor_reduce(small[:, 0, :], logit[:, :, :], AX_X, ALU.max))
                dve.tensor_tensor(logit[:, :, :], logit[:, :, :], over_experts(small[:, 0, :]),
                                  ALU.subtract).then_inc(s_sh, 1)
                dve.wait_ge(s_e, 1)
                chain(dve.tensor_reduce(small[:, 1, :], prob[:, :, :], AX_X, ALU.add))
                chain(dve.reciprocal(small[:, 2, :], small[:, 1, :]))
                chain(dve.tensor_tensor(prob[:, :, :], prob[:, :, :], over_experts(small[:, 2, :]), ALU.mult))
                for t in range(NT):
                    ins = dve.max(best[:, t, :], prob[:, t, :])
                chain(ins)
                for t in range(NT):
                    ins = dve.max_index(best_at[:, t, :], best[:, t, :], prob[:, t, :])
                chain(ins)
                chain(dve.tensor_copy(best_f[:, :, :], best_at[:, :, :]))
                for k in range(K):
                    chain(dve.tensor_tensor(pick[:, k, :, :], over_tiles(iota), over_experts(best_f[:, :, k]),
                                            ALU.is_equal))
                    dve_w = dve.tensor_copy(m.gate[:, k, :], best[:, :, k])
                    chain(dve_w)
                if m.shared:
                    chain(dve.memset(pick[:, K, :, :], 0.0))
                    chain(dve.memset(pick[:, K, :, 0:1], 1.0))
                    chain(dve.memset(m.gate[:, K, :], 1.0))
                if m.renormalise:
                    chain(dve.tensor_tensor(small[:, 0, :], m.gate[:, 0, :], m.gate[:, 1, :], ALU.add))
                    chain(dve.tensor_scalar(small[:, 0, :], small[:, 0, :], 1.0e-20, None, ALU.add))
                    chain(dve.reciprocal(small[:, 1, :], small[:, 0, :]))
                    for k in range(K):
                        chain(dve.tensor_tensor(m.gate[:, k, :], m.gate[:, k, :], small[:, 1, :], ALU.mult))
                chain(dve.tensor_tensor(taken[:, :, :], pick[:, 0, :, :], pick[:, 1, :, :], ALU.add))
                for k in range(2, C):
                    chain(dve.tensor_tensor(taken[:, :, :], taken[:, :, :], pick[:, k, :, :], ALU.add))
                dve.sem_inc(s_tk, 1)
                dve.wait_ge(s_rk, 1)
                chain(dve.memset(before[:, 0, :], 0.0))
                chain(dve.memset(zeros[:, :], 0.0))
                chain(dve.tensor_copy(totals[:, :, :], T.ps[:, 2, 0:NT * E].rearrange("p (t e) -> p t e", e=E)))
                for t in range(NT):
                    chain(dve.tensor_tensor(before[:, t + 1, :], before[:, t, :], totals[:, t, :], ALU.add))
                chain(dve.tensor_scalar(n_tiles[:, :], before[:, NT, :], 0.0, None, ALU.is_gt))
                for j in range(1, NT * (1 + m.shared)):
                    chain(dve.scalar_tensor_tensor(n_tiles[:, :], before[:, NT, :], float(P * j), n_tiles[:, :],
                                                   ALU.is_gt, ALU.add))
                chain(dve.tensor_tensor_scan(ends[:, :], n_tiles[:, :], zeros[:, :], 0.0, ALU.add, ALU.add))
                chain(dve.tensor_tensor(start[:, :], ends[:, :], n_tiles[:, :], ALU.subtract))
                chain(dve.tensor_scalar(start[:, :], start[:, :], float(P), None, ALU.mult))
                chain(dve.tensor_tensor(slot[:, :, :], T.ps[:, 1, 0:NT * E].rearrange("p (t e) -> p t e", e=E),
                                        before[:, 0:NT, :], ALU.add))
                chain(dve.tensor_tensor(slot[:, :, :], slot[:, :, :], over_tiles(start[:, :]), ALU.add))
                for k in range(C):
                    chain(dve.tensor_tensor(slot_of[:, k, :, :], pick[:, k, :, :], slot[:, :, :], ALU.mult))
                chain(dve.tensor_reduce(slot_f[:, :, :].rearrange("p c t -> p (c t)"),
                                        slot_of[:, :, :, :].rearrange("p c t e -> p (c t) e"), AX_X, ALU.add))
                dve.tensor_copy(m.slots[:, :, :], slot_f[:, :, :]).then_inc(s_sl, 1)
                chain(dve.tensor_tensor(past[:, :, :],
                                        T.consts[0:1, C_IOTA:C_IOTA + m.tiles].unsqueeze(2)
                                        .to_broadcast([1, m.tiles, E]),
                                        ends[0:1, :].unsqueeze(1).to_broadcast([1, m.tiles, E]), ALU.is_ge))
                chain(dve.tensor_reduce(map_f[:, 0:m.tiles], past[:, :, :], AX_X, ALU.add))
                chain(dve.tensor_scalar(map_f[:, 0:m.tiles], map_f[:, 0:m.tiles], float(E - 1), None, ALU.min))
                chain(dve.tensor_scalar(round_used[:, :], T.consts[0:1, C_IOTA:C_IOTA + m.tiles // U], float(U),
                                        ends[0:1, E - 1:E], ALU.mult, ALU.is_lt))
                chain(dve.tensor_reduce(map_f[:, m.tiles:m.tiles + 1], round_used[:, :], AX_X, ALU.add))
                chain(dve.tensor_copy(m.expert_of[:, :], map_f[:, :]))
                if m.biased:
                    for k in range(C):
                        weighted = m.gates[:, :, :] if k == 0 else slot_of[:, k, :, :]
                        chain(dve.tensor_tensor(weighted, pick[:, k, :, :], over_experts(m.gate[:, k, :]), ALU.mult))
                        if k:
                            chain(dve.tensor_tensor(m.gates[:, :, :], m.gates[:, :, :], weighted, ALU.add))

            @block.gpsimd
            def _(pool):
                pool.wait_ge(s_sl, 1)
                pool.wait_ge(T.s_cleared, 96)
                for t in range(NT):
                    for k in range(C):
                        pool.indirect_dma_start(
                            m.slots_x, bass.IndirectOffsetOnAxis(m.slots[:, k, t:t + 1], 0),
                            T.xn[:, t, :], None).then_inc(m.s_scattered, 16)
                pool.wait_ge(m.s_scattered, 16 * NT * C)


def combine_stage(nc, T, m, plus_x, bias=None):
    E = m.E
    with ExitStack() as ctx:
        y = ctx.enter_context(nc.sbuf_tensor(f"{m.name}c_y", [P, NT, m.C, D], F32))
        s_c, s_h = sems(nc, ctx, f"{m.name}c", "chain", "h")
        if bias is not None:
            b = ctx.enter_context(nc.sbuf_tensor(f"{m.name}c_b", [E, D], F32))
            gatesT = ctx.enter_context(nc.sbuf_tensor(f"{m.name}c_gatesT", [E, N_TOK], F32))
            s_b, s_tp, s_gT, s_bm = sems(nc, ctx, f"{m.name}b", "bias", "transposed", "gatesT", "bias_products")
        with nc.Block() as block:
            if bias is not None:
                @block.sync
                def _(sp):
                    sp.dma_start(b[:, :], bias).then_inc(s_b, 16)

                @block.tensor
                def _(pe):
                    for t in range(NT):
                        mm = pe.transpose(T.ps[0:E, t // 4, (t % 4) * P:(t % 4 + 1) * P], m.gates[:, t, :], T.ident)
                        if t % 4 == 3:
                            mm.then_inc(s_tp, 1)
                    pe.wait_ge(s_b, 16)
                    for t in range(NT):
                        pe.wait_ge(s_gT, t // 4 + 1)
                        if t >= 4:
                            pe.wait_ge(s_h, t - 3)
                        pe.matmul(T.ps[:, 4 + t % 4, 0:D], gatesT[:, t * P:(t + 1) * P], b[:, :],
                                  start=True, stop=True).then_inc(s_bm, 1)

                @block.scalar
                def _(act):
                    for i in range(2):
                        act.wait_ge(s_tp, i + 1)
                        act.activation(gatesT[:, i * HALF:(i + 1) * HALF], T.ps[0:E, i, :], ACT.Copy).then_inc(s_gT, 1)

            @block.gpsimd
            def _(pool):
                for t in range(NT):
                    for k in range(m.C):
                        pool.indirect_dma_start(
                            y[:, t, k, :], None, m.slots_y,
                            bass.IndirectOffsetOnAxis(m.slots[:, k, t:t + 1], 0)).then_inc(m.s_gathered[t], 16)

            @block.vector
            def _(dve):
                chain = Chain(dve, s_c)
                if plus_x:
                    chain(dve.tensor_tensor(T.h[:, :, :], T.h[:, :, :], T.xn[:, :, :], ALU.add))
                if bias is not None:
                    for t in range(NT):
                        dve.wait_ge(s_bm, t + 1)
                        dve.tensor_tensor(T.h[:, t, :], T.ps[:, 4 + t % 4, 0:D], T.h[:, t, :],
                                          ALU.add).then_inc(s_h, 1)
                    dve.wait_ge(s_h, NT)
                for t in range(NT):
                    dve.wait_ge(m.s_gathered[t], 16 * m.C)
                    for k in range(m.C):
                        chain(dve.scalar_tensor_tensor(T.h[:, t, :], y[:, t, k, :], m.gate[:, k, t:t + 1],
                                                       T.h[:, t, :], ALU.mult, ALU.add))


U = 4
LAG = 2


def pipelined(eng, m, steps, at_end=None):
    rounds, least = m.tiles // U, N_TOK * m.C // (P * U)
    used = eng.value_load(m.expert_of[0:1, m.tiles:m.tiles + 1], min_val=least, max_val=rounds)

    def turn(i, q, first_pair=None, last_pair=None):
        for lag, body in steps:
            back, pair = divmod(q - lag, 2)
            if first_pair is not None and q - lag < first_pair or last_pair is not None and q - lag > last_pair:
                continue
            body(eng, Loop(i + back if back else i, isinstance(i, int) and i + back == 0), (2 * pair, 2 * pair + 1))

    for i in range(2):
        for q in range(2):
            turn(i, q, first_pair=-2 * i)
    with eng.Fori(2, rounds) as i:
        with eng.If(i < used):
            for q in range(2):
                turn(i, q)
        with eng.If(i + 1 == used):
            for q in range(2, 2 + LAG):
                turn(i, q, last_pair=1)
            if at_end:
                at_end(i + 1)


class Loop:

    def __init__(self, i, first):
        self.i, self.first = i, first

    def after(self, u, times=1, back=0):
        return self.i * (U * times) + (u + 1 - back) * times


def expert_loop(nc, T, m, weights, layers):
    name = m.name
    with ExitStack() as ctx:
        sb = lambda n, s, dt=F32: ctx.enter_context(nc.sbuf_tensor(f"{name}e_{n}", s, dt))
        x = sb("x", [P, U, D])
        xsT = sb("xsT", [DC + 1, U, 2, P])
        y = sb("y", [P, U, D])
        bufs = [sb(f"w{n}", [w.shape[1], U, w.shape[2]]) for n, w in enumerate(weights)]
        s_x = sems(nc, ctx, f"{name}e", *[f"x{u}" for u in range(U)])
        s_w = [sems(nc, ctx, f"{name}e_w{n}", *[f"in{u}" for u in range(U)]) for n in range(len(weights))]
        s_out = m.s_stored
        s_tp, s_xs, s_1, s_ymm, s_y, s_one = sems(
            nc, ctx, f"{name}e", "transposed", "xsT", "layer1", "y_products", "y", "ones")

        def load_x(sp, at, tiles):
            for u in tiles:
                if not at.first:
                    sp.wait_ge(s_tp, at.after(u, back=U))
                sp.dma_start(x[:, u, :], m.slots_x[bass.ds(at.i * (U * P) + u * P, P), :]).then_inc(s_x[u], 16)

        def load_w(n, s_used):
            def load(sp, at, tiles):
                for u in tiles:
                    expert = sp.value_load(m.expert_of[0:1, bass.ds(at.i * U + u, 1)], min_val=0, max_val=m.E - 1)
                    if not at.first:
                        sp.wait_ge(s_used, at.after(u, back=U))
                    sp.dma_start(bufs[n][:, u, :],
                                 weights[n][bass.ds(expert, 1), :, :].rearrange("a p n -> p (a n)")
                                 ).then_inc(s_w[n][u], 16)
            return load

        def turn_x(pe, at, tiles):
            for u in tiles:
                pe.wait_ge(s_x[u], 16 * (at.i + 1))
                for c in range(2):
                    mm = pe.transpose(T.ps[0:DC, 4 * (u % 2), c * P:(c + 1) * P], x[:, u, c * DC:(c + 1) * DC],
                                      T.ident)
                mm.then_inc(s_tp, 1)

        def copy_x(dve, at, tiles):
            for u in tiles:
                dve.wait_ge(s_tp, at.after(u))
                dve.tensor_copy(xsT[0:DC, u, :, :], T.ps[0:DC, 4 * (u % 2), 0:2 * P].rearrange("p (c n) -> p c n", c=2)
                                ).then_inc(s_xs, 1)

        def copy_y(dve, at, tiles):
            for u in tiles:
                dve.wait_ge(s_ymm, at.after(u))
                if not at.first:
                    dve.wait_ge(s_out[u], 16 * at.i)
                dve.tensor_copy(y[:, u, :], T.ps[:, 4 * (u % 2) + 3, 0:D]).then_inc(s_y, 1)

        def store_y(pool, at, tiles):
            for u in tiles:
                pool.wait_ge(s_y, at.after(u))
                pool.dma_start(m.slots_y[bass.ds(at.i * (U * P) + u * P, P), :], y[:, u, :]).then_inc(s_out[u], 16)

        S = dict(xsT=xsT, bufs=bufs, s_w=s_w, s_xs=s_xs, s_1=s_1, s_ymm=s_ymm, s_y=s_y, ctx=ctx,
                 turn_x=turn_x, copy_x=copy_x, copy_y=copy_y, store_y=store_y)
        steps = layers(S)
        with nc.Block() as block:
            @block.sync
            def _(sp):
                loads = [(0, load_x), (0, load_w(0, s_1))]
                pipelined(sp, m, loads + [(1, load_w(n, s_ymm)) for n in range(1, len(weights))])

            @block.gpsimd
            def _(pool):
                def all_stored(rounds):
                    for u in range(U):
                        pool.wait_ge(s_out[u], rounds * 16)
                pipelined(pool, m, steps["pool"], all_stored)

            @block.tensor
            def _(pe):
                pipelined(pe, m, steps["pe"])

            @block.vector
            def _(dve):
                dve.memset(xsT[DC:DC + 1, :, 0, :], 1.0).then_inc(s_one, 1)
                dve.wait_ge(s_one, 1)
                steps["dve_first"](dve)
                pipelined(dve, m, steps["dve"])

            @block.scalar
            def _(act):
                pipelined(act, m, steps["act"])


def moe1(nc, T, a):
    m = T.m1
    F, FC = 768, 6
    route_stage(nc, T, m, "e1_gate")

    def layers(S):
        xsT, (w1, w2) = S["xsT"], S["bufs"]
        h1 = S["ctx"].enter_context(nc.sbuf_tensor("m1_h1", [P, U, F], F32))
        s_1, s_g = S["s_1"], sems(nc, S["ctx"], "m1x", "gelu")[0]

        def layer1(pe, at, tiles):
            for u in tiles:
                pe.wait_ge(S["s_xs"], at.after(u))
                pe.wait_ge(S["s_w"][0][u], 16 * (at.i + 1))
                if not (at.first and u < 2):
                    pe.wait_ge(s_g, at.after(u, back=2))
                b = 4 * (u % 2) + 1
                flat = T.ps[:, b:b + 2, :].rearrange("p b n -> p (b n)")
                for j in range(FC):
                    out = flat[:, j * P:(j + 1) * P]
                    pe.matmul(out, w1[:, u, j * P:(j + 1) * P], xsT[:, u, 0, :], start=True, stop=False)
                    mm = pe.matmul(out, w1[0:DC, u, F + j * P:F + (j + 1) * P], xsT[0:DC, u, 1, :],
                                   start=False, stop=True)
                mm.then_inc(s_1, 1)

        def layer2(pe, at, tiles):
            for u in tiles:
                pe.wait_ge(s_g, at.after(u))
                pe.wait_ge(S["s_w"][1][u], 16 * (at.i + 1))
                if not (at.first and u < 2):
                    pe.wait_ge(S["s_y"], at.after(u, back=2))
                out = T.ps[:, 4 * (u % 2) + 3, 0:D]
                for j in range(FC):
                    mm = pe.matmul(out, h1[:, u, j * P:(j + 1) * P], w2[:, u, j * D:(j + 1) * D],
                                   start=(j == 0), stop=(j == FC - 1))
                mm.then_inc(S["s_ymm"], 1)

        def gelu(act, at, tiles):
            for u in tiles:
                act.wait_ge(s_1, at.after(u))
                b = 4 * (u % 2) + 1
                act.activation(h1[:, u, :], T.ps[:, b:b + 2, :].rearrange("p b n -> p (b n)")[:, 0:F],
                               ACT.Gelu).then_inc(s_g, 1)

        return {"pe": [(1, layer1), (0, S["turn_x"]), (2, layer2)], "act": [(1, gelu)],
                "dve": [(0, S["copy_x"]), (2, S["copy_y"])], "pool": [(2, S["store_y"])],
                "dve_first": lambda dve: None}

    expert_loop(nc, T, m, [a["e1_w1"], a["e1_w2"]], layers)
    combine_stage(nc, T, m, plus_x=True, bias=a["e1_w1"][:, DC, F:F + D])


def moe2(nc, T, a):
    m = T.m2
    F, FC, B = 512, 4, 64
    W3 = FC * F
    B2 = W3 + FC * B
    route_stage(nc, T, m, "e2_gate")

    def layers(S):
        xsT, (w1, w23, wl) = S["xsT"], S["bufs"]
        sb = lambda n, s: S["ctx"].enter_context(nc.sbuf_tensor(f"m2_{n}", s, F32))
        h1, h2, z = sb("h1", [P, U, F]), sb("h2", [P, U, F]), sb("z", [B + 1, U, P])
        s_1 = S["s_1"]
        s_g1, s_2, s_g2, s_3, s_z, s_one = sems(nc, S["ctx"], "m2x", "gelu1", "layer2", "gelu2",
                                                     "layer3", "z", "ones")

        def layer1(pe, at, tiles):
            for u in tiles:
                pe.wait_ge(S["s_xs"], at.after(u))
                pe.wait_ge(S["s_w"][0][u], 16 * (at.i + 1))
                for j in range(FC):
                    out = T.ps[:, 4 * (u % 2) + 1, j * P:(j + 1) * P]
                    pe.matmul(out, w1[:, u, j * P:(j + 1) * P], xsT[:, u, 0, :], start=True, stop=False)
                    mm = pe.matmul(out, w1[0:DC, u, F + j * P:F + (j + 1) * P], xsT[0:DC, u, 1, :],
                                   start=False, stop=True)
                mm.then_inc(s_1, 1)

        def layer2(pe, at, tiles):
            for u in tiles:
                pe.wait_ge(s_g1, at.after(u))
                pe.wait_ge(S["s_w"][1][u], 16 * (at.i + 1))
                for j in range(FC):
                    out = T.ps[:, 4 * (u % 2) + 2, j * P:(j + 1) * P]
                    for k in range(FC):
                        mm = pe.matmul(out, w23[:, u, k * F + j * P:k * F + (j + 1) * P],
                                       h1[:, u, k * P:(k + 1) * P], start=(k == 0), stop=(k == FC - 1))
                mm.then_inc(s_2, 1)

        def layer34(pe, at, tiles):
            for u in tiles:
                pe.wait_ge(s_g2, at.after(u, times=FC))
                if not (at.first and u < 2):
                    pe.wait_ge(S["s_y"], at.after(u, back=2))
                for k in range(FC):
                    mm = pe.matmul(T.ps[0:B, 4 * (u % 2) + 3, 384:512], w23[:, u, W3 + k * B:W3 + (k + 1) * B],
                                   h2[:, u, k * P:(k + 1) * P], start=(k == 0), stop=(k == FC - 1))
                mm.then_inc(s_3, 1)
            for u in tiles:
                pe.wait_ge(s_z, at.after(u))
                pe.wait_ge(S["s_w"][2][u], 16 * (at.i + 1))
                pe.matmul(T.ps[:, 4 * (u % 2) + 3, 0:D], z[:, u, :], wl[:, u, 0:D],
                          start=True, stop=True).then_inc(S["s_ymm"], 1)

        def gelu1(act, at, tiles):
            for u in tiles:
                act.wait_ge(s_1, at.after(u))
                act.activation(h1[:, u, :], T.ps[:, 4 * (u % 2) + 1, :], ACT.Gelu).then_inc(s_g1, 1)

        def gelu2(act, at, tiles):
            for u in tiles:
                act.wait_ge(s_2, at.after(u))
                for j in range(FC):
                    act.activation(h2[:, u, j * P:(j + 1) * P], T.ps[:, 4 * (u % 2) + 2, j * P:(j + 1) * P],
                                   ACT.Gelu, bias=w23[:, u, B2 + j:B2 + j + 1]).then_inc(s_g2, 1)

        def add_b3(dve, at, tiles):
            for u in tiles:
                dve.wait_ge(s_3, at.after(u))
                dve.wait_ge(S["s_w"][2][u], 16 * (at.i + 1))
                dve.tensor_scalar(z[0:B, u, :], T.ps[0:B, 4 * (u % 2) + 3, 384:512], wl[0:B, u, D:D + 1], None,
                                  ALU.add).then_inc(s_z, 1)

        def dve_first(dve):
            dve.memset(z[B:B + 1, :, :], 1.0).then_inc(s_one, 1)
            dve.wait_ge(s_one, 1)

        return {"pe": [(2, layer2), (1, layer1), (0, S["turn_x"]), (2, layer34)],
                "act": [(2, gelu2), (1, gelu1)],
                "dve": [(0, S["copy_x"]), (2, add_b3), (2, S["copy_y"])],
                "pool": [(2, S["store_y"])], "dve_first": dve_first}

    expert_loop(nc, T, m, [a["e2_w1"], a["e2_w23"], a["e2_wl"]], layers)
    combine_stage(nc, T, m, plus_x=False)


def moe0(nc, T, a):
    m = T.m0
    F, FC = 384, 3
    LNW = FC * D
    LNB = LNW + FC
    route_stage(nc, T, m, "e0_gate")

    def layers(S):
        xsT, (w1, w2) = S["xsT"], S["bufs"]
        sb = lambda n, s: S["ctx"].enter_context(nc.sbuf_tensor(f"m0_{n}", s, F32))
        g, gn, hT = sb("g", [P, U, F]), sb("gn", [P, U, F]), sb("hT", [P, U, F])
        stats, mv, rstd, power = sb("stats", [P, U, 6]), sb("mv", [P, U, 2]), sb("rstd", [P, U]), sb("power", [P, 1])
        s_1 = S["s_1"]
        s_g, s_st, s_mv, s_var, s_r, s_n, s_t, s_hT, s_pw, s_waited = sems(
            nc, S["ctx"], "m0x", "gelu", "stats", "moments", "variance", "rstd", "normed", "transposed",
            "hT", "power", "waited")

        def layer1(pe, at, tiles):
            for u in tiles:
                pe.wait_ge(S["s_xs"], at.after(u))
                pe.wait_ge(S["s_w"][0][u], 16 * (at.i + 1))
                out = T.ps[:, 4 * (u % 2) + 1, 0:F]
                pe.matmul(out, xsT[:, u, 0, :], w1[:, u, 0:F], start=True, stop=False)
                pe.matmul(out, xsT[0:DC, u, 1, :], w1[0:DC, u, F:2 * F], start=False, stop=True).then_inc(s_1, 1)

        def turn_h(pe, at, tiles):
            for u in tiles:
                pe.wait_ge(s_n, at.after(u))
                for j in range(FC):
                    mm = pe.transpose(T.ps[:, 4 * (u % 2) + 2, j * P:(j + 1) * P], gn[:, u, j * P:(j + 1) * P], T.ident)
                mm.then_inc(s_t, 1)

        def layer2(pe, at, tiles):
            for u in tiles:
                pe.wait_ge(s_hT, at.after(u, times=FC))
                pe.wait_ge(S["s_w"][1][u], 16 * (at.i + 1))
                if not (at.first and u < 2):
                    pe.wait_ge(S["s_y"], at.after(u, back=2))
                out = T.ps[:, 4 * (u % 2) + 3, 0:D]
                for j in range(FC):
                    mm = pe.matmul(out, hT[:, u, j * P:(j + 1) * P], w2[:, u, j * D:(j + 1) * D],
                                   start=(j == 0), stop=(j == FC - 1))
                mm.then_inc(S["s_ymm"], 1)

        def gelu(act, at, tiles):
            for u in tiles:
                act.wait_ge(s_1, at.after(u))
                act.activation(g[:, u, :], T.ps[:, 4 * (u % 2) + 1, 0:F], ACT.Gelu).then_inc(s_g, 1)

        def scale_h(act, at, tiles):
            for u in tiles:
                act.wait_ge(s_t, at.after(u))
                act.wait_ge(S["s_w"][1][u], 16 * (at.i + 1))
                for j in range(FC):
                    act.activation(hT[:, u, j * P:(j + 1) * P], T.ps[:, 4 * (u % 2) + 2, j * P:(j + 1) * P],
                                   ACT.Identity, bias=w2[:, u, LNB + j:LNB + j + 1],
                                   scale=w2[:, u, LNW + j:LNW + j + 1]).then_inc(s_hT, 1)

        def normalise(dve, at, tiles):
            for u in tiles:
                dve.wait_ge(s_g, at.after(u))
                dve.bn_stats(stats[:, u, :], g[:, u, :]).then_inc(s_st, 1)
            for u in tiles:
                wait_alone(dve, s_st, at.after(u), s_waited)
                dve.bn_aggr(mv[:, u, :], stats[:, u, :]).then_inc(s_mv, 1)
            for u in tiles:
                dve.wait_ge(s_mv, at.after(u))
                dve.tensor_scalar(mv[:, u, 1:2], mv[:, u, 1:2], 1e-5, None, ALU.add).then_inc(s_var, 1)
            for u in tiles:
                dve.wait_ge(s_r, at.after(u))
                dve.tensor_scalar(gn[:, u, :], g[:, u, :], mv[:, u, 0:1], rstd[:, u:u + 1],
                                  ALU.subtract, ALU.mult).then_inc(s_n, 1)

        def inverse_root(pool, at, tiles):
            for u in tiles:
                pool.wait_ge(s_var, at.after(u))
                pool.tensor_tensor(rstd[:, u:u + 1], mv[:, u, 1:2], power[:, :], ALU.pow).then_inc(s_r, 1)

        def dve_first(dve):
            dve.memset(power[:, :], -0.5).then_inc(s_pw, 1)
            dve.wait_ge(s_pw, 1)

        return {"pe": [(2, turn_h), (1, layer1), (0, S["turn_x"]), (2, layer2)],
                "act": [(2, scale_h), (1, gelu)],
                "dve": [(0, S["copy_x"]), (1, normalise), (2, S["copy_y"])],
                "pool": [(1, inverse_root), (2, S["store_y"])], "dve_first": dve_first}

    expert_loop(nc, T, m, [a["e0_w1"], a["e0_w2"]], layers)
    combine_stage(nc, T, m, plus_x=False, bias=a["e0_w1"][:, DC, F:F + D])


def rms_stage(nc, T, name, weight):
    with ExitStack() as ctx:
        sb = lambda n, s: ctx.enter_context(nc.sbuf_tensor(f"{name}_{n}", s, F32))
        square, ms, rstd, power, xr = sb("square", [P, D]), sb("ms", [P, NT]), sb("rstd", [P, NT]), \
            sb("power", [P, NT]), sb("xr", [P, NT, D])
        s_c, s_sq, s_ms, s_r, s_xr, s_tp, s_cp = sems(nc, ctx, name, "chain", "squares", "mean_square", "rstd",
                                                      "xr", "transposed", "copied")
        with nc.Block() as block:
            @block.scalar
            def _(act):
                for t in range(NT):
                    if t:
                        act.wait_ge(s_sq, t)
                    act.activation(square[:, :], T.xn[:, t, :], ACT.Square,
                                   accum_out=ms[:, t:t + 1]).then_inc(s_sq, 1)

            @block.gpsimd
            def _(pool):
                pool.wait_ge(s_ms, 1)
                pool.tensor_tensor(rstd[:, :], ms[:, :], power[:, :], ALU.pow).then_inc(s_r, 1)

            @block.vector
            def _(dve):
                chain = Chain(dve, s_c)
                chain(dve.memset(power[:, :], -0.5))
                dve.wait_ge(s_sq, NT)
                dve.wait_ge(T.loaded["a3_norm1"], 16)
                dve.wait_ge(T.loaded["a3_norm2"], 16)
                dve.tensor_scalar(ms[:, :], ms[:, :], 1.0 / D, 1e-6, ALU.mult, ALU.add).then_inc(s_ms, 1)
                dve.wait_ge(s_r, 1)
                for t in range(NT):
                    dve.tensor_scalar(xr[:, t, :], T.xn[:, t, :], rstd[:, t:t + 1], None,
                                      ALU.mult).then_inc(s_xr, 1)
                for t in range(NT):
                    dve.wait_ge(s_tp, t + 1)
                    for c in range(2):
                        dve.tensor_scalar(T.xT[0:DC, c, t * P:(t + 1) * P], T.ps[0:DC, t, c * P:(c + 1) * P],
                                          weight[:, c:c + 1], None, ALU.mult).then_inc(s_cp, 1)
                dve.wait_ge(s_cp, 2 * NT)

            @block.tensor
            def _(pe):
                for t in range(NT):
                    pe.wait_ge(s_xr, t + 1)
                    for c in range(2):
                        mm = pe.transpose(T.ps[0:DC, t, c * P:(c + 1) * P], xr[:, t, c * DC:(c + 1) * DC], T.ident)
                    mm.then_inc(s_tp, 1)


def mixer_stage(nc, T, a):
    H, HD, DI, NS = 6, 64, 384, 8
    LANES = H * 16
    with ExitStack() as ctx:
        sb = lambda n, s: ctx.enter_context(nc.sbuf_tensor(f"a3_{n}", s, F32))
        vT = sb("vT", [P, 3, N_TOK])
        gate = sb("gate", [P, NT, DI])
        BT = T.xT[0:H * NS, 0, :]
        C_head = sb("C_head", [H * NS, H, N_TOK])
        u = sb("u", [P, NT, DI])
        response = sb("response", [P, NT, H, P])
        params = nc.dram_tensor("a3_params_out", (2 * H, N_TOK), F32, kind="Internal").ap()
        g_dram = nc.dram_tensor("a3_response_out", (LANES, SEQ, SEQ), F32, kind="Internal").ap()

        with ExitStack() as inner:
            sb2 = lambda n, s: inner.enter_context(nc.sbuf_tensor(f"a3p_{n}", s, F32))
            vpad = sb2("vpad", [P, 3, 16, SEQ + 3])
            taps = sb2("taps", [P, 3, 4, P])
            bc = sb2("bc", [P, NT, 96])
            sq = vpad[:, 0, 0:12, 0:SEQ]
            norm = sb2("norm", [P, NT, 12])
            rnorm = sb2("rnorm", [P, NT, 12])
            root = sb2("root", [P, NT, 12])
            par = sb2("par", [2 * H, N_TOK])
            pa, pd, A, d, s, nda, t0, t1, e0, e1 = (
                sb2(n, [LANES, SEQ]) for n in ("pa", "pd", "A", "d", "s", "nda", "t0", "t1", "e0", "e1"))
            rz = sb2("rz", [LANES, SEQ + 1, SEQ])
            G = [T.aT[0:LANES, k, :].rearrange("p (tau t) -> p tau t", t=SEQ) for k in range(2)]
            rx = sb2("rx", [LANES, SEQ])
            w = sb2("w", [LANES, SEQ])
            PARTS, STEPS = 4, SEQ // 4
            (s_c, s_vm, s_vp, s_pm, s_par, s_pd, s_gm, s_g, s_tap, s_cm, s_v, s_bm, s_bcc, s_n, s_r, s_bn, s_tp,
             s_ev, s_zero, s_um, s_u, s_in, s_ab, s_e, s_l, s_part, s_G, s_blank, s_root) = sems(
                nc, inner, "a3p", "chain", "v_products", "v_padded", "param_products", "params", "params_out",
                "gate_products", "gate", "taps", "conv_products", "v", "bc_products", "bc", "norms", "rnorm",
                "bc_normed", "transposed", "evacuated", "zeros", "u_transposed", "u", "params_in", "abs", "exps",
                "log", "part", "response", "response_blank", "roots")
            s_gd = sems(nc, inner, "a3o", *[f"response_out{k}" for k in range(PARTS)])
            s_rd = sems(nc, inner, "a3i", *[f"response_in{k}" for k in range(PARTS)])
            with nc.Block() as block:
                @block.tensor
                def _(pe):
                    pe.wait_ge(T.loaded["a3_in"], 16)
                    for half in range(2):
                        cols = slice(half * HALF, (half + 1) * HALF)
                        for c in range(2):
                            mm = pe.matmul(T.ps[0:2 * H, 6 + half, :], T.w["a3_in"][:, c, 2 * DI:], T.xT[0:DC, c, cols],
                                           start=(c == 0), stop=(c == 1))
                        mm.then_inc(s_pm, 1)
                    for j in range(3):
                        for half in range(2):
                            cols = slice(half * HALF, (half + 1) * HALF)
                            for c in range(2):
                                mm = pe.matmul(T.ps[:, 2 * j + half, :], T.w["a3_in"][:, c, DI + j * P:DI + (j + 1) * P],
                                               T.xT[0:DC, c, cols], start=(c == 0), stop=(c == 1))
                            mm.then_inc(s_vm, 1)
                    pe.wait_ge(s_tap, 12)
                    for b in range(6):
                        pe.wait_ge(s_vp, b + 1)
                        j, images = b // 2, slice((b % 2) * 8, (b % 2 + 1) * 8)
                        for k in range(4):
                            mm = pe.matmul(T.ps[:, b, :], taps[:, j, k, :], vpad[:, j, images, k:k + SEQ],
                                           start=(k == 0), stop=(k == 3))
                        mm.then_inc(s_cm, 1)
                    pe.wait_ge(T.loaded["a3_bc"], 16)
                    pe.wait_ge(s_v, 6)
                    for t in range(NT):
                        out = T.ps[:, t // 4, (t % 4) * 96:(t % 4 + 1) * 96]
                        for j in range(3):
                            mm = pe.matmul(out, vT[:, j, t * P:(t + 1) * P], T.w["a3_bc"][:, j, :],
                                           start=(j == 0), stop=(j == 2))
                    mm.then_inc(s_bm, 1)
                    pe.wait_ge(s_par, 2)
                    for t in range(NT):
                        if t >= 2:
                            pe.wait_ge(s_g, t - 1)
                        for c in range(2):
                            mm = pe.matmul(T.ps[:, 6 + t % 2, 0:DI], T.xT[0:DC, c, t * P:(t + 1) * P],
                                           T.w["a3_in"][:, c, 0:DI], start=(c == 0), stop=(c == 1))
                        mm.then_inc(s_gm, 1)
                    for t in range(NT):
                        if t >= 2:
                            pe.wait_ge(s_u, t - 1)
                        elif t == 0:
                            pe.wait_ge(s_g, NT)
                        for j in range(3):
                            mm = pe.transpose(T.ps[:, 6 + t % 2, j * P:(j + 1) * P], vT[:, j, t * P:(t + 1) * P],
                                              T.ident)
                        mm.then_inc(s_um, 1)
                    pe.wait_ge(s_bn, 1)
                    for t in range(NT):
                        for k in range(2):
                            mm = pe.transpose(T.ps[0:48, 2 + 2 * k + t // 4, (t % 4) * P:(t % 4 + 1) * P],
                                              bc[:, t, 48 * k:48 * k + 48], T.ident)
                    mm.then_inc(s_tp, 1)

                @block.scalar
                def _(act):
                    for half in range(2):
                        act.wait_ge(s_pm, half + 1)
                        act.activation(par[:, half * HALF:(half + 1) * HALF], T.ps[0:2 * H, 6 + half, :],
                                       ACT.Copy).then_inc(s_par, 1)
                    act.wait_ge(s_zero, 1)
                    for b in range(6):
                        act.wait_ge(s_vm, b + 1)
                        act.activation(vpad[:, b // 2, (b % 2) * 8:(b % 2 + 1) * 8, 3:],
                                       T.ps[:, b, :].rearrange("p (s n) -> p s n", n=SEQ),
                                       ACT.Copy).then_inc(s_vp, 1)
                    act.wait_ge(s_in, 32)
                    act.activation(e1[:, :], pd[:, :], ACT.Exp, scale=-1.0).then_inc(s_e, 1)
                    act.activation(t0[:, :], pa[:, :], ACT.Abs).then_inc(s_ab, 1)
                    act.wait_ge(s_ab, 1)
                    act.activation(e0[:, :], t0[:, :], ACT.Exp, scale=-1.0).then_inc(s_e, 1)
                    act.wait_ge(s_e, 2)
                    act.activation(t1[:, :], e0[:, :], ACT.Ln, bias=1.0).then_inc(s_l, 1)
                    for b in range(6):
                        act.wait_ge(s_cm, b + 1)
                        act.activation(vT[:, b // 2, (b % 2) * HALF:(b % 2 + 1) * HALF], T.ps[:, b, :],
                                       ACT.Silu).then_inc(s_v, 1)
                    act.wait_ge(s_bm, 1)
                    for i in range(2):
                        act.activation(bc[:, 4 * i:4 * i + 4, :],
                                       T.ps[:, i, 0:384].rearrange("p (t n) -> p t n", n=96),
                                       ACT.Copy).then_inc(s_bcc, 1)
                    for t in range(NT):
                        act.wait_ge(s_gm, t + 1)
                        act.activation(gate[:, t, :], T.ps[:, 6 + t % 2, 0:DI], ACT.Silu).then_inc(s_g, 1)
                    act.wait_ge(s_n, 1)
                    act.activation(root[:, :, :], norm[:, :, :], ACT.Sqrt).then_inc(s_root, 1)
                    for t in range(NT):
                        act.wait_ge(s_um, t + 1)
                        act.activation(u[:, t, :], T.ps[:, 6 + t % 2, 0:DI], ACT.Copy).then_inc(s_u, 1)
                    act.wait_ge(s_tp, 1)
                    for i in range(2):
                        cols = slice(i * HALF, (i + 1) * HALF)
                        act.activation(BT[:, cols], T.ps[0:48, 2 + i, :], ACT.Copy).then_inc(s_ev, 1)
                        for h in range(H):
                            act.activation(C_head[:, h, cols], T.ps[0:48, 4 + i, :], ACT.Copy,
                                           scale=T.consts[0:48, C_M8 + h:C_M8 + h + 1]).then_inc(s_ev, 1)
                    act.wait_ge(s_ev, 2 * (H + 1))

                @block.sync
                def _(sp):
                    sp.wait_ge(s_par, 2)
                    sp.dma_start(params, par[:, :]).then_inc(s_pd, 16)
                    sp.wait_ge(s_pd, 16)
                    lanes = lambda k: params[k * H:(k + 1) * H, :].rearrange("h (b t) -> (h b) t", t=SEQ)
                    sp.dma_start(pa[:, :], lanes(0)).then_inc(s_in, 16)
                    sp.dma_start(pd[:, :], lanes(1)).then_inc(s_in, 16)
                    blocks = g_dram.rearrange("(h i r) tau t -> h r tau i t", h=H, r=2)
                    sp.wait_ge(s_blank, 1)
                    for k in range(PARTS):
                        first = SEQ - (k + 1) * STEPS
                        steps = slice(first, first + STEPS)
                        sp.wait_ge(s_G, k + 1)
                        sp.dma_start(g_dram[:, steps, :], G[k % 2]).then_inc(s_gd[k], 16)
                        sp.wait_ge(s_gd[k], 16)
                        for h in range(H):
                            for r in range(2):
                                sp.dma_start(response[r * SEQ + first:r * SEQ + first + STEPS, :, h,
                                                      r * SEQ:(r + 1) * SEQ],
                                             blocks[h, r, steps]).then_inc(s_rd[k], 16)
                    for k in range(PARTS):
                        sp.wait_ge(s_rd[k], 16 * 2 * H)

                @block.gpsimd
                def _(pool):
                    pool.wait_ge(T.loaded["a3_conv"], 16)
                    for j in range(3):
                        for k in range(4):
                            pool.tensor_tensor(taps[:, j, k, :], T.ident,
                                               T.w["a3_conv"][:, j, k:k + 1].to_broadcast([P, P]),
                                               ALU.mult).then_inc(s_tap, 1)
                    pool.memset(response[:, :, :, :], 0.0).then_inc(s_blank, 1)

                    def scaled(k):
                        first = SEQ - (k + 1) * STEPS
                        pool.wait_ge(s_part, k + 1)
                        if k >= 2:
                            pool.wait_ge(s_gd[k - 2], 16)
                        pool.tensor_tensor(G[k % 2], rz[:, first:first + STEPS, :],
                                           d[:, first:first + STEPS].unsqueeze(2)
                                           .to_broadcast([LANES, STEPS, SEQ]), ALU.mult).then_inc(s_G, 1)

                    scaled(0)
                    scaled(1)
                    scaled(2)
                    pool.wait_ge(s_r, 1)
                    grouped = bc[:, :, :].rearrange("p t (g n) -> p (t g) n", n=NS)
                    pool.tensor_tensor(grouped, grouped,
                                       rnorm[:, :, :].rearrange("p t g -> p (t g)").unsqueeze(2)
                                       .to_broadcast([P, NT * 12, NS]), ALU.mult).then_inc(s_bn, 1)
                    scaled(3)

                @block.vector
                def _(dve):
                    chain = Chain(dve, s_c)
                    dve.memset(vpad[:, :, :, 0:3], 0.0).then_inc(s_zero, 1)
                    dve.memset(rz[:, :, :], 0.0)
                    chain(dve.memset(rx[:, :], 1.0))
                    dve.wait_ge(s_in, 32)
                    dve.wait_ge(s_e, 1)
                    chain(dve.tensor_scalar(d[:, :], e1[:, :], 1.0, None, ALU.add))
                    chain(dve.reciprocal(d[:, :], d[:, :]))
                    dve.wait_ge(s_l, 1)
                    chain(dve.scalar_tensor_tensor(A[:, :], pa[:, :], 0.0, t1[:, :], ALU.max, ALU.add))
                    chain(dve.scalar_tensor_tensor(nda[:, :], A[:, :], -1.0, d[:, :], ALU.mult, ALU.mult))
                    chain(dve.scalar_tensor_tensor(s[:, :], nda[:, :], -1.0, d[:, :], ALU.mult, ALU.mult))
                    chain(dve.tensor_scalar(s[:, :], s[:, :], 1.0, None, ALU.add))
                    chain(dve.reciprocal(s[:, :], s[:, :]))
                    for tau in range(SEQ - 1, -1, -1):
                        col = lambda x: x[:, tau:tau + 1]
                        chain(dve.scalar_tensor_tensor(w[:, tau:], rx[:, tau:], col(d), rz[:, tau + 1, tau:],
                                                       ALU.mult, ALU.add))
                        chain(dve.tensor_scalar(rz[:, tau, tau:], w[:, tau:], col(s), None, ALU.mult))
                        if tau % STEPS == 0:
                            dve.sem_inc(s_part, 1)
                        if tau:
                            chain(dve.scalar_tensor_tensor(rx[:, tau:], rz[:, tau, tau:], col(nda), rx[:, tau:],
                                                           ALU.mult, ALU.add))
                        if tau == STEPS // 2:
                            dve.wait_ge(s_root, 1)
                            dve.reciprocal(rnorm[:, :, :], root[:, :, :]).then_inc(s_r, 1)
                        if tau == STEPS + STEPS // 2:
                            dve.wait_ge(s_bcc, 2)
                            flat = bc[:, :, :].rearrange("p t n -> p (t n)").rearrange("p (a b) -> p a b", b=SEQ)
                            chain(dve.tensor_tensor(sq, flat, flat, ALU.mult))
                            chain(dve.tensor_reduce(norm[:, :, :].rearrange("p t g -> p (t g)")
                                                    .rearrange("p (a g) -> p a g", g=SEQ // NS),
                                                    sq.rearrange("p a (g n) -> p a g n", n=NS),
                                                    AX_X, ALU.add))
                            dve.tensor_scalar(norm[:, :, :], norm[:, :, :], 1e-12, None, ALU.add).then_inc(s_n, 1)

        with ExitStack() as inner:
            sb2 = lambda n, s: inner.enter_context(nc.sbuf_tensor(f"a3y_{n}", s, F32))
            mixT = sb2("mixT", [P, 2, H * P])
            skip = sb2("skip", [P, NT, DI])
            gated = sb2("gated", [P, 2, DI])
            gatedT = sb2("gatedT", [P, 2, DI])
            s_c, s_b, s_m, s_y, s_sk, s_gt, s_t, s_gT, s_o, s_x = sems(
                nc, inner, "a3y", "chain", "bc_products", "mix", "y_products", "skip", "gated", "transposed",
                "gatedT", "products", "x")
            with nc.Block() as block:
                @block.tensor
                def _(pe):
                    def cb(t):
                        if t >= 1:
                            pe.wait_ge(s_m, 2 * t)
                        for q in range(2):
                            mm = pe.matmul(T.ps[:, q, 0:3 * P], BT[:, t * P:(t + 1) * P],
                                           C_head[:, 3 * q:3 * q + 3, t * P:(t + 1) * P], start=True, stop=True)
                        mm.then_inc(s_b, 1)

                    pe.wait_ge(T.loaded["a3_out"], 16)
                    def y(t):
                        pe.wait_ge(s_m, 2 * (t + 1))
                        if t >= 2:
                            pe.wait_ge(s_gt, t - 1)
                        for h in range(H):
                            mm = pe.matmul(T.ps[:, 2 + t % 2, h * HD:(h + 1) * HD],
                                           mixT[:, t % 2, h * P:(h + 1) * P], u[:, t, h * HD:(h + 1) * HD],
                                           start=True, stop=True)
                        mm.then_inc(s_y, 1)

                    def turn(t):
                        pe.wait_ge(s_gt, t + 1)
                        if t >= 2:
                            pe.wait_ge(s_gT, t - 1)
                        for j in range(3):
                            mm = pe.transpose(T.ps[:, 4 + t % 2, j * P:(j + 1) * P],
                                              gated[:, t % 2, j * P:(j + 1) * P], T.ident)
                        mm.then_inc(s_t, 1)

                    def project(t):
                        pe.wait_ge(s_gT, t + 1)
                        if t >= 2:
                            pe.wait_ge(s_x, t - 1)
                        for j in range(3):
                            mm = pe.matmul(T.ps[:, 6 + t % 2, 0:D], gatedT[:, t % 2, j * P:(j + 1) * P],
                                           T.w["a3_out"][:, j, :], start=(j == 0), stop=(j == 2))
                        mm.then_inc(s_o, 1)

                    cb(0)
                    for t in range(NT + 2):
                        if t + 1 < NT:
                            cb(t + 1)
                        if t < NT:
                            y(t)
                        if 0 <= t - 1 < NT:
                            turn(t - 1)
                        if 0 <= t - 2:
                            project(t - 2)

                @block.gpsimd
                def _(pool):
                    pool.wait_ge(T.loaded["a3_skip"], 16)
                    for t in range(NT):
                        pool.tensor_tensor(skip[:, t, :], u[:, t, :], T.w["a3_skip"][:, :], ALU.mult).then_inc(s_sk, 1)

                @block.scalar
                def _(act):
                    for t in range(NT):
                        act.wait_ge(s_t, t + 1)
                        if t >= 2:
                            act.wait_ge(s_o, t - 1)
                        act.activation(gatedT[:, t % 2, :], T.ps[:, 4 + t % 2, 0:DI], ACT.Copy).then_inc(s_gT, 1)

                @block.vector
                def _(dve):
                    chain = Chain(dve, s_c)

                    def mix(t):
                        dve.wait_ge(s_b, t + 1)
                        if t >= 2:
                            dve.wait_ge(s_y, t - 1)
                        for q in range(2):
                            dve.tensor_tensor(mixT[:, t % 2, 3 * q * P:3 * (q + 1) * P], T.ps[:, q, 0:3 * P],
                                              response[:, t, 3 * q:3 * q + 3, :].rearrange("p h t -> p (h t)"),
                                              ALU.mult).then_inc(s_m, 1)

                    mix(0)
                    for t in range(NT + 2):
                        if t + 1 < NT:
                            mix(t + 1)
                        if t < NT:
                            dve.wait_ge(s_y, t + 1)
                            dve.wait_ge(s_sk, t + 1)
                            if t >= 2:
                                dve.wait_ge(s_t, t - 1)
                            chain(dve.tensor_tensor(gated[:, t % 2, :], T.ps[:, 2 + t % 2, 0:DI], skip[:, t, :],
                                                    ALU.add))
                            dve.tensor_tensor(gated[:, t % 2, :], gated[:, t % 2, :], gate[:, t, :],
                                              ALU.mult).then_inc(s_gt, 1)
                        if t >= 2:
                            dve.wait_ge(s_o, t - 1)
                            dve.tensor_tensor(T.xn[:, t - 2, :], T.ps[:, 6 + t % 2, 0:D], T.xn[:, t - 2, :],
                                              ALU.add).then_inc(s_x, 1)
                    dve.wait_ge(s_x, NT)

    rms_stage(nc, T, "x2", T.w["a3_norm2"])
    with ExitStack() as ctx:
        f1 = ctx.enter_context(nc.sbuf_tensor("a3f_f1", [P, 6, N_TOK], F32))
        s_f, s_g, s_o, s_hx, s_h = sems(nc, ctx, "a3f", "ff1", "gelu", "ff2", "h_x", "h")
        with nc.Block() as block:
            @block.tensor
            def _(pe):
                pe.wait_ge(T.loaded["a3_ff1"], 16)
                pe.wait_ge(T.loaded["a3_ff2"], 16)
                for n in range(12):
                    j, half = n // 2, n % 2
                    cols = slice(half * HALF, (half + 1) * HALF)
                    if n >= 4:
                        pe.wait_ge(s_g, n - 3)
                    pe.matmul(T.ps[:, n % 4, :], T.w["a3_ff1"][:, 0, j * P:(j + 1) * P], T.xT[:, 0, cols],
                              start=True, stop=False)
                    pe.matmul(T.ps[:, n % 4, :], T.w["a3_ff1"][0:DC, 1, j * P:(j + 1) * P], T.xT[0:DC, 1, cols],
                              start=False, stop=True).then_inc(s_f, 1)
                pe.wait_ge(s_g, 12)
                for t in range(NT):
                    if t >= 4:
                        pe.wait_ge(s_h, t - 3)
                    for j in range(6):
                        mm = pe.matmul(T.ps[:, 4 + t % 4, 0:D], f1[:, j, t * P:(t + 1) * P], T.w["a3_ff2"][:, j, :],
                                       start=(j == 0), stop=(j == 5))
                    mm.then_inc(s_o, 1)

            @block.scalar
            def _(act):
                for n in range(12):
                    act.wait_ge(s_f, n + 1)
                    act.activation(f1[:, n // 2, (n % 2) * HALF:(n % 2 + 1) * HALF], T.ps[:, n % 4, :],
                                   ACT.Gelu_apprx_tanh).then_inc(s_g, 1)

            @block.vector
            def _(dve):
                dve.wait_ge(T.loaded["a3_b2"], 16)
                dve.tensor_tensor(T.h[:, :, :], T.h[:, :, :], T.xn[:, :, :], ALU.add).then_inc(s_hx, 1)
                dve.wait_ge(s_hx, 1)
                dve.tensor_tensor(T.h[:, :, :], T.h[:, :, :], T.w["a3_b2"][:, :].unsqueeze(1).to_broadcast([P, NT, D]),
                                  ALU.add).then_inc(s_hx, 1)
                dve.wait_ge(s_hx, 2)
                for t in range(NT):
                    dve.wait_ge(s_o, t + 1)
                    dve.tensor_tensor(T.h[:, t, :], T.ps[:, 4 + t % 4, 0:D], T.h[:, t, :], ALU.add).then_inc(s_h, 1)
                dve.wait_ge(s_h, NT)


KNOTS, GRID = 16, 13.0 / 8.0


def kan_layer(nc, T, name, x, rounds, centres, weights, columns, products, finish):
    U_ = x.shape[1]
    by_scalar = lambda u: U_ == 4 and u == 3
    by_gpsimd = lambda u: U_ == 4 and u == 1
    AHEAD = 2
    with ExitStack() as ctx:
        sb = lambda n, s: ctx.enter_context(nc.sbuf_tensor(f"{name}_{n}", s, F32))
        v, near, far, near3, far3, basis = (sb(n, [P, U_, N_TOK])
                                            for n in ("v", "near", "far", "near3", "far3", "basis"))
        w = sb("w", [P, U_, columns])
        s_w = sems(nc, ctx, name, *[f"w{u}" for u in range(U_)])
        s_v, s_near, s_cut, s_sq, s_cube, s_basis, s_used, s_pool, s_waited = sems(
            nc, ctx, name, "v", "near", "cut", "squares", "cubes", "basis", "used", "pool_cube", "waited")

        def every_round(eng, body):
            body(0, True, False)
            with eng.Fori(1, rounds - 1) as i:
                body(i, False, False)
            body(rounds - 1, False, True)

        with nc.Block() as block:
            @block.sync
            def _(sp):
                def body(i, first, last):
                    for u in range(U_):
                        if not first:
                            sp.wait_ge(s_used, (i - 1) * U_ + u + 1)
                        sp.dma_start(w[:, u, :], weights[bass.ds(i * U_ + u, 1), :, :]
                                     .rearrange("a p n -> p (a n)")).then_inc(s_w[u], 16)
                every_round(sp, body)

            @block.scalar
            def _(act):
                def squares(i, u, first):
                    if by_scalar(u):
                        act.wait_ge(s_near, i + 1)
                    act.wait_ge(s_cut, i * U_ + u + 1)
                    if not first:
                        act.wait_ge(s_basis, (i - 1) * U_ + u + 1)
                    act.activation(near3[:, u, :], near[:, u, :], ACT.Square, scale=6.0 ** -0.5)
                    act.activation(far3[:, u, :], far[:, u, :], ACT.Square, scale=(4.0 / 6.0) ** 0.5
                                   ).then_inc(s_sq, 1)

                def distance(i, u, first):
                    if not first:
                        wait_alone(act, s_cut, (i - 1) * U_ + u + 1, s_waited)
                    act.activation(v[:, u, :], x[:, u, :], ACT.Abs, scale=GRID,
                                   bias=centres[:, bass.ds(i, 1)]).then_inc(s_v, 1)

                def body(i, first, last):
                    for u in range(U_):
                        squares(i, u, first)
                        if by_scalar(u + 1):
                            act.wait_ge(s_v, i * U_ + u + 2)
                            if not first:
                                act.wait_ge(s_cube, (i - 1) * U_ + u + 2)
                            act.activation(near[:, u + 1, :], v[:, u + 1, :], ACT.Relu, scale=-1.0, bias=2.0
                                           ).then_inc(s_near, 1)
                        if u + AHEAD < U_:
                            distance(i, u + AHEAD, first)
                        elif not last:
                            distance(i + 1, u + AHEAD - U_, False)
                for u in range(AHEAD):
                    distance(0, u, True)
                every_round(act, body)

            @block.vector
            def _(dve):
                def cut(i, u, first):
                    if not first:
                        dve.wait_ge(s_cube, (i - 1) * U_ + u + 1)
                        if by_gpsimd(u):
                            dve.wait_ge(s_pool, i)
                    dve.wait_ge(s_v, i * U_ + u + 1)
                    if not by_scalar(u):
                        dve.tensor_scalar(near[:, u, :], v[:, u, :], 2.0, -2.0, ALU.min, ALU.add)
                    dve.tensor_scalar(far[:, u, :], v[:, u, :], 1.0, -1.0, ALU.min, ALU.add).then_inc(s_cut, 1)

                def body(i, first, last):
                    for u in range(U_):
                        dve.wait_ge(s_sq, i * U_ + u + 1)
                        if not by_gpsimd(u):
                            dve.tensor_tensor(near3[:, u, :], near3[:, u, :], near[:, u, :], ALU.mult)
                        dve.tensor_tensor(far3[:, u, :], far3[:, u, :], far[:, u, :], ALU.mult).then_inc(s_cube, 1)
                        if u + AHEAD < U_:
                            cut(i, u + AHEAD, first)
                        elif not last:
                            cut(i + 1, u + AHEAD - U_, False)
                for u in range(AHEAD):
                    cut(0, u, True)
                every_round(dve, body)

            @block.gpsimd
            def _(pool):
                def body(i, first, last):
                    for u in range(U_):
                        if by_gpsimd(u):
                            pool.wait_ge(s_sq, i * U_ + u + 1)
                            pool.tensor_tensor(near3[:, u, :], near3[:, u, :], near[:, u, :], ALU.mult
                                               ).then_inc(s_pool, 1)
                            pool.wait_ge(s_pool, i + 1)
                        pool.wait_ge(s_cube, i * U_ + u + 1)
                        if not first:
                            pool.wait_ge(s_used, (i - 1) * U_ + u + 1)
                        pool.tensor_tensor(basis[:, u, :], far3[:, u, :], near3[:, u, :],
                                           ALU.add if by_scalar(u) else ALU.subtract).then_inc(s_basis, 1)
                every_round(pool, body)

            @block.tensor
            def _(pe):
                def body(i, first, last):
                    for u in range(U_):
                        pe.wait_ge(s_basis, i * U_ + u + 1)
                        pe.wait_ge(s_w[u], 16 * (i + 1))
                        products(pe, basis[:, u, :], w[:, u, :], first and u == 0, last and u == U_ - 1
                                 ).then_inc(s_used, 1)
                every_round(pe, body)

        finish()


def kan_stages(nc, T, a):
    HID, HC = 512, 4
    with ExitStack() as ctx:
        sb = lambda n, s: ctx.enter_context(nc.sbuf_tensor(f"kan_{n}", s, F32))
        hid = sb("hid", [P, HC, N_TOK])
        with ExitStack() as inner:
            x2 = inner.enter_context(nc.sbuf_tensor("kan_x2", [P, 3, N_TOK], F32))
            xd = inner.enter_context(nc.sbuf_tensor("kan_xd", [P, NT, 3, 2, 64], F32))
            s_d, s_tp, s_cp = sems(nc, inner, "kan0", "doubled", "transposed", "copied")
            with nc.Block() as block:
                @block.vector
                def _(dve):
                    for t in range(NT):
                        dve.tensor_copy(xd[:, t, :, :, :], T.xn[:, t, :].rearrange("p (c f) -> p c f", c=3)
                                        .unsqueeze(2).to_broadcast([P, 3, 2, 64])).then_inc(s_d, 1)

                @block.tensor
                def _(pe):
                    for t in range(NT):
                        pe.wait_ge(s_d, t + 1)
                        for c in range(3):
                            mm = pe.transpose(T.ps[:, t, c * P:(c + 1) * P],
                                              xd[:, t, c, :, :].rearrange("p a b -> p (a b)"), T.ident)
                        mm.then_inc(s_tp, 1)

                @block.scalar
                def _(act):
                    for t in range(NT):
                        act.wait_ge(s_tp, t + 1)
                        act.activation(x2[:, :, t * P:(t + 1) * P],
                                       T.ps[:, t, 0:3 * P].rearrange("p (c n) -> p c n", c=3),
                                       ACT.Copy).then_inc(s_cp, 1)
                    act.wait_ge(s_cp, NT)

            def products1(pe, basis, w, start, stop):
                for j in range(HC):
                    for half in range(2):
                        mm = pe.matmul(T.ps[:, 2 * j + half, :], w[:, j * P:(j + 1) * P],
                                       basis[:, half * HALF:(half + 1) * HALF], start=start, stop=stop)
                return mm

            def finish1():
                s_h, = sems(nc, inner, "kan1f", "hidden")
                with nc.Block() as block:
                    @block.scalar
                    def _(act):
                        for b in range(0, 8, 2):
                            act.activation(hid[:, b // 2, 0:HALF], T.ps[:, b, :], ACT.Copy).then_inc(s_h, 1)
                        act.wait_ge(s_h, 8)

                    @block.vector
                    def _(dve):
                        for b in range(1, 8, 2):
                            dve.tensor_copy(hid[:, b // 2, HALF:N_TOK], T.ps[:, b, :]).then_inc(s_h, 1)
                        dve.wait_ge(s_h, 8)

            kan_layer(nc, T, "kan1", x2, KNOTS // 2, T.consts[:, C_K1:C_K1 + KNOTS // 2], a["kan_w1"], HID,
                      products1, finish1)

        def products2(pe, basis, w, start, stop):
            for t in range(NT):
                mm = pe.matmul(T.ps[:, t, 0:D], basis[:, t * P:(t + 1) * P], w, start=start, stop=stop)
            return mm

        def finish2():
            s_h, = sems(nc, ctx, "kan2f", "h")
            with nc.Block() as block:
                @block.vector
                def _(dve):
                    for t in range(NT):
                        dve.tensor_tensor(T.h[:, t, :], T.ps[:, t, 0:D], T.h[:, t, :], ALU.add).then_inc(s_h, 1)
                    dve.wait_ge(s_h, NT)

        kan_layer(nc, T, "kan2", hid, KNOTS, T.consts[:, C_K2:C_K2 + KNOTS], a["kan_w2"], D, products2, finish2)


def tower(nc, a, out):
    with ExitStack() as ctx:
        T = Tower()
        T.w = {}
        sb = lambda n, s, dt=F32: ctx.enter_context(nc.sbuf_tensor(n, s, dt))
        consts = sb("consts", [P, C_N])
        T.consts = consts
        T.ident = consts[:, C_ID:C_ID + P]
        T.block_mask = consts[:, C_BLK:C_BLK + P]
        T.causal3 = consts[:, C_CAU:C_CAU + 3 * P]
        T.h = sb("h", [P, NT, D])
        T.xn = sb("xn", [P, NT, D])
        T.xT = sb("xT", [DC + 1, 2, N_TOK])
        T.aT = sb("aT", [DC + 1, 2, N_TOK])
        T.ones = sb("ones", [P, P])
        T.zeros = sb("zeros", [P, D])
        T.power = sb("power", [P, NT])
        T.ps = ctx.enter_context(nc.psum_tensor("ps", [P, 8, HALF], F32))
        loads = {"consts": (consts[:, :], a["consts"])}
        for name in WEIGHTS:
            src = a[name]
            t = sb(name, list(src.shape))
            T.w[name] = t
            full = t[:, :] if len(src.shape) == 2 else t[:, :, :] if len(src.shape) == 3 else t[:, :, :, :]
            loads[name] = (full, src)
        T.loaded = {n: ctx.enter_context(nc.semaphore(f"in_{n}")) for n in loads}
        T.s_cleared = ctx.enter_context(nc.semaphore("cleared"))
        T.m0, T.m1, T.m2 = Moe("m0", 16, 3, shared=True), Moe("m1", 16, 2), Moe("m2", 32, 2, renormalise=True, biased=False)
        for m in (T.m0, T.m1, T.m2):
            m.s_scattered, = sems(nc, ctx, m.name, "scattered")
            m.s_gathered = sems(nc, ctx, m.name, *[f"gathered{t}" for t in range(NT)])
            m.s_stored = sems(nc, ctx, m.name, *[f"stored{u}" for u in range(U)])
            if m.biased:
                m.gates = sb(f"{m.name}_gates", [P, NT, m.E])
            m.gate = sb(f"{m.name}_gate", [P, m.C, NT])
            m.slots = sb(f"{m.name}_slots", [P, m.C, NT], U32)
            m.expert_of = sb(f"{m.name}_expert_of", [1, m.tiles + 1], I32)
            m.slots_x = nc.dram_tensor(f"{m.name}_slots_x", (m.tiles * P, D), F32, kind="Internal").ap()
            m.slots_y = nc.dram_tensor(f"{m.name}_slots_y", (m.tiles * P, D), F32, kind="Internal").ap()
        stages = [
            lambda: tokens_stage(nc, T, a["patches"], loads, (T.m0, T.m1, T.m2)),
            lambda: (norm_stage(nc, T, "n0"), attention0_stage(nc, T)),
            lambda: (norm_stage(nc, T, "n1"), moe0(nc, T, a)),
            lambda: (norm_stage(nc, T, "n2"), attention1_stage(nc, T)),
            lambda: (norm_stage(nc, T, "n3"), moe1(nc, T, a)),
            lambda: (norm_stage(nc, T, "n4"), attention2_stage(nc, T, a)),
            lambda: (norm_stage(nc, T, "n5"), moe2(nc, T, a)),
            lambda: (norm_stage(nc, T, "n6", T.w["a3_norm1"]), mixer_stage(nc, T, a)),
            lambda: (norm_stage(nc, T, "n7"), kan_stages(nc, T, a)),
        ]
        for stage in stages:
            stage()
        s_out, = sems(nc, ctx, "end", "stored")
        with nc.Block() as block:
            @block.sync
            def _(sp):
                sp.dma_start(out.rearrange("(t p) d -> p t d", p=P), T.h[:, :, :]).then_inc(s_out, 16)
                sp.wait_ge(s_out, 16)
                sp.wait_ge(T.s_cleared, 96)
                for loaded in T.loaded.values():
                    sp.wait_ge(loaded, 16)


WEIGHTS = ["tok_w", "tok_b", "a0_w", "e0_gate", "e1_gate", "e2_gate", "a1_w", "a1_proj",
           "a2_fc1", "a2_convA", "a2_convB", "a2_qkv", "a2_proj", "a2_fc2", "a2_cols",
           "a3_in", "a3_conv", "a3_bc", "a3_skip", "a3_out", "a3_norm1", "a3_norm2", "a3_ff1", "a3_ff2", "a3_b2"]


def constants():
    import numpy as np
    c = np.zeros((P, C_N), np.float32)
    row = np.arange(P)
    c[:, C_ID:C_ID + P] = np.eye(P)
    for base, width, n in ((C_M16, 16, 6), (C_M24, 24, 4), (C_M8, 8, 6)):
        for j in range(n):
            c[:, base + j] = row // width == j
    same = row[:, None] // SEQ == row[None, :] // SEQ
    c[:, C_BLK:C_BLK + P] = np.where(same, 0.0, NEG)
    causal = np.where(same & (row[None, :] <= row[:, None]), 0.0, np.where(same, -1.0e10, NEG))
    c[:, C_CAU:C_CAU + 3 * P] = np.tile(causal, 3)
    c[:, C_LT:C_LT + P] = row[None, :] > row[:, None]
    c[:, C_IOTA:C_IOTA + P] = row[None, :]
    c[:, C_K1:C_K1 + 8] = 7.5 - (2 * np.arange(8)[None, :] + row[:, None] // 64)
    c[:, C_K2:C_K2 + 16] = 7.5 - np.arange(16)[None, :]
    return c


def neighbour_bias(rpb):
    import numpy as np
    rows, k = 16, 5
    start = lambda i, n: np.clip(i - k // 2, 0, n - k)
    out = np.full((P, 3, 4, 6, SEQ), NEG, np.float32)
    w = np.arange(SEQ)
    for kind, tile in enumerate((0, 1, NT - 1)):
        key_row0 = 2 * min(max(tile - 1, 0), NT - 3)
        for r in range(2):
            row = 2 * tile + r
            for key_row in range(start(row, rows), start(row, rows) + k):
                for b in range(k):
                    key = start(w, SEQ) + b
                    out[r * SEQ + w, kind, :, key_row - key_row0, key] = rpb[:, key_row - row + k - 1, key - w + k - 1].T
    return out.reshape(P, -1)


def lay_out(x):
    import numpy as np
    f = lambda n: np.asarray(x[n])

    def chunks(w, n):
        return np.ascontiguousarray(w.reshape(n, w.shape[0] // n, -1).transpose(1, 0, 2))

    def with_bias(w, b):
        out = np.zeros((DC + 1, 2, w.shape[1]), np.float32)
        out[0:DC] = chunks(w, 2)
        out[DC, 0] = b
        return out

    def rows(b):
        return np.ascontiguousarray(np.broadcast_to(b, (P, b.shape[0])))

    a = {"consts": constants()}
    p = f("x").reshape(16, 3, 8, 16, 8, 16).transpose(0, 1, 2, 4, 3, 5).reshape(N_TOK, 768)
    a["patches"] = chunks(p.T, 6)
    a["tok_w"] = chunks(f("L0_tok_weight").T, 6)
    a["tok_b"] = rows(f("L0_tok_bias"))
    a["a0_w"] = with_bias(f("L0_attn_W_qkv"), f("L0_attn_b_qkv"))
    a["a1_w"] = with_bias(f("L1_attn_Wqkv_w")[:D].T, f("L1_attn_Wqkv_b")[:D])
    a["a1_proj"] = with_bias(f("L1_attn_Wproj_w").T, f("L1_attn_Wproj_b"))
    a["a2_fc1"] = with_bias(f("L2_attn_fc1_w").T, f("L2_attn_fc1_b"))
    a["a2_convA"] = np.ascontiguousarray(f("L2_attn_convA_w").T)
    a["a2_convB"] = np.ascontiguousarray(f("L2_attn_convB_w").T)
    a["a2_qkv"] = np.concatenate([f("L2_attn_qkv_w").T, f("L2_attn_qkv_b")[None]])
    a["a2_proj"] = np.ascontiguousarray(f("L2_attn_proj_w").T)
    a["a2_fc2"] = np.concatenate([f("L2_attn_fc2_w").T, f("L2_attn_fc2_b")[None]])
    a["a2_cols"] = np.zeros((DC, 3), np.float32)
    a["a2_cols"][0:64, 0] = f("L2_attn_convA_b")
    a["a2_cols"][:, 1] = f("L2_attn_convB_b")
    a["a2_cols"][:, 2] = f("L2_attn_proj_b")
    a["a2_bias"] = neighbour_bias(f("L2_attn_rpb"))

    def experts_with_bias(w, b, b2=None):
        e, _, n = w.shape
        out = np.zeros((e, DC + 1, 2, n), np.float32)
        out[:, 0:DC] = w.reshape(e, 2, DC, n).transpose(0, 2, 1, 3)
        out[:, DC, 0] = b
        if b2 is not None:
            out[:, DC, 1, 0:D] = b2
        return out.reshape(e, DC + 1, 2 * n)

    def expert_chunks(w):
        e, k, n = w.shape
        return np.ascontiguousarray(w.reshape(e, k // P, P, n).transpose(0, 2, 1, 3).reshape(e, P, -1))

    a["e0_gate"] = with_bias(f("L0_ffn_gate_w"), f("L0_ffn_gate_b"))
    a["e1_gate"] = with_bias(f("L1_ffn_Wr").T, np.zeros(16, np.float32))
    a["e2_gate"] = with_bias(f("L2_ffn_gate_w").T, np.zeros(32, np.float32))
    a["e0_w1"] = experts_with_bias(f("L0_ffn_fc1_w"), f("L0_ffn_fc1_b"), f("L0_ffn_fc2_b"))
    a["e0_w2"] = np.concatenate([expert_chunks(f("L0_ffn_fc2_w")), expert_chunks(f("L0_ffn_ln_w")[:, :, None]),
                                 expert_chunks(f("L0_ffn_ln_b")[:, :, None])], axis=2)
    a["e1_w1"] = experts_with_bias(f("L1_ffn_W1"), f("L1_ffn_b1"), f("L1_ffn_b2"))
    a["e1_w2"] = expert_chunks(f("L1_ffn_W2"))
    a["e2_w1"] = experts_with_bias(f("L2_ffn_W1"), f("L2_ffn_b1"))
    a["e2_w23"] = np.concatenate([expert_chunks(f("L2_ffn_W2")), expert_chunks(f("L2_ffn_W3")),
                                  expert_chunks(f("L2_ffn_b2")[:, :, None])], axis=2)
    a["e2_wl"] = np.zeros((32, 65, D + 1), np.float32)
    a["e2_wl"][:, 0:64, 0:D] = f("L2_ffn_Wl")
    a["e2_wl"][:, 64, 0:D] = f("L2_ffn_bl")
    a["e2_wl"][:, 0:64, D] = f("L2_ffn_b3")
    w_in = f("L3_attn_w_in")
    w_in = np.concatenate([w_in[:, :768], w_in[:, 768::2], w_in[:, 769::2]], axis=1)
    a["a3_in"] = chunks(w_in, 2)
    a["a3_conv"] = chunks(f("L3_attn_conv_w"), 3)
    w_bc = f("L3_attn_w_bc").reshape(384, 6, 2, 8).transpose(0, 2, 1, 3).reshape(384, 96)
    a["a3_bc"] = chunks(w_bc, 3)
    a["a3_skip"] = rows(np.repeat(f("L3_attn_D_skip"), 64))
    a["a3_out"] = chunks(f("L3_attn_w_out"), 3)
    a["a3_norm1"] = np.ascontiguousarray(f("L3_attn_norm1_w").reshape(2, DC).T)
    a["a3_norm2"] = np.ascontiguousarray(f("L3_attn_norm2_w").reshape(2, DC).T)
    a["a3_ff1"] = with_bias(f("L3_attn_ff_w1"), f("L3_attn_ff_b1"))
    a["a3_ff2"] = chunks(f("L3_attn_ff_w2"), 6)
    a["a3_b2"] = rows(f("L3_attn_ff_b2"))
    a["kan_w1"] = np.ascontiguousarray(f("L3_ffn_w1").reshape(512, 3, 64, 8, 2).transpose(3, 1, 4, 2, 0)
                                       .reshape(24, P, 512))
    a["kan_w2"] = np.ascontiguousarray(f("L3_ffn_w2").reshape(D, 4, P, 16).transpose(3, 1, 2, 0).reshape(64, P, D))
    return a


def kernel(**inputs):
    import numpy as np
    import concourse.bacc as bacc
    from concourse.bass_utils import run_bass_kernel_spmd

    nc = bacc.Bacc("TRN2", target_bir_lowering=False, num_devices=1)
    arrays = {f"in_{name}": np.ascontiguousarray(x) for name, x in lay_out(inputs).items()}
    args = {name[3:]: nc.dram_tensor(name, x.shape, mybir.dt.from_np(x.dtype), kind="ExternalInput").ap()
            for name, x in arrays.items()}
    out = nc.dram_tensor("out", (N_TOK, D), F32, kind="ExternalOutput").ap()
    tower(nc, args, out)
    result = run_bass_kernel_spmd(nc, [arrays], core_ids=[0]).results[0]["out"]
    return result.reshape(16, SEQ, D)
```

```python
from contextlib import ExitStack

import concourse.bass as bass
from concourse import mybir

F32 = mybir.dt.float32
I32 = mybir.dt.int32
U32 = mybir.dt.uint32
ALU = mybir.AluOpType
ACT = mybir.ActivationFunctionType
AX_X = mybir.AxisListType.X

P = 128
D = 192
DC = 96
N_TOK = 1024
NT = N_TOK // P
HALF = 512
SEQ = 64
NEG = -1.0e30

C_ID = 0
C_M16 = C_ID + P
C_M24 = C_M16 + 6
C_M8 = C_M24 + 4
C_BLK = C_M8 + 6
C_CAU = C_BLK + P
C_LT = C_CAU + 3 * P
C_IOTA = C_LT + P
C_K1 = C_IOTA + P
C_K2 = C_K1 + 8
C_N = C_K2 + 16


class Chain:

    def __init__(self, eng, sem):
        self.eng, self.sem, self.n, self.base = eng, sem, 0, 0

    def __call__(self, *instructions):
        for ins in instructions:
            ins.then_inc(self.sem, 1)
            self.n += 1
        self.eng.wait_ge(self.sem, self.base + self.n)


class Tower:
    pass


def sems(nc, ctx, prefix, *names):
    handles = [ctx.enter_context(nc.semaphore(f"{prefix}_{n}")) for n in names]

    def clear():
        for handle in handles:
            nc.gpsimd.sem_clear(handle)

    if prefix not in ("m0", "m1", "m2"):
        ctx.callback(clear)
    return handles


def wait_alone(eng, sem, value, waited):
    eng.wait_ge(sem, value)
    eng.sem_inc(waited, 1)


def tokens_stage(nc, T, patches, loads):
    with ExitStack() as ctx:
        xs = ctx.enter_context(nc.sbuf_tensor("tok_x", [P, 6, N_TOK], F32))
        s_x = sems(nc, ctx, "tok", *[f"patches{k}" for k in range(6)])
        s_mm, s_h, s_z = sems(nc, ctx, "tok", "products", "h", "zeros")
        norm = Norm(nc, T, ctx, "n0", lambda t: (t, 2 * P))
        with nc.Block() as block:
            @block.sync
            def _(sp):
                sp.dma_start(T.w["tok_w"][:, :, :], loads["tok_w"][1]).then_inc(T.loaded["tok_w"], 16)
                for k in range(1, 6, 2):
                    sp.dma_start(xs[:, k, :], patches[:, k, :]).then_inc(s_x[k], 16)
                for name, (dst, src) in loads.items():
                    if name != "tok_w":
                        sp.dma_start(dst, src).then_inc(T.loaded[name], 16)

            @block.scalar
            def _(act):
                for k in range(0, 6, 2):
                    act.dma_start(xs[:, k, :], patches[:, k, :]).then_inc(s_x[k], 16)
                act.wait_ge(s_z, 1)
                for name in ("tok_b", "consts", "a0_w"):
                    act.wait_ge(T.loaded[name], 16)
                for slots in (T.slots_x, T.slots_y):
                    act.dma_start(slots.rearrange("(n p) d -> p n d", p=P),
                                  T.zeros[:, :].unsqueeze(1).to_broadcast([P, slots.shape[0] // P, D])
                                  ).then_inc(T.s_cleared, 16)
                norm.act(act)

            @block.gpsimd
            def _(pool):
                for t in range(NT):
                    norm.pool(pool, t)

            @block.tensor
            def _(pe):
                pe.wait_ge(T.loaded["tok_w"], 16)
                for k in range(6):
                    pe.wait_ge(s_x[k], 16)
                    for t in range(NT):
                        mm = pe.matmul(T.ps[:, t, 0:D], xs[:, k, t * P:(t + 1) * P], T.w["tok_w"][:, k, :],
                                       start=(k == 0), stop=(k == 5))
                        if k == 5:
                            mm.then_inc(s_mm, 1)
                pe.wait_ge(T.loaded["consts"], 16)
                for t in range(NT):
                    norm.pe(pe, t)
                norm.pe_end(pe)

            @block.vector
            def _(dve):
                dve.memset(T.zeros[:, :], 0.0).then_inc(s_z, 1)
                dve.memset(T.ones[:, :], 1.0)
                dve.memset(T.power[:, :], -0.5)
                norm.eng = dve
                dve.memset(T.xT[DC:DC + 1, 0, :], 1.0)
                dve.memset(T.aT[DC:DC + 1, 0, :], 1.0)
                dve.wait_ge(T.loaded["tok_b"], 16)
                for t in range(NT):
                    dve.wait_ge(s_mm, t + 1)
                    dve.tensor_tensor(T.h[:, t, :], T.ps[:, t, 0:D], T.w["tok_b"][:, :], ALU.add).then_inc(s_h, 1)
                    dve.wait_ge(s_h, t + 1)
                    norm.dve(t)
                norm.dve_end()


class Norm:

    def __init__(self, nc, T, ctx, name, place, reuse=NT, rms_weight=None, route=None, doubled=False):
        self.T, self.place, self.reuse, self.weight, self.route = T, place, reuse, rms_weight, route
        self.doubled = ctx.enter_context(nc.sbuf_tensor(f"{name}_xd", [P, NT, 3, 2, 64], F32)) if doubled else None
        sb = lambda n, s: ctx.enter_context(nc.sbuf_tensor(f"{name}_{n}", s, F32))
        self.stats, self.mv, self.var, self.rstd = sb("stats", [P, NT, 6]), sb("mv", [P, NT, 2]), sb("var", [P, NT]), \
            sb("rstd", [P, NT])
        self.s_st, self.s_mv, self.s_var, self.s_rstd, self.s_xn, self.s_tp, self.s_cp = sems(
            nc, ctx, name, "stats", "moments", "variance", "rstd", "xn", "transposed", "copied")
        if rms_weight is not None:
            self.ms, self.rrms, self.xr = sb("ms", [P, NT]), sb("rrms", [P, NT]), sb("xr", [P, NT, D])
            self.s_sq, self.s_ms, self.s_rrms, self.s_xr = sems(
                nc, ctx, name, "squares", "mean_square", "rrms", "xr")

    def dve(self, t):
        self.eng.bn_stats(self.stats[:, t, :], self.T.h[:, t, :]).then_inc(self.s_st, 1)
        if t >= 1:
            self._moments(t - 1)
        if t >= 3:
            self._normalise(t - 3)
        if self.weight is not None and t >= 5:
            self._scale(t - 5)

    def dve_end(self):
        self._moments(NT - 1)
        for t in range(NT - 3, NT):
            self._normalise(t)
        if self.weight is not None:
            for t in range(NT - 5, NT):
                self._scale(t)
            self.eng.wait_ge(self.s_xr, NT)
        self.eng.wait_ge(self.s_xn, NT)

    def _moments(self, t):
        self.eng.wait_ge(self.s_st, t + 1)
        self.eng.bn_aggr(self.mv[:, t, :], self.stats[:, t, :]).then_inc(self.s_mv, 1)
        self.eng.wait_ge(self.s_mv, t + 1)
        self.eng.tensor_scalar(self.var[:, t:t + 1], self.mv[:, t, 1:2], 1e-5, None, ALU.add).then_inc(self.s_var, 1)

    def _normalise(self, t):
        T, dve = self.T, self.eng
        dve.wait_ge(self.s_rstd, t + 1)
        if self.weight is not None:
            dve.scalar_tensor_tensor(self.ms[:, t:t + 1], self.rstd[:, t:t + 1], self.rstd[:, t:t + 1],
                                     self.mv[:, t, 1:2], ALU.mult, ALU.mult).then_inc(self.s_sq, 1)
        if self.doubled is not None:
            dve.tensor_scalar(self.doubled[:, t, :, :, :],
                              T.h[:, t, :].rearrange("p (c f) -> p c f", c=3).unsqueeze(2).to_broadcast([P, 3, 2, 64]),
                              self.mv[:, t, 0:1], self.rstd[:, t:t + 1], ALU.subtract, ALU.mult).then_inc(self.s_xn, 1)
            return
        dve.tensor_scalar(T.xn[:, t, :], T.h[:, t, :], self.mv[:, t, 0:1], self.rstd[:, t:t + 1],
                          ALU.subtract, ALU.mult).then_inc(self.s_xn, 1)
        if self.weight is not None:
            dve.wait_ge(self.s_sq, t + 1)
            dve.tensor_scalar(self.ms[:, t:t + 1], self.ms[:, t:t + 1], 1e-6, None, ALU.add).then_inc(self.s_ms, 1)

    def _scale(self, t):
        self.eng.wait_ge(self.s_xn, t + 1)
        self.eng.wait_ge(self.s_rrms, t + 1)
        self.eng.tensor_scalar(self.xr[:, t, :], self.T.xn[:, t, :], self.rrms[:, t:t + 1], None,
                               ALU.mult).then_inc(self.s_xr, 1)

    def pool(self, pool, t):
        power = self.T.power[:, 0:1]
        pool.wait_ge(self.s_var, t + 1)
        pool.tensor_tensor(self.rstd[:, t:t + 1], self.var[:, t:t + 1], power, ALU.pow).then_inc(self.s_rstd, 1)

    def pool_rms(self, pool, t):
        power = self.T.power[:, 0:1]
        if self.weight is not None:
            pool.wait_ge(self.s_ms, t + 1)
            pool.tensor_tensor(self.rrms[:, t:t + 1], self.ms[:, t:t + 1], power, ALU.pow).then_inc(self.s_rrms, 1)

    def pe(self, pe, t):
        T, (bank, col) = self.T, self.place(t)
        pe.wait_ge(self.s_xn if self.weight is None else self.s_xr, t + 1)
        if t >= self.reuse:
            pe.wait_ge(self.s_cp, t - self.reuse + 1)
        if self.doubled is not None:
            for c in range(3):
                mm = pe.transpose(T.ps[:, bank, col + c * P:col + (c + 1) * P],
                                  self.doubled[:, t, c, :, :].rearrange("p a b -> p (a b)"), T.ident)
            mm.then_inc(self.s_tp, 1)
            return
        src = T.xn if self.weight is None else self.xr
        for c in range(2):
            mm = pe.transpose(T.ps[0:DC, bank, col + c * P:col + (c + 1) * P], src[:, t, c * DC:(c + 1) * DC], T.ident)
        mm.then_inc(self.s_tp, 1)
        if self.route and t >= 2:
            self._logits(pe, t - 2)

    def pe_end(self, pe):
        if self.route:
            self._logits(pe, NT - 2)
            self._logits(pe, NT - 1)

    def _logits(self, pe, t):
        T, m = self.T, self.route
        if t == 0:
            pe.wait_ge(T.loaded[m.gate_w], 16)
        pe.wait_ge(self.s_cp, t + 1)
        w, out = T.w[m.gate_w], T.ps[:, m.logit_bank, t * m.E:(t + 1) * m.E]
        pe.matmul(out, T.xT[:, 0, t * P:(t + 1) * P], w[:, 0, :], start=True, stop=False)
        pe.matmul(out, T.xT[0:DC, 1, t * P:(t + 1) * P], w[0:DC, 1, :], start=False, stop=True)

    def act(self, act):
        T = self.T
        if self.weight is not None:
            act.wait_ge(T.loaded["a3_norm1"], 16)
            act.wait_ge(T.loaded["a3_norm2"], 16)
        for t in range(NT):
            bank, col = self.place(t)
            act.wait_ge(self.s_tp, t + 1)
            if self.doubled is not None:
                act.activation(T.x2[:, :, t * P:(t + 1) * P],
                               T.ps[:, bank, col:col + 3 * P].rearrange("p (c n) -> p c n", c=3),
                               ACT.Copy).then_inc(self.s_cp, 1)
                continue
            if self.weight is None:
                act.activation(T.xT[0:DC, :, t * P:(t + 1) * P],
                               T.ps[0:DC, bank, col:col + 2 * P].rearrange("p (c n) -> p c n", c=2),
                               ACT.Copy).then_inc(self.s_cp, 1)
                continue
            act.activation(T.xT[0:DC, 0, t * P:(t + 1) * P], T.ps[0:DC, bank, col:col + P], ACT.Copy,
                           scale=self.weight[:, 0:1])
            act.activation(T.xT[0:DC, 1, t * P:(t + 1) * P], T.ps[0:DC, bank, col + P:col + 2 * P], ACT.Copy,
                           scale=self.weight[:, 1:2]).then_inc(self.s_cp, 1)
        act.wait_ge(self.s_cp, NT)


def attention0_stage(nc, T):
    scale = float(D) ** -0.5
    with ExitStack() as ctx:
        sb = lambda n, s: ctx.enter_context(nc.sbuf_tensor(f"a0_{n}", s, F32))
        qk = sb("qk", [DC, 4, N_TOK])
        v = sb("v", [P, NT, D])
        logit = sb("logit", [P, NT, P])
        prob = sb("prob", [P, NT, P])
        probT = sb("probT", [P, NT, P])
        top = sb("top", [P, NT])
        total = sb("total", [P, NT])
        inv = sb("inv", [P, NT])
        s_c, s_qkmm, s_qk, s_vmm, s_v, s_smm, s_l, s_e, s_t, s_pT, s_o, s_h = sems(
            nc, ctx, "a0", "chain", "qk_products", "qk", "v_products", "v", "scores", "logits", "exps",
            "transposed", "probT", "contexts", "h")
        norm = Norm(nc, T, ctx, "n1", lambda t: (t, 0), route=T.m0)
        with nc.Block() as block:
            @block.tensor
            def _(pe):
                pe.wait_ge(T.loaded["a0_w"], 16)
                for o in range(4):
                    for half in range(2):
                        cols = slice(half * HALF, (half + 1) * HALF)
                        pe.matmul(T.ps[0:DC, 2 * o + half, :], T.w["a0_w"][:, 0, o * DC:(o + 1) * DC],
                                  T.xT[:, 0, cols], start=True, stop=False)
                        pe.matmul(T.ps[0:DC, 2 * o + half, :], T.w["a0_w"][0:DC, 1, o * DC:(o + 1) * DC],
                                  T.xT[0:DC, 1, cols], start=False, stop=True).then_inc(s_qkmm, 1)
                for t in range(NT):
                    pe.wait_ge(s_qk, t + 1)
                    pe.matmul(T.ps[:, t, 0:D], T.xT[:, 0, t * P:(t + 1) * P], T.w["a0_w"][:, 0, 2 * D:3 * D],
                              start=True, stop=False)
                    pe.matmul(T.ps[:, t, 0:D], T.xT[0:DC, 1, t * P:(t + 1) * P], T.w["a0_w"][0:DC, 1, 2 * D:3 * D],
                              start=False, stop=True).then_inc(s_vmm, 1)
                for t in range(NT):
                    pe.wait_ge(s_v, t + 1)
                    for c in range(2):
                        mm = pe.matmul(T.ps[:, t, 0:P], qk[:, c, t * P:(t + 1) * P],
                                       qk[:, 2 + c, t * P:(t + 1) * P], start=(c == 0), stop=(c == 1))
                    mm.then_inc(s_smm, 1)
                for t in range(NT):
                    pe.wait_ge(s_e, t + 1)
                    pe.transpose(T.ps[:, t, P:2 * P], prob[:, t, :], T.ident).then_inc(s_t, 1)
                for t in range(NT):
                    pe.wait_ge(s_pT, t + 1)
                    pe.matmul(T.ps[:, t, 2 * P:2 * P + D], probT[:, t, :], v[:, t, :],
                              start=True, stop=True).then_inc(s_o, 1)
                for t in range(NT):
                    norm.pe(pe, t)
                norm.pe_end(pe)

            @block.gpsimd
            def _(pool):
                for t in range(NT):
                    norm.pool(pool, t)

            @block.scalar
            def _(act):
                for b in range(8):
                    act.wait_ge(s_qkmm, b + 1)
                    act.activation(qk[:, b // 2, (b % 2) * HALF:(b % 2 + 1) * HALF], T.ps[0:DC, b, :],
                                   ACT.Copy).then_inc(s_qk, 1)
                for t in range(NT):
                    act.wait_ge(s_l, t + 1)
                    act.activation(prob[:, t, :], logit[:, t, :], ACT.Exp, bias=top[:, t:t + 1],
                                   accum_out=total[:, t:t + 1]).then_inc(s_e, 1)
                for t in range(NT):
                    act.wait_ge(s_t, t + 1)
                    act.activation(probT[:, t, :], T.ps[:, t, P:2 * P], ACT.Copy).then_inc(s_pT, 1)
                norm.act(act)

            @block.vector
            def _(dve):
                chain = Chain(dve, s_c)
                norm.eng = dve
                for t in range(NT):
                    dve.wait_ge(s_vmm, t + 1)
                    dve.tensor_copy(v[:, t, :], T.ps[:, t, 0:D]).then_inc(s_v, 1)
                for t in range(NT):
                    dve.wait_ge(s_smm, t + 1)
                    chain(dve.scalar_tensor_tensor(logit[:, t, :], T.ps[:, t, 0:P], scale, T.block_mask,
                                                   ALU.mult, ALU.add))
                    dve.tensor_reduce(top[:, t:t + 1], logit[:, t, :], AX_X, ALU.max,
                                      negate=True).then_inc(s_l, 1)
                dve.wait_ge(s_e, NT)
                chain(dve.reciprocal(inv[:, :], total[:, :]))
                for t in range(NT):
                    dve.wait_ge(s_o, t + 1)
                    dve.scalar_tensor_tensor(T.h[:, t, :], T.ps[:, t, 2 * P:2 * P + D], inv[:, t:t + 1],
                                             T.h[:, t, :], ALU.mult, ALU.add).then_inc(s_h, 1)
                    dve.wait_ge(s_h, t + 1)
                    norm.dve(t)
                norm.dve_end()
def windowed_attention(nc, T, name, scores, scale, bias, heads, width, v, first_key_tile, ctxs):
    blocks = 12 // heads
    W = 384
    with ExitStack() as ctx:
        sb = lambda n, s: ctx.enter_context(nc.sbuf_tensor(f"{name}_{n}", s, F32))
        logit = sb("logit", [P, 2, 4, W])
        shifted = sb("shifted", [P, 2, 4 * W])
        prob = sb("prob", [P, 2, 12, P])
        probT = sb("probT", [P, 2, 12 * P])
        top = sb("top", [P, NT, heads])
        inv = sb("inv", [P, NT, heads])
        s_c, s_s, s_l, s_m, s_sh, s_e, s_t, s_pT, s_o, s_a = sems(
            nc, ctx, name, "chain", "scores", "logits", "maxima", "shifted", "exps", "transposed", "probT",
            "products", "contexts")
        with nc.Block() as block:
            @block.tensor
            def _(pe):
                def score(t):
                    if t:
                        pe.wait_ge(s_l, t)
                    for g in range(4):
                        lhsT, rhs = scores(t, g)
                        mm = pe.matmul(T.ps[:, g, 0:W], lhsT, rhs, start=True, stop=True)
                    mm.then_inc(s_s, 1)

                def turn(t):
                    pe.wait_ge(s_e, t + 1)
                    if t:
                        pe.wait_ge(s_pT, 3 * t)
                    for b in range(12):
                        mm = pe.transpose(T.ps[:, 4 + b // 4, (b % 4) * P:(b % 4 + 1) * P],
                                          prob[:, t % 2, b, :], T.ident)
                        if b % 4 == 3:
                            mm.then_inc(s_t, 1)

                def product(t):
                    if t:
                        pe.wait_ge(s_a, t)
                    pe.wait_ge(s_pT, 3 * (t + 1))
                    for n in range(heads):
                        for i in range(blocks):
                            b = n * blocks + i
                            mm = pe.matmul(T.ps[:, 7, n * (width + 1):(n + 1) * (width + 1)],
                                           probT[:, t % 2, b * P:(b + 1) * P],
                                           v[:, first_key_tile(t) + i, n, :],
                                           start=(i == 0), stop=(i == blocks - 1))
                    mm.then_inc(s_o, 1)

                score(0)
                score(1)
                for t in range(NT + 1):
                    if t + 2 < NT:
                        score(t + 2)
                    if t < NT:
                        turn(t)
                    if t:
                        product(t - 1)

            @block.vector
            def _(dve):
                chain = Chain(dve, s_c)

                def context(t):
                    dve.wait_ge(s_o, t + 1)
                    o = T.ps[:, 7, 0:heads * (width + 1)].rearrange("p (h d) -> p h d", h=heads)
                    chain(dve.reciprocal(inv[:, t, :], o[:, :, width]))
                    dve.tensor_tensor(ctxs[:, t, :].rearrange("p (h d) -> p h d", h=heads), o[:, :, 0:width],
                                      inv[:, t, :].unsqueeze(2).to_broadcast([P, heads, width]),
                                      ALU.mult).then_inc(s_a, 1)

                for t in range(NT):
                    dve.wait_ge(s_s, t + 1)
                    if t >= 2:
                        dve.wait_ge(s_sh, t - 1)
                    dve.scalar_tensor_tensor(logit[:, t % 2, :, :], T.ps[:, 0:4, 0:W], scale, bias(t),
                                             ALU.mult, ALU.add).then_inc(s_l, 1)
                    dve.wait_ge(s_l, t + 1)
                    dve.tensor_reduce(top[:, t, :],
                                      logit[:, t % 2, :, :].rearrange("p g k -> p (g k)")
                                      .rearrange("p (h k) -> p h k", h=heads), AX_X, ALU.max).then_inc(s_m, 1)
                    if t >= 3:
                        context(t - 3)
                for t in range(NT - 3, NT):
                    context(t)
                dve.wait_ge(s_a, NT)

            @block.gpsimd
            def _(pool):
                for t in range(NT):
                    pool.wait_ge(s_m, t + 1)
                    if t >= 2:
                        pool.wait_ge(s_e, t - 1)
                    pool.tensor_tensor(shifted[:, t % 2, :].rearrange("p (h k) -> p h k", h=heads),
                                       logit[:, t % 2, :, :].rearrange("p g k -> p (g k)")
                                       .rearrange("p (h k) -> p h k", h=heads),
                                       top[:, t, :].unsqueeze(2).to_broadcast([P, heads, 4 * W // heads]),
                                       ALU.subtract).then_inc(s_sh, 1)

            @block.scalar
            def _(act):
                def exps(t):
                    act.wait_ge(s_sh, t + 1)
                    if t >= 2:
                        act.wait_ge(s_t, 3 * (t - 1))
                    act.activation(prob[:, t % 2, :, :].rearrange("p b k -> p (b k)"), shifted[:, t % 2, :],
                                   ACT.Exp).then_inc(s_e, 1)

                exps(0)
                for t in range(NT):
                    if t + 1 < NT:
                        exps(t + 1)
                    if t >= 2:
                        act.wait_ge(s_o, t - 1)
                    for q in range(3):
                        act.wait_ge(s_t, 3 * t + q + 1)
                        act.activation(probT[:, t % 2, q * HALF:(q + 1) * HALF], T.ps[:, 4 + q, :],
                                       ACT.Copy).then_inc(s_pT, 1)


def attention1_stage(nc, T):
    H, W = 12, 16
    with ExitStack() as ctx:
        sb = lambda n, s: ctx.enter_context(nc.sbuf_tensor(f"a1_{n}", s, F32))
        qT = sb("qT", [DC, 2, N_TOK])
        q_head = sb("q_head", [DC, 2, 6, N_TOK])
        v = sb("v", [P, NT, H, W + 1])
        ctxs = sb("ctxs", [P, NT, D])
        s_qmm, s_q, s_vmm, s_v, s_one, s_qh = sems(nc, ctx, "a1p", "q_products", "q", "v_products", "v", "ones",
                                                   "q_heads")
        with nc.Block() as block:
            @block.tensor
            def _(pe):
                pe.wait_ge(T.loaded["a1_w"], 16)
                pe.wait_ge(T.loaded["a1_proj"], 16)
                for c in range(2):
                    for half in range(2):
                        cols = slice(half * HALF, (half + 1) * HALF)
                        pe.matmul(T.ps[0:DC, 2 * c + half, :], T.w["a1_w"][:, 0, c * DC:(c + 1) * DC],
                                  T.xT[:, 0, cols], start=True, stop=False)
                        pe.matmul(T.ps[0:DC, 2 * c + half, :], T.w["a1_w"][0:DC, 1, c * DC:(c + 1) * DC],
                                  T.xT[0:DC, 1, cols], start=False, stop=True).then_inc(s_qmm, 1)
                for t in range(NT):
                    if t >= 4:
                        pe.wait_ge(s_v, t - 3)
                    pe.matmul(T.ps[:, 4 + t % 4, 0:D], T.xT[:, 0, t * P:(t + 1) * P], T.w["a1_w"][:, 0, :],
                              start=True, stop=False)
                    pe.matmul(T.ps[:, 4 + t % 4, 0:D], T.xT[0:DC, 1, t * P:(t + 1) * P], T.w["a1_w"][0:DC, 1, :],
                              start=False, stop=True).then_inc(s_vmm, 1)

            @block.scalar
            def _(act):
                for b in range(4):
                    act.wait_ge(s_qmm, b + 1)
                    act.activation(qT[:, b // 2, (b % 2) * HALF:(b % 2 + 1) * HALF], T.ps[0:DC, b, :],
                                   ACT.Copy).then_inc(s_q, 1)
                for t in range(NT):
                    act.wait_ge(s_vmm, t + 1)
                    act.activation(v[:, t, :, 0:W], T.ps[:, 4 + t % 4, 0:D].rearrange("p (h d) -> p h d", h=H),
                                   ACT.Copy).then_inc(s_v, 1)
                act.wait_ge(s_v, NT)

            @block.vector
            def _(dve):
                dve.memset(v[:, :, :, W:W + 1], 1.0).then_inc(s_one, 1)
                for c in range(2):
                    dve.wait_ge(s_q, 2 * c + 2)
                    for j in range(6):
                        dve.tensor_scalar(q_head[:, c, j, :], qT[:, c, :], T.consts[0:DC, C_M16 + j:C_M16 + j + 1],
                                          None, ALU.mult).then_inc(s_qh, 1)
                dve.wait_ge(s_one, 1)
                dve.wait_ge(s_qh, 12)

        def scores(t, g):
            c, j = g // 2, 3 * (g % 2)
            return qT[:, c, t * P:(t + 1) * P], q_head[:, c, j:j + 3, t * P:(t + 1) * P]

        windowed_attention(nc, T, "a1", scores, float(W) ** -0.5,
                           lambda t: T.causal3.unsqueeze(1).to_broadcast([P, 4, 384]),
                           H, W, v, lambda t: t, ctxs)

        s_tp, s_aT, s_mm, s_h = sems(nc, ctx, "a1o", "transposed", "aT", "products", "h")
        norm = Norm(nc, T, ctx, "n3", lambda t: (t, 0), route=T.m1)
        with nc.Block() as block:
            @block.tensor
            def _(pe):
                for t in range(NT):
                    for c in range(2):
                        mm = pe.transpose(T.ps[0:DC, t, c * P:(c + 1) * P], ctxs[:, t, c * DC:(c + 1) * DC], T.ident)
                    mm.then_inc(s_tp, 1)
                for t in range(NT):
                    pe.wait_ge(s_aT, t + 1)
                    pe.matmul(T.ps[:, t, 2 * P:2 * P + D], T.aT[:, 0, t * P:(t + 1) * P], T.w["a1_proj"][:, 0, :],
                              start=True, stop=False)
                    pe.matmul(T.ps[:, t, 2 * P:2 * P + D], T.aT[0:DC, 1, t * P:(t + 1) * P],
                              T.w["a1_proj"][0:DC, 1, :], start=False, stop=True).then_inc(s_mm, 1)
                for t in range(NT):
                    norm.pe(pe, t)
                norm.pe_end(pe)

            @block.gpsimd
            def _(pool):
                for t in range(NT):
                    norm.pool(pool, t)

            @block.scalar
            def _(act):
                for t in range(NT):
                    act.wait_ge(s_tp, t + 1)
                    act.activation(T.aT[0:DC, :, t * P:(t + 1) * P],
                                   T.ps[0:DC, t, 0:2 * P].rearrange("p (c n) -> p c n", c=2),
                                   ACT.Copy).then_inc(s_aT, 1)
                norm.act(act)

            @block.vector
            def _(dve):
                norm.eng = dve
                for t in range(NT):
                    dve.wait_ge(s_mm, t + 1)
                    dve.tensor_tensor(T.h[:, t, :], T.ps[:, t, 2 * P:2 * P + D], T.h[:, t, :],
                                      ALU.add).then_inc(s_h, 1)
                    dve.wait_ge(s_h, t + 1)
                    norm.dve(t)
                norm.dve_end()


def attention2_stage(nc, T, a):
    H, W, M = 4, 24, 64
    first_key_tile = lambda t: min(max(t - 1, 0), NT - 3)
    kind = lambda t: 0 if t == 0 else 2 if t == NT - 1 else 1
    with ExitStack() as ctx:
        sb = lambda n, s: ctx.enter_context(nc.sbuf_tensor(f"a2_{n}", s, F32))
        bias = sb("bias", [P, 3, 4, 384])
        xs = sb("xs", [DC, N_TOK])
        mid = sb("mid", [M, N_TOK])
        pre = sb("pre", [DC, N_TOK])
        qT = sb("qT", [DC, N_TOK])
        k_head = sb("k_head", [DC, H, N_TOK])
        v = sb("v", [P, NT, H, W + 1])
        ctxs = sb("ctxs", [P, NT, DC])
        ctxT = sb("ctxT", [DC, N_TOK])
        gT = T.aT[:, 0, :]
        s_b, s_f, s_xs, s_am, s_a, s_bm, s_p, s_g, s_qm, s_q, s_km, s_k, s_vm, s_v, s_one = sems(
            nc, ctx, "a2p", "bias", "fc1_products", "fc1", "convA_products", "convA", "convB_products",
            "pre", "gelu", "q_products", "q", "k_products", "k_heads", "v_products", "v", "ones")
        with nc.Block() as block:
            @block.sync
            def _(sp):
                sp.dma_start(bias[:, :, :, :].rearrange("p a b c -> p (a b c)"), a["a2_bias"]).then_inc(s_b, 16)
                sp.wait_ge(s_b, 16)

            @block.tensor
            def _(pe):
                for n in ("a2_fc1", "a2_convA", "a2_convB", "a2_qkv", "a2_proj", "a2_fc2", "a2_cols"):
                    pe.wait_ge(T.loaded[n], 16)
                cols = [slice(0, HALF), slice(HALF, N_TOK)]
                for i in range(2):
                    pe.matmul(T.ps[0:DC, i, :], T.w["a2_fc1"][:, 0, :], T.xT[:, 0, cols[i]], start=True, stop=False)
                    pe.matmul(T.ps[0:DC, i, :], T.w["a2_fc1"][0:DC, 1, :], T.xT[0:DC, 1, cols[i]],
                              start=False, stop=True).then_inc(s_f, 1)
                for i in range(2):
                    pe.wait_ge(s_xs, i + 1)
                    pe.matmul(T.ps[0:M, 2 + i, :], T.w["a2_convA"][:, :], xs[:, cols[i]],
                              start=True, stop=True).then_inc(s_am, 1)
                for i in range(2):
                    pe.wait_ge(s_a, i + 1)
                    pe.matmul(T.ps[0:DC, 4 + i, :], T.w["a2_convB"][:, :], mid[:, cols[i]],
                              start=True, stop=True).then_inc(s_bm, 1)
                for i in range(2):
                    pe.wait_ge(s_g, i + 1)
                    pe.matmul(T.ps[0:DC, i, :], T.w["a2_qkv"][:, 0:DC], gT[:, cols[i]],
                              start=True, stop=True).then_inc(s_qm, 1)
                    pe.matmul(T.ps[0:DC, 2 + i, :], T.w["a2_qkv"][:, DC:2 * DC], gT[:, cols[i]],
                              start=True, stop=True).then_inc(s_km, 1)
                for t in range(NT):
                    if t >= 2:
                        pe.wait_ge(s_v, t - 1)
                    pe.matmul(T.ps[:, 6 + t % 2, 0:DC], gT[:, t * P:(t + 1) * P], T.w["a2_qkv"][:, 2 * DC:3 * DC],
                              start=True, stop=True).then_inc(s_vm, 1)

            @block.scalar
            def _(act):
                for i in range(2):
                    act.wait_ge(s_f, i + 1)
                    act.activation(xs[:, i * HALF:(i + 1) * HALF], T.ps[0:DC, i, :], ACT.Copy).then_inc(s_xs, 1)
                for i in range(2):
                    act.wait_ge(s_am, i + 1)
                    act.activation(mid[:, i * HALF:(i + 1) * HALF], T.ps[0:M, 2 + i, :], ACT.Identity,
                                   bias=T.w["a2_cols"][0:M, 0:1]).then_inc(s_a, 1)
                for i in range(2):
                    act.wait_ge(s_p, i + 1)
                    act.activation(T.aT[0:DC, 0, i * HALF:(i + 1) * HALF], pre[:, i * HALF:(i + 1) * HALF],
                                   ACT.Gelu).then_inc(s_g, 1)
                for i in range(2):
                    act.wait_ge(s_qm, i + 1)
                    act.activation(qT[:, i * HALF:(i + 1) * HALF], T.ps[0:DC, i, :], ACT.Copy).then_inc(s_q, 1)
                for t in range(NT):
                    act.wait_ge(s_vm, t + 1)
                    act.activation(v[:, t, :, 0:W], T.ps[:, 6 + t % 2, 0:DC].rearrange("p (h d) -> p h d", h=H),
                                   ACT.Copy).then_inc(s_v, 1)
                act.wait_ge(s_v, NT)

            @block.vector
            def _(dve):
                dve.memset(v[:, :, :, W:W + 1], 1.0).then_inc(s_one, 1)
                for i in range(2):
                    cols = slice(i * HALF, (i + 1) * HALF)
                    dve.wait_ge(s_bm, i + 1)
                    dve.wait_ge(s_xs, i + 1)
                    dve.scalar_tensor_tensor(pre[:, cols], T.ps[0:DC, 4 + i, :], T.w["a2_cols"][:, 1:2], xs[:, cols],
                                             ALU.add, ALU.add).then_inc(s_p, 1)
                for i in range(2):
                    dve.wait_ge(s_km, i + 1)
                    for n in range(H):
                        dve.tensor_scalar(k_head[:, n, i * HALF:(i + 1) * HALF], T.ps[0:DC, 2 + i, :],
                                          T.consts[0:DC, C_M24 + n:C_M24 + n + 1], None, ALU.mult).then_inc(s_k, 1)
                dve.wait_ge(s_k, 2 * H)
                dve.wait_ge(s_one, 1)

        def scores(t, g):
            k0 = first_key_tile(t) * P
            return qT[:, t * P:(t + 1) * P], k_head[:, g, k0:k0 + 384]

        windowed_attention(nc, T, "a2", scores, float(W) ** -0.5, lambda t: bias[:, kind(t), :, :],
                           H, W, v, first_key_tile, ctxs)

        s_tp, s_cT, s_pm, s_pT, s_mm, s_hx, s_h = sems(nc, ctx, "a2o", "transposed", "ctxT", "proj_products",
                                                       "proj", "products", "h_x", "h")
        norm = Norm(nc, T, ctx, "n5", lambda t: (t % 3, 0), reuse=3, route=T.m2)
        with nc.Block() as block:
            @block.tensor
            def _(pe):
                for t in range(NT):
                    mm = pe.transpose(T.ps[0:DC, t // 4, (t % 4) * P:(t % 4 + 1) * P], ctxs[:, t, :], T.ident)
                    if t % 4 == 3:
                        mm.then_inc(s_tp, 1)
                for i in range(2):
                    pe.wait_ge(s_cT, i + 1)
                    pe.matmul(T.ps[0:DC, 2 + i, :], T.w["a2_proj"][:, :], ctxT[:, i * HALF:(i + 1) * HALF],
                              start=True, stop=True).then_inc(s_pm, 1)
                for t in range(NT):
                    pe.wait_ge(s_pT, t // 4 + 1)
                    if t >= 4:
                        pe.wait_ge(s_h, t - 3)
                    pe.matmul(T.ps[:, 4 + t % 4, 0:D], gT[:, t * P:(t + 1) * P], T.w["a2_fc2"][:, :],
                              start=True, stop=True).then_inc(s_mm, 1)
                    if t >= 4:
                        norm.pe(pe, t - 4)
                for t in range(NT - 4, NT):
                    norm.pe(pe, t)
                norm.pe_end(pe)

            @block.gpsimd
            def _(pool):
                for t in range(NT):
                    norm.pool(pool, t)

            @block.scalar
            def _(act):
                for i in range(2):
                    act.wait_ge(s_tp, i + 1)
                    act.activation(ctxT[:, i * HALF:(i + 1) * HALF], T.ps[0:DC, i, :], ACT.Copy).then_inc(s_cT, 1)
                for i in range(2):
                    act.wait_ge(s_pm, i + 1)
                    act.activation(T.aT[0:DC, 0, i * HALF:(i + 1) * HALF], T.ps[0:DC, 2 + i, :], ACT.Identity,
                                   bias=T.w["a2_cols"][:, 2:3]).then_inc(s_pT, 1)
                norm.act(act)

            @block.vector
            def _(dve):
                dve.tensor_tensor(T.h[:, :, :], T.h[:, :, :], T.xn[:, :, :], ALU.add).then_inc(s_hx, 1)
                dve.wait_ge(s_hx, 1)
                norm.eng = dve
                for t in range(NT):
                    dve.wait_ge(s_mm, t + 1)
                    dve.tensor_tensor(T.h[:, t, :], T.ps[:, 4 + t % 4, 0:D], T.h[:, t, :],
                                      ALU.add).then_inc(s_h, 1)
                    dve.wait_ge(s_h, t + 1)
                    norm.dve(t)
                norm.dve_end()


class Moe:

    def __init__(self, name, gate_w, experts, picks, logit_bank=0, shared=False, renormalise=False, biased=True):
        self.gate_w, self.logit_bank = gate_w, logit_bank
        self.name, self.E, self.K, self.shared, self.renormalise = name, experts, picks, shared, renormalise
        self.biased = biased
        self.C = picks
        most = (N_TOK * self.C + experts * (P - 1)) // P
        self.tiles = -(-most // 4) * 4


class ExpertWeights:

    def __init__(self, nc, ctx, m, arrays):
        self.m, self.arrays = m, arrays
        self.bufs = [ctx.enter_context(nc.sbuf_tensor(f"{m.name}e_w{n}", [w.shape[1], U, w.shape[2]], F32))
                     for n, w in enumerate(arrays)]
        self.s_in = [sems(nc, ctx, f"{m.name}e_w{n}", *[f"in{u}" for u in range(U)]) for n in range(len(arrays))]

    def load(self, sp, n, tile, u, s_used=None, times=None):
        expert = sp.value_load(self.m.expert_of[0:1, tile], min_val=0, max_val=self.m.E - 1)
        if s_used is not None:
            sp.wait_ge(s_used, times)
        sp.dma_start(self.bufs[n][:, u, :], self.arrays[n][bass.ds(expert, 1), :, :].rearrange("a p n -> p (a n)")
                     ).then_inc(self.s_in[n][u], 16)

    def load_first(self, sp):
        for u in range(U):
            for n in range(len(self.arrays)):
                self.load(sp, n, slice(u, u + 1), u)


def route_stage(nc, T, m, weights, meanwhile=None):
    meanwhile = meanwhile or {}
    E, K, C, name = m.E, m.K, m.C, m.name
    with ExitStack() as ctx:
        sb = lambda n, s, dt=F32: ctx.enter_context(nc.sbuf_tensor(f"{name}r_{n}", s, dt))
        logit = sb("logit", [P, NT, E])
        prob = sb("prob", [P, NT, E])
        small = sb("small", [P, 3, NT])
        best = sb("best", [P, NT, 8])
        best_at = sb("best_at", [P, NT, 8], U32)
        best_f = sb("best_f", [P, NT, 8])
        pick = sb("pick", [P, C, NT, E])
        taken = sb("taken", [P, NT, E])
        goes_on = sb("goes_on", [P, E, NT])
        sums = sb("sums", [P, 1 + E * NT])
        before = sums[:, 0:E * NT].rearrange("p (e t) -> p e t", t=NT)
        n_tiles = sb("n_tiles", [P, E])
        more = sb("more", [P, E, NT])
        ends = sb("ends", [P, E])
        zeros = sb("zeros", [P, E])
        start = sb("start", [P, E])
        slot = sb("slot", [P, NT, E])
        slot_of = sb("slot_of", [P, C, NT, E])
        slot_f = sb("slot_f", [P, C, NT])
        past = sb("past", [1, m.tiles, E])
        map_f = sb("map_f", [1, m.tiles + 1])
        round_used = sb("round_used", [1, m.tiles // U])
        s_c, s_sh, s_e, s_tk, s_rk, s_sl, s_map = sems(
            nc, ctx, f"{name}r", "chain", "shifted", "exps", "taken", "ranks", "slots", "experts")
        iota = T.consts[:, C_IOTA:C_IOTA + E]
        over_tiles = lambda x: x.unsqueeze(1).to_broadcast([P, NT, E])
        over_experts = lambda x: x.unsqueeze(2).to_broadcast([P, NT, E])
        with nc.Block() as block:
            @block.tensor
            def _(pe):
                if meanwhile:
                    meanwhile["pe_first"](pe)
                pe.wait_ge(s_tk, 1)
                both = taken[:, :, :].rearrange("p t e -> p (t e)")
                pe.matmul(T.ps[:, 1, 0:NT * E], T.consts[:, C_LT:C_LT + P], both, start=True, stop=True)
                pe.matmul(T.ps[:, 2, 0:NT * E], T.ones[:, :], taken[:, :, :].rearrange("p t e -> p e t"),
                          start=True, stop=True).then_inc(s_rk, 1)
                if meanwhile:
                    meanwhile["pe"](pe)

            @block.scalar
            def _(act):
                act.wait_ge(s_sh, 1)
                act.activation(prob[:, :, :], logit[:, :, :], ACT.Exp).then_inc(s_e, 1)
                if meanwhile:
                    meanwhile["act"](act)

            @block.sync
            def _(sp):
                if meanwhile:
                    meanwhile["sync"](sp)
                sp.wait_ge(s_map, 1)
                weights.load_first(sp)

            @block.vector
            def _(dve):
                chain = Chain(dve, s_c)
                logits = T.ps[:, m.logit_bank, 0:NT * E].rearrange("p (t e) -> p t e", e=E)
                if m.shared:
                    chain(dve.tensor_copy(logit[:, :, :], logits))
                    chain(dve.memset(logit[:, :, 0:1], -1.0e9))
                    logits = logit[:, :, :]
                chain(dve.tensor_reduce(small[:, 0, :], logits, AX_X, ALU.max))
                dve.tensor_tensor(logit[:, :, :], logits, over_experts(small[:, 0, :]),
                                  ALU.subtract).then_inc(s_sh, 1)
                dve.memset(zeros[:, :], 0.0)
                chain(dve.memset(goes_on[:, :, :], 1.0))
                chain(dve.memset(goes_on[:, :, 0:1], 0.0))
                dve.wait_ge(s_e, 1)
                chain(dve.tensor_reduce(small[:, 1, :], prob[:, :, :], AX_X, ALU.add))
                chain(dve.reciprocal(small[:, 2, :], small[:, 1, :]))
                chain(dve.tensor_tensor(prob[:, :, :], prob[:, :, :], over_experts(small[:, 2, :]), ALU.mult))
                for t in range(NT):
                    ins = dve.max(best[:, t, :], prob[:, t, :])
                chain(ins)
                for t in range(NT):
                    ins = dve.max_index(best_at[:, t, :], best[:, t, :], prob[:, t, :])
                chain(ins)
                chain(dve.tensor_copy(best_f[:, :, :], best_at[:, :, :]))
                for k in range(K):
                    chain(dve.tensor_tensor(pick[:, k, :, :], over_tiles(iota), over_experts(best_f[:, :, k]),
                                            ALU.is_equal))
                chain(dve.tensor_tensor(taken[:, :, :], pick[:, 0, :, :], pick[:, 1, :, :], ALU.add))
                for k in range(2, C):
                    chain(dve.tensor_tensor(taken[:, :, :], taken[:, :, :], pick[:, k, :, :], ALU.add))
                dve.sem_inc(s_tk, 1)
                dve.wait_ge(s_rk, 1)
                chain(dve.tensor_tensor_scan(sums[:, 1:], goes_on[:, :, :].rearrange("p e t -> p (e t)"),
                                             T.ps[:, 2, 0:NT * E], 0.0, ALU.mult, ALU.add))
                chain(dve.tensor_scalar(n_tiles[:, :], sums[:, NT::NT], 1.0 / P, None, ALU.mult))
                dve.memset(before[:, :, 0:1], 0.0)
                chain(dve.tensor_tensor(more[:, :, :], n_tiles[:, :].unsqueeze(2).to_broadcast([P, E, NT]),
                                        T.consts[:, C_IOTA:C_IOTA + NT].unsqueeze(1).to_broadcast([P, E, NT]),
                                        ALU.is_gt))
                chain(dve.tensor_reduce(n_tiles[:, :], more[:, :, :], AX_X, ALU.add))
                chain(dve.tensor_tensor_scan(ends[:, :], n_tiles[:, :], zeros[:, :], 0.0, ALU.add, ALU.add))
                chain(dve.tensor_tensor(start[:, :], ends[:, :], n_tiles[:, :], ALU.subtract))
                chain(dve.tensor_scalar(start[:, :], start[:, :], float(P), None, ALU.mult))
                chain(dve.tensor_tensor(slot[:, :, :], T.ps[:, 1, 0:NT * E].rearrange("p (t e) -> p t e", e=E),
                                        before.rearrange("p e t -> p t e"), ALU.add))
                chain(dve.tensor_tensor(slot[:, :, :], slot[:, :, :], over_tiles(start[:, :]), ALU.add))
                chain(dve.tensor_tensor(slot_of[:, :, :, :].rearrange("p c t e -> p c (t e)"),
                                        pick[:, :, :, :].rearrange("p c t e -> p c (t e)"),
                                        slot[:, :, :].rearrange("p t e -> p (t e)").unsqueeze(1)
                                        .to_broadcast([P, C, NT * E]), ALU.mult))
                chain(dve.tensor_reduce(slot_f[:, :, :].rearrange("p c t -> p (c t)"),
                                        slot_of[:, :, :, :].rearrange("p c t e -> p (c t) e"), AX_X, ALU.add))
                dve.tensor_copy(m.slots[:, :, :], slot_f[:, :, :]).then_inc(s_sl, 1)
                chain(dve.tensor_tensor(past[:, :, :],
                                        T.consts[0:1, C_IOTA:C_IOTA + m.tiles].unsqueeze(2)
                                        .to_broadcast([1, m.tiles, E]),
                                        ends[0:1, :].unsqueeze(1).to_broadcast([1, m.tiles, E]), ALU.is_ge))
                chain(dve.tensor_reduce(map_f[:, 0:m.tiles], past[:, :, :], AX_X, ALU.add))
                chain(dve.tensor_scalar(map_f[:, 0:m.tiles], map_f[:, 0:m.tiles], float(E - 1), None, ALU.min))
                chain(dve.tensor_scalar(round_used[:, :], T.consts[0:1, C_IOTA:C_IOTA + m.tiles // U], float(U),
                                        ends[0:1, E - 1:E], ALU.mult, ALU.is_lt))
                chain(dve.tensor_reduce(map_f[:, m.tiles:m.tiles + 1], round_used[:, :], AX_X, ALU.add))
                dve.tensor_copy(m.expert_of[:, :], map_f[:, :]).then_inc(s_map, 1)
                for k in range(K):
                    chain(dve.tensor_copy(m.gate[:, k, :], best[:, :, k]))
                if m.renormalise:
                    chain(dve.tensor_tensor(small[:, 0, :], m.gate[:, 0, :], m.gate[:, 1, :], ALU.add))
                    chain(dve.tensor_scalar(small[:, 0, :], small[:, 0, :], 1.0e-20, None, ALU.add))
                    chain(dve.reciprocal(small[:, 1, :], small[:, 0, :]))
                    for k in range(K):
                        chain(dve.tensor_tensor(m.gate[:, k, :], m.gate[:, k, :], small[:, 1, :], ALU.mult))
                if m.biased:
                    for k in range(C):
                        weighted = m.gates[:, :, :] if k == 0 else slot_of[:, k, :, :]
                        chain(dve.tensor_tensor(weighted, pick[:, k, :, :], over_experts(m.gate[:, k, :]), ALU.mult))
                        if k:
                            chain(dve.tensor_tensor(m.gates[:, :, :], m.gates[:, :, :], weighted, ALU.add))
                    if m.shared:
                        chain(dve.tensor_scalar(m.gates[:, :, 0:1], m.gates[:, :, 0:1], 1.0, None, ALU.add))
                if meanwhile:
                    meanwhile["dve"](dve)

            @block.gpsimd
            def _(pool):
                pool.wait_ge(s_sl, 1)
                pool.wait_ge(T.s_cleared, 32)
                for t in range(NT):
                    for k in range(C):
                        pool.indirect_dma_start(
                            T.slots_x, bass.IndirectOffsetOnAxis(m.slots[:, k, t:t + 1], 0),
                            T.xn[:, t, :], None).then_inc(m.s_scattered, 16)
                pool.wait_ge(m.s_scattered, 16 * NT * C)


def combine_stage(nc, T, m, norm_name, plus_x, bias=None, rms_weight=None):
    E = m.E
    with ExitStack() as ctx:
        y = ctx.enter_context(nc.sbuf_tensor(f"{m.name}c_y", [P, NT, m.C, D], F32))
        s_c, s_h = sems(nc, ctx, f"{m.name}c", "chain", "h")
        norm = Norm(nc, T, ctx, norm_name, lambda t: (2 + t % 2, 0), reuse=2, rms_weight=rms_weight)
        if bias is not None:
            b = ctx.enter_context(nc.sbuf_tensor(f"{m.name}c_b", [E, D], F32))
            gatesT = ctx.enter_context(nc.sbuf_tensor(f"{m.name}c_gatesT", [E, N_TOK], F32))
            s_b, s_tp, s_gT, s_bm = sems(nc, ctx, f"{m.name}b", "bias", "transposed", "gatesT", "bias_products")
        with nc.Block() as block:
            if bias is not None:
                @block.sync
                def _(sp):
                    sp.dma_start(b[:, :], bias).then_inc(s_b, 16)

            @block.tensor
            def _(pe):
                if bias is not None:
                    for t in range(NT):
                        mm = pe.transpose(T.ps[0:E, t // 4, (t % 4) * P:(t % 4 + 1) * P], m.gates[:, t, :], T.ident)
                        if t % 4 == 3:
                            mm.then_inc(s_tp, 1)
                    pe.wait_ge(s_b, 16)
                    for t in range(NT):
                        pe.wait_ge(s_gT, t // 4 + 1)
                        if t >= 4:
                            pe.wait_ge(s_h, t - 3)
                        pe.matmul(T.ps[:, 4 + t % 4, 0:D], gatesT[:, t * P:(t + 1) * P], b[:, :],
                                  start=True, stop=True).then_inc(s_bm, 1)
                for t in range(NT):
                    norm.pe(pe, t)
                norm.pe_end(pe)

            @block.scalar
            def _(act):
                if bias is not None:
                    for i in range(2):
                        act.wait_ge(s_tp, i + 1)
                        act.activation(gatesT[:, i * HALF:(i + 1) * HALF], T.ps[0:E, i, :], ACT.Copy).then_inc(s_gT, 1)
                norm.act(act)

            @block.gpsimd
            def _(pool):
                for t in range(NT):
                    for k in range(m.C):
                        pool.indirect_dma_start(
                            y[:, t, k, :], None, T.slots_y,
                            bass.IndirectOffsetOnAxis(m.slots[:, k, t:t + 1], 0)).then_inc(m.s_gathered[t], 16)
                    if t >= 3:
                        norm.pool(pool, t - 3)
                    if t >= 6:
                        norm.pool_rms(pool, t - 6)
                for t in range(NT - 3, NT):
                    norm.pool(pool, t)
                    norm.pool_rms(pool, t - 3)
                for t in range(NT - 3, NT):
                    norm.pool_rms(pool, t)

            @block.vector
            def _(dve):
                chain = Chain(dve, s_c)
                if plus_x:
                    chain(dve.tensor_tensor(T.h[:, :, :], T.h[:, :, :], T.xn[:, :, :], ALU.add))
                norm.eng = dve
                if bias is not None:
                    for t in range(NT):
                        dve.wait_ge(s_bm, t + 1)
                        dve.tensor_tensor(T.h[:, t, :], T.ps[:, 4 + t % 4, 0:D], T.h[:, t, :],
                                          ALU.add).then_inc(s_h, 1)
                    dve.wait_ge(s_h, NT)
                for t in range(NT):
                    dve.wait_ge(m.s_gathered[t], 16 * m.C)
                    for k in range(m.C):
                        chain(dve.scalar_tensor_tensor(T.h[:, t, :], y[:, t, k, :], m.gate[:, k, t:t + 1],
                                                       T.h[:, t, :], ALU.mult, ALU.add))
                    norm.dve(t)
                norm.dve_end()


U = 4
LAG = 2


def pipelined(eng, m, steps, at_end=None):
    rounds, least = m.tiles // U, N_TOK * m.C // (P * U)
    used = eng.value_load(m.expert_of[0:1, m.tiles:m.tiles + 1], min_val=least, max_val=rounds)

    def turn(i, q, first_pair=None, last_pair=None):
        for lag, body in steps:
            back, pair = divmod(q - lag, 2)
            if first_pair is not None and q - lag < first_pair or last_pair is not None and q - lag > last_pair:
                continue
            body(eng, Loop(i + back if back else i, isinstance(i, int) and i + back == 0), (2 * pair, 2 * pair + 1))

    for i in range(2):
        for q in range(2):
            turn(i, q, first_pair=-2 * i)
    with eng.Fori(2, rounds) as i:
        with eng.If(i < used):
            for q in range(2):
                turn(i, q)
        with eng.If(i + 1 == used):
            for q in range(2, 2 + LAG):
                turn(i, q, last_pair=1)
            if at_end:
                at_end(i + 1)


class Loop:

    def __init__(self, i, first):
        self.i, self.first = i, first

    def after(self, u, times=1, back=0):
        return self.i * (U * times) + (u + 1 - back) * times


def expert_loop(nc, T, m, weights, layers):
    name = m.name
    with ExitStack() as ctx:
        sb = lambda n, s, dt=F32: ctx.enter_context(nc.sbuf_tensor(f"{name}e_{n}", s, dt))
        x = sb("x", [P, U, D])
        xsT = sb("xsT", [DC + 1, U, 2, P])
        y = sb("y", [P, U, D])
        s_x = sems(nc, ctx, f"{name}e", *[f"x{u}" for u in range(U)])
        s_out = m.s_stored
        s_tp, s_xs, s_1, s_ymm, s_y, s_one = sems(
            nc, ctx, f"{name}e", "transposed", "xsT", "layer1", "y_products", "y", "ones")

        def load_x(sp, at, tiles):
            for u in tiles:
                if not at.first:
                    sp.wait_ge(s_tp, at.after(u, back=U))
                sp.dma_start(x[:, u, :], T.slots_x[bass.ds(at.i * (U * P) + u * P, P), :]).then_inc(s_x[u], 16)

        def load_w(n, s_used):
            def load(sp, at, tiles):
                for u in tiles:
                    if not at.first:
                        weights.load(sp, n, bass.ds(at.i * U + u, 1), u, s_used, at.after(u, back=U))
            return load

        def turn_x(pe, at, tiles):
            for u in tiles:
                pe.wait_ge(s_x[u], 16 * (at.i + 1))
                for c in range(2):
                    mm = pe.transpose(T.ps[0:DC, 4 * (u % 2), c * P:(c + 1) * P], x[:, u, c * DC:(c + 1) * DC],
                                      T.ident)
                mm.then_inc(s_tp, 1)

        def copy_x(dve, at, tiles):
            for u in tiles:
                dve.wait_ge(s_tp, at.after(u))
                dve.tensor_copy(xsT[0:DC, u, :, :], T.ps[0:DC, 4 * (u % 2), 0:2 * P].rearrange("p (c n) -> p c n", c=2)
                                ).then_inc(s_xs, 1)

        def copy_y(dve, at, tiles):
            for u in tiles:
                dve.wait_ge(s_ymm, at.after(u))
                if not at.first:
                    dve.wait_ge(s_out[u], 16 * at.i)
                dve.tensor_copy(y[:, u, :], T.ps[:, 4 * (u % 2) + 3, 0:D]).then_inc(s_y, 1)

        def store_y(pool, at, tiles):
            for u in tiles:
                pool.wait_ge(s_y, at.after(u))
                pool.dma_start(T.slots_y[bass.ds(at.i * (U * P) + u * P, P), :], y[:, u, :]).then_inc(s_out[u], 16)

        S = dict(xsT=xsT, bufs=weights.bufs, s_w=weights.s_in, s_xs=s_xs, s_1=s_1, s_ymm=s_ymm, s_y=s_y, ctx=ctx,
                 turn_x=turn_x, copy_x=copy_x, copy_y=copy_y, store_y=store_y)
        steps = layers(S)
        with nc.Block() as block:
            @block.sync
            def _(sp):
                loads = [(0, load_x), (0, load_w(0, s_1))]
                pipelined(sp, m, loads + [(1, load_w(n, s_ymm)) for n in range(1, len(weights.bufs))])

            @block.gpsimd
            def _(pool):
                def all_stored(rounds):
                    for u in range(U):
                        pool.wait_ge(s_out[u], rounds * 16)
                pipelined(pool, m, steps["pool"], all_stored)

            @block.tensor
            def _(pe):
                pipelined(pe, m, steps["pe"])

            @block.vector
            def _(dve):
                dve.memset(xsT[DC:DC + 1, :, 0, :], 1.0).then_inc(s_one, 1)
                dve.wait_ge(s_one, 1)
                steps["dve_first"](dve)
                pipelined(dve, m, steps["dve"])

            @block.scalar
            def _(act):
                pipelined(act, m, steps["act"])


def moe1(nc, T, a):
    m = T.m1
    F, FC = 768, 6
    def layers(S):
        xsT, (w1, w2) = S["xsT"], S["bufs"]
        h1 = S["ctx"].enter_context(nc.sbuf_tensor("m1_h1", [P, U, F], F32))
        s_1, s_g = S["s_1"], sems(nc, S["ctx"], "m1x", "gelu")[0]

        def layer1(pe, at, tiles):
            for u in tiles:
                pe.wait_ge(S["s_xs"], at.after(u))
                pe.wait_ge(S["s_w"][0][u], 16 * (at.i + 1))
                if not (at.first and u < 2):
                    pe.wait_ge(s_g, at.after(u, back=2))
                b = 4 * (u % 2) + 1
                flat = T.ps[:, b:b + 2, :].rearrange("p b n -> p (b n)")
                for j in range(FC):
                    out = flat[:, j * P:(j + 1) * P]
                    pe.matmul(out, w1[:, u, j * P:(j + 1) * P], xsT[:, u, 0, :], start=True, stop=False)
                    mm = pe.matmul(out, w1[0:DC, u, F + j * P:F + (j + 1) * P], xsT[0:DC, u, 1, :],
                                   start=False, stop=True)
                mm.then_inc(s_1, 1)

        def layer2(pe, at, tiles):
            for u in tiles:
                pe.wait_ge(s_g, at.after(u))
                pe.wait_ge(S["s_w"][1][u], 16 * (at.i + 1))
                if not (at.first and u < 2):
                    pe.wait_ge(S["s_y"], at.after(u, back=2))
                out = T.ps[:, 4 * (u % 2) + 3, 0:D]
                for j in range(FC):
                    mm = pe.matmul(out, h1[:, u, j * P:(j + 1) * P], w2[:, u, j * D:(j + 1) * D],
                                   start=(j == 0), stop=(j == FC - 1))
                mm.then_inc(S["s_ymm"], 1)

        def gelu(act, at, tiles):
            for u in tiles:
                act.wait_ge(s_1, at.after(u))
                b = 4 * (u % 2) + 1
                act.activation(h1[:, u, :], T.ps[:, b:b + 2, :].rearrange("p b n -> p (b n)")[:, 0:F],
                               ACT.Gelu).then_inc(s_g, 1)

        return {"pe": [(1, layer1), (0, S["turn_x"]), (2, layer2)], "act": [(1, gelu)],
                "dve": [(0, S["copy_x"]), (2, S["copy_y"])], "pool": [(2, S["store_y"])],
                "dve_first": lambda dve: None}

    with ExitStack() as ctx:
        weights = ExpertWeights(nc, ctx, m, [a["e1_w1"], a["e1_w2"]])
        route_stage(nc, T, m, weights)
        expert_loop(nc, T, m, weights, layers)
    combine_stage(nc, T, m, "n4", plus_x=True, bias=a["e1_w1"][:, DC, F:F + D])


def moe2(nc, T, a):
    m = T.m2
    F, FC, B = 512, 4, 64
    W3 = FC * F
    B2 = W3 + FC * B
    def layers(S):
        xsT, (w1, w23, wl) = S["xsT"], S["bufs"]
        sb = lambda n, s: S["ctx"].enter_context(nc.sbuf_tensor(f"m2_{n}", s, F32))
        h1, h2, z = sb("h1", [P, U, F]), sb("h2", [P, U, F]), sb("z", [B + 1, U, P])
        s_1 = S["s_1"]
        s_g1, s_2, s_g2, s_3, s_z, s_one = sems(nc, S["ctx"], "m2x", "gelu1", "layer2", "gelu2",
                                                     "layer3", "z", "ones")

        def layer1(pe, at, tiles):
            for u in tiles:
                pe.wait_ge(S["s_xs"], at.after(u))
                pe.wait_ge(S["s_w"][0][u], 16 * (at.i + 1))
                for j in range(FC):
                    out = T.ps[:, 4 * (u % 2) + 1, j * P:(j + 1) * P]
                    pe.matmul(out, w1[:, u, j * P:(j + 1) * P], xsT[:, u, 0, :], start=True, stop=False)
                    mm = pe.matmul(out, w1[0:DC, u, F + j * P:F + (j + 1) * P], xsT[0:DC, u, 1, :],
                                   start=False, stop=True)
                mm.then_inc(s_1, 1)

        def layer2(pe, at, tiles):
            for u in tiles:
                pe.wait_ge(s_g1, at.after(u))
                pe.wait_ge(S["s_w"][1][u], 16 * (at.i + 1))
                for j in range(FC):
                    out = T.ps[:, 4 * (u % 2) + 2, j * P:(j + 1) * P]
                    for k in range(FC):
                        mm = pe.matmul(out, w23[:, u, k * F + j * P:k * F + (j + 1) * P],
                                       h1[:, u, k * P:(k + 1) * P], start=(k == 0), stop=(k == FC - 1))
                mm.then_inc(s_2, 1)

        def layer34(pe, at, tiles):
            for u in tiles:
                pe.wait_ge(s_g2, at.after(u, times=FC))
                if not (at.first and u < 2):
                    pe.wait_ge(S["s_y"], at.after(u, back=2))
                for k in range(FC):
                    mm = pe.matmul(T.ps[0:B, 4 * (u % 2) + 3, 384:512], w23[:, u, W3 + k * B:W3 + (k + 1) * B],
                                   h2[:, u, k * P:(k + 1) * P], start=(k == 0), stop=(k == FC - 1))
                mm.then_inc(s_3, 1)
            for u in tiles:
                pe.wait_ge(s_z, at.after(u))
                pe.wait_ge(S["s_w"][2][u], 16 * (at.i + 1))
                pe.matmul(T.ps[:, 4 * (u % 2) + 3, 0:D], z[:, u, :], wl[:, u, 0:D],
                          start=True, stop=True).then_inc(S["s_ymm"], 1)

        def gelu1(act, at, tiles):
            for u in tiles:
                act.wait_ge(s_1, at.after(u))
                act.activation(h1[:, u, :], T.ps[:, 4 * (u % 2) + 1, :], ACT.Gelu).then_inc(s_g1, 1)

        def gelu2(act, at, tiles):
            for u in tiles:
                act.wait_ge(s_2, at.after(u))
                for j in range(FC):
                    act.activation(h2[:, u, j * P:(j + 1) * P], T.ps[:, 4 * (u % 2) + 2, j * P:(j + 1) * P],
                                   ACT.Gelu, bias=w23[:, u, B2 + j:B2 + j + 1]).then_inc(s_g2, 1)

        def add_b3(dve, at, tiles):
            for u in tiles:
                dve.wait_ge(s_3, at.after(u))
                dve.wait_ge(S["s_w"][2][u], 16 * (at.i + 1))
                dve.tensor_scalar(z[0:B, u, :], T.ps[0:B, 4 * (u % 2) + 3, 384:512], wl[0:B, u, D:D + 1], None,
                                  ALU.add).then_inc(s_z, 1)

        def dve_first(dve):
            dve.memset(z[B:B + 1, :, :], 1.0).then_inc(s_one, 1)
            dve.wait_ge(s_one, 1)

        return {"pe": [(2, layer2), (1, layer1), (0, S["turn_x"]), (2, layer34)],
                "act": [(2, gelu2), (1, gelu1)],
                "dve": [(0, S["copy_x"]), (2, add_b3), (2, S["copy_y"])],
                "pool": [(2, S["store_y"])], "dve_first": dve_first}

    with ExitStack() as ctx:
        weights = ExpertWeights(nc, ctx, m, [a["e2_w1"], a["e2_w23"], a["e2_wl"]])
        route_stage(nc, T, m, weights)
        expert_loop(nc, T, m, weights, layers)
    combine_stage(nc, T, m, "n6", plus_x=False, rms_weight=T.w["a3_norm1"])


def shared_expert(nc, T, ctx, e_w1, e_w2, F, FC, LNW, LNB):
    sb = lambda n, s: ctx.enter_context(nc.sbuf_tensor(f"sh_{n}", s, F32))
    w1, w2 = sb("w1", [DC + 1, 2 * F]), sb("w2", [P, e_w2.shape[2]])
    g, hT = sb("g", [P, NT, F]), sb("hT", [P, 2, F])
    stats, mv, var, root, rstd = sb("stats", [P, NT, 6]), sb("mv", [P, NT, 2]), sb("var", [P, NT]), \
        sb("root", [P, NT]), sb("rstd", [P, NT])
    s_w1, s_w2, s_1, s_g, s_c, s_var, s_root, s_n, s_t, s_hT, s_2, s_h = sems(
        nc, ctx, "sh", "w1", "w2", "layer1", "gelu", "chain", "variance", "roots", "normed", "transposed", "hT",
        "layer2", "h")

    def load(sp):
        sp.dma_start(w1[:, :], e_w1[0, :, :]).then_inc(s_w1, 16)
        sp.dma_start(w2[:, :], e_w2[0, :, :]).then_inc(s_w2, 16)

    def layer1(pe):
        pe.wait_ge(s_w1, 16)
        for t in range(NT):
            if t >= 3:
                pe.wait_ge(s_g, t - 2)
            out = T.ps[:, 3 + t % 3, 0:F]
            pe.matmul(out, T.xT[:, 0, t * P:(t + 1) * P], w1[:, 0:F], start=True, stop=False)
            pe.matmul(out, T.xT[0:DC, 1, t * P:(t + 1) * P], w1[0:DC, F:2 * F], start=False, stop=True
                      ).then_inc(s_1, 1)

    def layer2(pe):
        pe.wait_ge(s_w2, 16)
        for t in range(NT + 1):
            if t < NT:
                pe.wait_ge(s_n, t + 1)
                if t >= 2:
                    pe.wait_ge(s_hT, (t - 1) * FC)
                for j in range(FC):
                    mm = pe.transpose(T.ps[:, 4 + t % 2, j * P:(j + 1) * P], g[:, t, j * P:(j + 1) * P], T.ident)
                mm.then_inc(s_t, 1)
            if t:
                n = t - 1
                pe.wait_ge(s_hT, t * FC)
                if n >= 2:
                    pe.wait_ge(s_h, n - 1)
                for j in range(FC):
                    mm = pe.matmul(T.ps[:, 6 + n % 2, 0:D], hT[:, n % 2, j * P:(j + 1) * P], w2[:, j * D:(j + 1) * D],
                                   start=(j == 0), stop=(j == FC - 1))
                mm.then_inc(s_2, 1)

    def activations(act):
        for t in range(NT):
            act.wait_ge(s_1, t + 1)
            act.activation(g[:, t, :], T.ps[:, 3 + t % 3, 0:F], ACT.Gelu).then_inc(s_g, 1)
        act.wait_ge(s_var, 1)
        act.activation(root[:, :], var[:, :], ACT.Sqrt).then_inc(s_root, 1)
        act.wait_ge(s_w2, 16)
        for t in range(NT):
            act.wait_ge(s_t, t + 1)
            if t >= 2:
                act.wait_ge(s_2, t - 1)
            for j in range(FC):
                act.activation(hT[:, t % 2, j * P:(j + 1) * P], T.ps[:, 4 + t % 2, j * P:(j + 1) * P],
                               ACT.Identity, bias=w2[:, LNB + j:LNB + j + 1],
                               scale=w2[:, LNW + j:LNW + j + 1]).then_inc(s_hT, 1)

    def normalise(dve):
        chain = Chain(dve, s_c)
        dve.wait_ge(s_g, NT)
        for t in range(NT):
            ins = dve.bn_stats(stats[:, t, :], g[:, t, :])
        chain(ins)
        for t in range(NT):
            ins = dve.bn_aggr(mv[:, t, :], stats[:, t, :])
        chain(ins)
        dve.tensor_scalar(var[:, :], mv[:, :, 1], 1e-5, None, ALU.add).then_inc(s_var, 1)
        dve.wait_ge(s_root, 1)
        chain(dve.reciprocal(rstd[:, :], root[:, :]))
        for t in range(NT):
            dve.tensor_scalar(g[:, t, :], g[:, t, :], mv[:, t, 0:1], rstd[:, t:t + 1],
                              ALU.subtract, ALU.mult).then_inc(s_n, 1)
        for t in range(NT):
            dve.wait_ge(s_2, t + 1)
            dve.tensor_tensor(T.h[:, t, :], T.ps[:, 6 + t % 2, 0:D], T.h[:, t, :], ALU.add).then_inc(s_h, 1)
        dve.wait_ge(s_h, NT)

    return {"sync": load, "pe_first": layer1, "pe": layer2, "act": activations, "dve": normalise}


def moe0(nc, T, a):
    m = T.m0
    F, FC = 384, 3
    LNW = FC * D
    LNB = LNW + FC

    def layers(S):
        xsT, (w1, w2) = S["xsT"], S["bufs"]
        sb = lambda n, s: S["ctx"].enter_context(nc.sbuf_tensor(f"m0_{n}", s, F32))
        g, gn, hT = sb("g", [P, U, F]), sb("gn", [P, U, F]), sb("hT", [P, U, F])
        stats, mv, rstd, power = sb("stats", [P, U, 6]), sb("mv", [P, U, 2]), sb("rstd", [P, U]), sb("power", [P, 1])
        s_1 = S["s_1"]
        s_g, s_st, s_mv, s_var, s_r, s_n, s_t, s_hT, s_pw, s_waited = sems(
            nc, S["ctx"], "m0x", "gelu", "stats", "moments", "variance", "rstd", "normed", "transposed",
            "hT", "power", "waited")

        def layer1(pe, at, tiles):
            for u in tiles:
                pe.wait_ge(S["s_xs"], at.after(u))
                pe.wait_ge(S["s_w"][0][u], 16 * (at.i + 1))
                out = T.ps[:, 4 * (u % 2) + 1, 0:F]
                pe.matmul(out, xsT[:, u, 0, :], w1[:, u, 0:F], start=True, stop=False)
                pe.matmul(out, xsT[0:DC, u, 1, :], w1[0:DC, u, F:2 * F], start=False, stop=True).then_inc(s_1, 1)

        def turn_h(pe, at, tiles):
            for u in tiles:
                pe.wait_ge(s_n, at.after(u))
                for j in range(FC):
                    mm = pe.transpose(T.ps[:, 4 * (u % 2) + 2, j * P:(j + 1) * P], gn[:, u, j * P:(j + 1) * P], T.ident)
                mm.then_inc(s_t, 1)

        def layer2(pe, at, tiles):
            for u in tiles:
                pe.wait_ge(s_hT, at.after(u, times=FC))
                pe.wait_ge(S["s_w"][1][u], 16 * (at.i + 1))
                if not (at.first and u < 2):
                    pe.wait_ge(S["s_y"], at.after(u, back=2))
                out = T.ps[:, 4 * (u % 2) + 3, 0:D]
                for j in range(FC):
                    mm = pe.matmul(out, hT[:, u, j * P:(j + 1) * P], w2[:, u, j * D:(j + 1) * D],
                                   start=(j == 0), stop=(j == FC - 1))
                mm.then_inc(S["s_ymm"], 1)

        def gelu(act, at, tiles):
            for u in tiles:
                act.wait_ge(s_1, at.after(u))
                act.activation(g[:, u, :], T.ps[:, 4 * (u % 2) + 1, 0:F], ACT.Gelu).then_inc(s_g, 1)

        def scale_h(act, at, tiles):
            for u in tiles:
                act.wait_ge(s_t, at.after(u))
                act.wait_ge(S["s_w"][1][u], 16 * (at.i + 1))
                for j in range(FC):
                    act.activation(hT[:, u, j * P:(j + 1) * P], T.ps[:, 4 * (u % 2) + 2, j * P:(j + 1) * P],
                                   ACT.Identity, bias=w2[:, u, LNB + j:LNB + j + 1],
                                   scale=w2[:, u, LNW + j:LNW + j + 1]).then_inc(s_hT, 1)

        def moments(dve, at, tiles):
            for u in tiles:
                dve.wait_ge(s_g, at.after(u))
                dve.bn_stats(stats[:, u, :], g[:, u, :]).then_inc(s_st, 1)
            for u in tiles:
                wait_alone(dve, s_st, at.after(u), s_waited)
                dve.bn_aggr(mv[:, u, :], stats[:, u, :]).then_inc(s_mv, 1)
            for u in tiles:
                dve.wait_ge(s_mv, at.after(u))
                dve.tensor_scalar(mv[:, u, 1:2], mv[:, u, 1:2], 1e-5, None, ALU.add).then_inc(s_var, 1)

        def normalise(dve, at, tiles):
            for u in tiles:
                dve.wait_ge(s_r, at.after(u))
                dve.tensor_scalar(gn[:, u, :], g[:, u, :], mv[:, u, 0:1], rstd[:, u:u + 1],
                                  ALU.subtract, ALU.mult).then_inc(s_n, 1)

        def inverse_root(pool, at, tiles):
            for u in tiles:
                pool.wait_ge(s_var, at.after(u))
                pool.tensor_tensor(rstd[:, u:u + 1], mv[:, u, 1:2], power[:, :], ALU.pow).then_inc(s_r, 1)

        def dve_first(dve):
            dve.memset(power[:, :], -0.5).then_inc(s_pw, 1)
            dve.wait_ge(s_pw, 1)

        return {"pe": [(2, turn_h), (1, layer1), (0, S["turn_x"]), (2, layer2)],
                "act": [(2, scale_h), (1, gelu)],
                "dve": [(1, moments), (0, S["copy_x"]), (1, normalise), (2, S["copy_y"])],
                "pool": [(1, inverse_root), (2, S["store_y"])], "dve_first": dve_first}

    with ExitStack() as ctx:
        weights = ExpertWeights(nc, ctx, m, [a["e0_w1"], a["e0_w2"]])
        with ExitStack() as inner:
            route_stage(nc, T, m, weights,
                        shared_expert(nc, T, inner, a["e0_w1"], a["e0_w2"], F, FC, LNW, LNB))
        expert_loop(nc, T, m, weights, layers)
    combine_stage(nc, T, m, "n2", plus_x=False, bias=a["e0_w1"][:, DC, F:F + D])


def mixer_stage(nc, T, a):
    H, HD, DI, NS = 6, 64, 384, 8
    LANES = 16 * H
    with ExitStack() as ctx:
        sb = lambda n, s: ctx.enter_context(nc.sbuf_tensor(f"a3_{n}", s, F32))
        vT = sb("vT", [P, 3, N_TOK])
        gate = sb("gate", [P, NT, DI])
        BT = T.xT[0:H * NS, 0, :]
        C_head = sb("C_head", [H * NS, H, N_TOK])
        u = sb("u", [P, NT, DI])
        response = sb("response", [P, NT, H, P])
        params = nc.dram_tensor("a3_params_out", (LANES, 2, SEQ), F32, kind="Internal").ap()
        g_dram = nc.dram_tensor("a3_response_out", (LANES, SEQ, SEQ), F32, kind="Internal").ap()
        blocks = g_dram.rearrange("(r b) tau t -> r tau b t", r=2)
        FIRST, STEPS = (48, 32, 16, 4, 0), (16, 16, 16, 12, 4)
        PARTS = len(FIRST)
        G = [T.aT[0:LANES, k % 2, 0:STEPS[k] * SEQ].rearrange("p (tau t) -> p tau t", t=SEQ) for k in range(PARTS)]
        s_G, = sems(nc, ctx, "a3", "response")
        s_gd = sems(nc, ctx, "a3o", *[f"response_out{k}" for k in range(PARTS)])
        s_rd = sems(nc, ctx, "a3i", *[f"response_in{k}" for k in range(PARTS)])

        def move_part(sp, k):
            steps = slice(FIRST[k], FIRST[k] + STEPS[k])
            sp.wait_ge(s_G, k + 1)
            sp.dma_start(g_dram[:, steps, :], G[k]).then_inc(s_gd[k], 16)
            sp.wait_ge(s_gd[k], 16)
            for r in range(2):
                sp.dma_start(response[r * SEQ + FIRST[k]:r * SEQ + FIRST[k] + STEPS[k], :, :,
                                      r * SEQ:(r + 1) * SEQ].rearrange("p i h t -> p (i h) t"),
                             blocks[r, steps]).then_inc(s_rd[k], 16)


        with ExitStack() as inner:
            sb2 = lambda n, s: inner.enter_context(nc.sbuf_tensor(f"a3p_{n}", s, F32))
            vpad = sb2("vpad", [P, 3, 16, SEQ + 3])
            taps = sb2("taps", [P, 3, 4, P])
            bc = sb2("bc", [P, NT, 96])
            sq = vpad[:, 0, 0:12, 0:SEQ]
            norm = sb2("norm", [P, NT, 12])
            rnorm = sb2("rnorm", [P, NT, 12])
            root = norm
            par = sb2("par", [2 * H, N_TOK])
            p_ad = sb2("p_ad", [LANES, 2, SEQ])
            pa, pd = p_ad[:, 0, :], p_ad[:, 1, :]
            A, d, s, nda, t0, t1, e0, e1 = (
                sb2(n, [LANES, SEQ]) for n in ("A", "d", "s", "nda", "t0", "t1", "e0", "e1"))
            rz = sb2("rz", [LANES, SEQ, SEQ])
            rx = sb2("rx", [LANES, SEQ])
            w = sb2("w", [LANES, SEQ])
            (s_c, s_vm, s_vp, s_pm, s_par, s_pd, s_gm, s_g, s_tap, s_cm, s_v, s_bm, s_bcc, s_n, s_r, s_bn, s_tp,
             s_ev, s_zero, s_um, s_u, s_in, s_ab, s_e, s_l, s_part, s_blank, s_root) = sems(
                nc, inner, "a3p", "chain", "v_products", "v_padded", "param_products", "params", "params_out",
                "gate_products", "gate", "taps", "conv_products", "v", "bc_products", "bc", "norms", "rnorm",
                "bc_normed", "transposed", "evacuated", "zeros", "u_transposed", "u", "params_in", "abs", "exps",
                "log", "part", "response_blank", "roots")
            with nc.Block() as block:
                @block.tensor
                def _(pe):
                    pe.wait_ge(T.loaded["a3_in"], 16)
                    for half in range(2):
                        cols = slice(half * HALF, (half + 1) * HALF)
                        for c in range(2):
                            mm = pe.matmul(T.ps[0:2 * H, 6 + half, :], T.w["a3_in"][:, c, 2 * DI:], T.xT[0:DC, c, cols],
                                           start=(c == 0), stop=(c == 1))
                        mm.then_inc(s_pm, 1)
                    for j in range(3):
                        for half in range(2):
                            cols = slice(half * HALF, (half + 1) * HALF)
                            for c in range(2):
                                mm = pe.matmul(T.ps[:, 2 * j + half, :], T.w["a3_in"][:, c, DI + j * P:DI + (j + 1) * P],
                                               T.xT[0:DC, c, cols], start=(c == 0), stop=(c == 1))
                            mm.then_inc(s_vm, 1)
                    pe.wait_ge(s_tap, 12)
                    for b in range(6):
                        pe.wait_ge(s_vp, b + 1)
                        j, images = b // 2, slice((b % 2) * 8, (b % 2 + 1) * 8)
                        for k in range(4):
                            mm = pe.matmul(T.ps[:, b, :], taps[:, j, k, :], vpad[:, j, images, k:k + SEQ],
                                           start=(k == 0), stop=(k == 3))
                        mm.then_inc(s_cm, 1)
                    pe.wait_ge(T.loaded["a3_bc"], 16)
                    pe.wait_ge(s_v, 6)
                    for t in range(NT):
                        out = T.ps[:, t // 4, (t % 4) * 96:(t % 4 + 1) * 96]
                        for j in range(3):
                            mm = pe.matmul(out, vT[:, j, t * P:(t + 1) * P], T.w["a3_bc"][:, j, :],
                                           start=(j == 0), stop=(j == 2))
                    mm.then_inc(s_bm, 1)
                    pe.wait_ge(s_par, 2)
                    for t in range(NT):
                        if t >= 2:
                            pe.wait_ge(s_g, t - 1)
                        for c in range(2):
                            mm = pe.matmul(T.ps[:, 6 + t % 2, 0:DI], T.xT[0:DC, c, t * P:(t + 1) * P],
                                           T.w["a3_in"][:, c, 0:DI], start=(c == 0), stop=(c == 1))
                        mm.then_inc(s_gm, 1)
                    for t in range(NT):
                        if t >= 2:
                            pe.wait_ge(s_u, t - 1)
                        elif t == 0:
                            pe.wait_ge(s_g, NT)
                        for j in range(3):
                            mm = pe.transpose(T.ps[:, 6 + t % 2, j * P:(j + 1) * P], vT[:, j, t * P:(t + 1) * P],
                                              T.ident)
                        mm.then_inc(s_um, 1)
                    pe.wait_ge(s_bn, 1)
                    for t in range(NT):
                        for k in range(2):
                            mm = pe.transpose(T.ps[0:48, 2 + 2 * k + t // 4, (t % 4) * P:(t % 4 + 1) * P],
                                              bc[:, t, 48 * k:48 * k + 48], T.ident)
                    mm.then_inc(s_tp, 1)

                @block.scalar
                def _(act):
                    for half in range(2):
                        act.wait_ge(s_pm, half + 1)
                        act.activation(par[:, half * HALF:(half + 1) * HALF], T.ps[0:2 * H, 6 + half, :],
                                       ACT.Copy).then_inc(s_par, 1)
                    act.wait_ge(s_zero, 1)
                    for b in range(6):
                        act.wait_ge(s_vm, b + 1)
                        act.activation(vpad[:, b // 2, (b % 2) * 8:(b % 2 + 1) * 8, 3:],
                                       T.ps[:, b, :].rearrange("p (s n) -> p s n", n=SEQ),
                                       ACT.Copy).then_inc(s_vp, 1)
                        if b == 2:
                            act.wait_ge(s_in, 16)
                            act.activation(e1[:, :], pd, ACT.Exp, scale=-1.0).then_inc(s_e, 1)
                            act.activation(t0[:, :], pa, ACT.Abs).then_inc(s_ab, 1)
                            act.wait_ge(s_ab, 1)
                            act.activation(e0[:, :], t0[:, :], ACT.Exp, scale=-1.0).then_inc(s_e, 1)
                            act.wait_ge(s_e, 2)
                            act.activation(t1[:, :], e0[:, :], ACT.Ln, bias=1.0).then_inc(s_l, 1)
                    for b in range(6):
                        act.wait_ge(s_cm, b + 1)
                        act.activation(vT[:, b // 2, (b % 2) * HALF:(b % 2 + 1) * HALF], T.ps[:, b, :],
                                       ACT.Silu).then_inc(s_v, 1)
                    act.wait_ge(s_bm, 1)
                    for i in range(2):
                        act.activation(bc[:, 4 * i:4 * i + 4, :],
                                       T.ps[:, i, 0:384].rearrange("p (t n) -> p t n", n=96),
                                       ACT.Copy).then_inc(s_bcc, 1)
                    for t in range(NT):
                        act.wait_ge(s_gm, t + 1)
                        act.activation(gate[:, t, :], T.ps[:, 6 + t % 2, 0:DI], ACT.Silu).then_inc(s_g, 1)
                    act.wait_ge(s_n, 1)
                    act.activation(root[:, :, :], norm[:, :, :], ACT.Sqrt).then_inc(s_root, 1)
                    for t in range(NT):
                        act.wait_ge(s_um, t + 1)
                        act.activation(u[:, t, :], T.ps[:, 6 + t % 2, 0:DI], ACT.Copy).then_inc(s_u, 1)
                    act.wait_ge(s_tp, 1)
                    for i in range(2):
                        cols = slice(i * HALF, (i + 1) * HALF)
                        act.activation(BT[:, cols], T.ps[0:48, 2 + i, :], ACT.Copy).then_inc(s_ev, 1)
                        for h in range(H):
                            act.activation(C_head[:, h, cols], T.ps[0:48, 4 + i, :], ACT.Copy,
                                           scale=T.consts[0:48, C_M8 + h:C_M8 + h + 1]).then_inc(s_ev, 1)
                    act.wait_ge(s_ev, 2 * (H + 1))

                @block.sync
                def _(sp):
                    sp.wait_ge(s_par, 2)
                    rows = params.rearrange("(r i h) k t -> r (h k) i t", r=2, h=H)
                    for r in range(2):
                        sp.dma_start(rows[r], par[:, :].rearrange("p (i r t) -> p i r t", i=NT, r=2)[:, :, r, :]
                                     ).then_inc(s_pd, 16)
                    sp.wait_ge(s_pd, 32)
                    sp.dma_start(p_ad[:, :, :], params).then_inc(s_in, 16)
                    sp.wait_ge(s_blank, 1)
                    for k in range(PARTS - 1):
                        move_part(sp, k)

                @block.gpsimd
                def _(pool):
                    pool.wait_ge(T.loaded["a3_conv"], 16)
                    for j in range(3):
                        for k in range(4):
                            pool.tensor_tensor(taps[:, j, k, :], T.ident,
                                               T.w["a3_conv"][:, j, k:k + 1].to_broadcast([P, P]),
                                               ALU.mult).then_inc(s_tap, 1)
                    pool.memset(response[:, :, :, :], 0.0).then_inc(s_blank, 1)

                    def scaled(k):
                        steps = slice(FIRST[k], FIRST[k] + STEPS[k])
                        pool.wait_ge(s_part, k + 1)
                        if k >= 2:
                            pool.wait_ge(s_gd[k - 2], 16)
                        pool.tensor_tensor(G[k], rz[:, steps, :],
                                           d[:, steps].unsqueeze(2).to_broadcast([LANES, STEPS[k], SEQ]),
                                           ALU.mult).then_inc(s_G, 1)

                    scaled(0)
                    scaled(1)
                    scaled(2)
                    pool.wait_ge(s_r, 1)
                    grouped = bc[:, :, :].rearrange("p t (g n) -> p (t g) n", n=NS)
                    pool.tensor_tensor(grouped, grouped,
                                       rnorm[:, :, :].rearrange("p t g -> p (t g)").unsqueeze(2)
                                       .to_broadcast([P, NT * 12, NS]), ALU.mult).then_inc(s_bn, 1)
                    scaled(3)
                    scaled(4)

                @block.vector
                def _(dve):
                    chain = Chain(dve, s_c)
                    dve.memset(vpad[:, :, :, 0:3], 0.0).then_inc(s_zero, 1)
                    dve.memset(rz[:, :, :], 0.0)
                    chain(dve.memset(rx[:, :], 1.0))
                    dve.wait_ge(s_in, 16)
                    dve.wait_ge(s_e, 1)
                    chain(dve.tensor_scalar(d[:, :], e1[:, :], 1.0, None, ALU.add))
                    chain(dve.reciprocal(d[:, :], d[:, :]))
                    dve.wait_ge(s_l, 1)
                    chain(dve.scalar_tensor_tensor(A[:, :], pa, 0.0, t1[:, :], ALU.max, ALU.add))
                    chain(dve.scalar_tensor_tensor(nda[:, :], A[:, :], -1.0, d[:, :], ALU.mult, ALU.mult))
                    chain(dve.scalar_tensor_tensor(s[:, :], nda[:, :], -1.0, d[:, :], ALU.mult, ALU.mult))
                    chain(dve.tensor_scalar(s[:, :], s[:, :], 1.0, None, ALU.add))
                    chain(dve.reciprocal(s[:, :], s[:, :]))
                    chain(dve.tensor_tensor(nda[:, :], nda[:, :], s[:, :], ALU.mult))
                    chain(dve.tensor_scalar(w[:, SEQ - 1:], rx[:, SEQ - 1:], d[:, SEQ - 1:SEQ], None, ALU.mult))
                    for tau in range(SEQ - 1, -1, -1):
                        col = lambda x: x[:, tau:tau + 1]
                        steps = [dve.tensor_scalar(rz[:, tau, tau:], w[:, tau:], col(s), None, ALU.mult)]
                        if tau:
                            steps.append(dve.scalar_tensor_tensor(rx[:, tau:], w[:, tau:], col(nda), rx[:, tau:],
                                                                  ALU.mult, ALU.add))
                        chain(*steps)
                        if tau in FIRST:
                            dve.sem_inc(s_part, 1)
                        if tau:
                            chain(dve.scalar_tensor_tensor(w[:, tau - 1:], rx[:, tau - 1:], d[:, tau - 1:tau],
                                                           rz[:, tau, tau - 1:], ALU.mult, ALU.add))
                        if tau == 8:
                            dve.wait_ge(s_root, 1)
                            dve.reciprocal(rnorm[:, :, :], root[:, :, :]).then_inc(s_r, 1)
                        if tau == 24:
                            dve.wait_ge(s_bcc, 2)
                            flat = bc[:, :, :].rearrange("p t n -> p (t n)").rearrange("p (a b) -> p a b", b=SEQ)
                            chain(dve.tensor_tensor(sq, flat, flat, ALU.mult))
                            chain(dve.tensor_reduce(norm[:, :, :].rearrange("p t g -> p (t g)")
                                                    .rearrange("p (a g) -> p a g", g=SEQ // NS),
                                                    sq.rearrange("p a (g n) -> p a g n", n=NS),
                                                    AX_X, ALU.add))
                            dve.tensor_scalar(norm[:, :, :], norm[:, :, :], 1e-12, None, ALU.add).then_inc(s_n, 1)

        with ExitStack() as inner:
            sb2 = lambda n, s: inner.enter_context(nc.sbuf_tensor(f"a3y_{n}", s, F32))
            mixT = sb2("mixT", [P, 2, H * P])
            skip = sb2("skip", [P, NT, DI])
            gated = sb2("gated", [P, 2, DI])
            gatedT = sb2("gatedT", [P, 2, DI])
            square, ms, rrms, xr = sb2("square", [P, D]), sb2("ms", [P, NT]), sb2("rrms", [P, NT]), sb2("xr", [P, 2, D])
            s_c, s_b, s_m, s_y, s_sk, s_gt, s_t, s_gT, s_o, s_x, s_sq, s_ms, s_rrms, s_xr, s_xt, s_xT = sems(
                nc, inner, "a3y", "chain", "bc_products", "mix", "y_products", "skip", "gated", "transposed",
                "gatedT", "products", "x", "squares", "mean_square", "rrms", "x_scaled", "x_transposed", "xT")
            with nc.Block() as block:
                @block.sync
                def _(sp):
                    move_part(sp, PARTS - 1)
                    sp.wait_ge(s_rd[PARTS - 1], 32)

                @block.tensor
                def _(pe):
                    def cb(t):
                        if t >= 1:
                            pe.wait_ge(s_m, 2 * t)
                        for q in range(2):
                            mm = pe.matmul(T.ps[:, q, 0:3 * P], BT[:, t * P:(t + 1) * P],
                                           C_head[:, 3 * q:3 * q + 3, t * P:(t + 1) * P], start=True, stop=True)
                        mm.then_inc(s_b, 1)

                    pe.wait_ge(T.loaded["a3_out"], 16)
                    def y(t):
                        pe.wait_ge(s_m, 2 * (t + 1))
                        if t >= 2:
                            pe.wait_ge(s_gt, t - 1)
                        for h in range(H):
                            mm = pe.matmul(T.ps[:, 2 + t % 2, h * HD:(h + 1) * HD],
                                           mixT[:, t % 2, h * P:(h + 1) * P], u[:, t, h * HD:(h + 1) * HD],
                                           start=True, stop=True)
                        mm.then_inc(s_y, 1)

                    def turn(t):
                        pe.wait_ge(s_gt, t + 1)
                        if t >= 2:
                            pe.wait_ge(s_gT, t - 1)
                        for j in range(3):
                            mm = pe.transpose(T.ps[:, 4 + t % 2, j * P:(j + 1) * P],
                                              gated[:, t % 2, j * P:(j + 1) * P], T.ident)
                        mm.then_inc(s_t, 1)

                    def project(t):
                        pe.wait_ge(s_gT, t + 1)
                        if t >= 2:
                            pe.wait_ge(s_x, t - 1)
                        if t >= 4:
                            pe.wait_ge(s_xT, 2 * (t - 3))
                        for j in range(3):
                            mm = pe.matmul(T.ps[:, 6 + t % 2, 0:D], gatedT[:, t % 2, j * P:(j + 1) * P],
                                           T.w["a3_out"][:, j, :], start=(j == 0), stop=(j == 2))
                        mm.then_inc(s_o, 1)

                    def turn_x(t):
                        pe.wait_ge(s_xr, t + 1)
                        if t >= 2:
                            pe.wait_ge(s_xT, 2 * (t - 1))
                        pe.wait_ge(s_x, min(t + 3, NT))
                        for c in range(2):
                            mm = pe.transpose(T.ps[0:DC, 6 + t % 2, D + c * P:D + (c + 1) * P],
                                              xr[:, t % 2, c * DC:(c + 1) * DC], T.ident)
                        mm.then_inc(s_xt, 1)

                    cb(0)
                    for t in range(NT + 5):
                        if t + 1 < NT:
                            cb(t + 1)
                        if t < NT:
                            y(t)
                        if 0 <= t - 1 < NT:
                            turn(t - 1)
                        if 0 <= t - 2 < NT:
                            project(t - 2)
                        if t >= 5:
                            turn_x(t - 5)

                @block.gpsimd
                def _(pool):
                    pool.wait_ge(T.loaded["a3_skip"], 16)
                    for t in range(NT):
                        pool.tensor_tensor(skip[:, t, :], u[:, t, :], T.w["a3_skip"][:, :], ALU.mult).then_inc(s_sk, 1)
                    for t in range(NT):
                        pool.wait_ge(s_ms, t + 1)
                        pool.tensor_tensor(rrms[:, t:t + 1], ms[:, t:t + 1], T.power[:, 0:1], ALU.pow).then_inc(s_rrms, 1)

                @block.scalar
                def _(act):
                    act.wait_ge(T.loaded["a3_norm1"], 16)
                    act.wait_ge(T.loaded["a3_norm2"], 16)
                    for t in range(NT + 4):
                        if t < NT:
                            act.wait_ge(s_t, t + 1)
                            if t >= 2:
                                act.wait_ge(s_o, t - 1)
                            act.activation(gatedT[:, t % 2, :], T.ps[:, 4 + t % 2, 0:DI], ACT.Copy).then_inc(s_gT, 1)
                        if 0 <= t - 1 < NT:
                            act.wait_ge(s_x, t)
                            if t >= 2:
                                act.wait_ge(s_sq, t - 1)
                            act.activation(square[:, :], T.xn[:, t - 1, :], ACT.Square, scale=float(D) ** -0.5,
                                           accum_out=ms[:, t - 1:t]).then_inc(s_sq, 1)
                        if t >= 4:
                            act.wait_ge(s_xt, t - 3)
                            for c in range(2):
                                act.activation(T.xT[0:DC, c, (t - 4) * P:(t - 3) * P],
                                               T.ps[0:DC, 6 + t % 2, D + c * P:D + (c + 1) * P], ACT.Copy,
                                               scale=T.w["a3_norm2"][:, c:c + 1]).then_inc(s_xT, 1)
                    act.wait_ge(s_xT, 2 * NT)

                @block.vector
                def _(dve):
                    chain = Chain(dve, s_c)

                    def mix(t):
                        dve.wait_ge(s_b, t + 1)
                        if t >= 2:
                            dve.wait_ge(s_y, t - 1)
                        for q in range(2):
                            dve.tensor_tensor(mixT[:, t % 2, 3 * q * P:3 * (q + 1) * P], T.ps[:, q, 0:3 * P],
                                              response[:, t, 3 * q:3 * q + 3, :].rearrange("p h t -> p (h t)"),
                                              ALU.mult).then_inc(s_m, 1)

                    for k in range(PARTS):
                        dve.wait_ge(s_rd[k], 32)
                    mix(0)
                    for t in range(NT + 4):
                        if t + 1 < NT:
                            mix(t + 1)
                        if t < NT:
                            dve.wait_ge(s_y, t + 1)
                            dve.wait_ge(s_sk, t + 1)
                            if t >= 2:
                                dve.wait_ge(s_t, t - 1)
                            chain(dve.tensor_tensor(gated[:, t % 2, :], T.ps[:, 2 + t % 2, 0:DI], skip[:, t, :],
                                                    ALU.add))
                            dve.tensor_tensor(gated[:, t % 2, :], gated[:, t % 2, :], gate[:, t, :],
                                              ALU.mult).then_inc(s_gt, 1)
                        if 0 <= t - 2 < NT:
                            dve.wait_ge(s_o, t - 1)
                            dve.tensor_tensor(T.xn[:, t - 2, :], T.ps[:, 6 + t % 2, 0:D], T.xn[:, t - 2, :],
                                              ALU.add).then_inc(s_x, 1)
                        if 0 <= t - 3 < NT:
                            dve.wait_ge(s_sq, t - 2)
                            dve.tensor_scalar(ms[:, t - 3:t - 2], ms[:, t - 3:t - 2], 1e-6, None,
                                              ALU.add).then_inc(s_ms, 1)
                        if t >= 4:
                            dve.wait_ge(s_rrms, t - 3)
                            if t >= 6:
                                dve.wait_ge(s_xt, t - 5)
                            dve.tensor_scalar(xr[:, t % 2, :], T.xn[:, t - 4, :], rrms[:, t - 4:t - 3], None,
                                              ALU.mult).then_inc(s_xr, 1)

    with ExitStack() as ctx:
        f1 = ctx.enter_context(nc.sbuf_tensor("a3f_f1", [P, 6, N_TOK], F32))
        s_f, s_g, s_o, s_hx, s_h = sems(nc, ctx, "a3f", "ff1", "gelu", "ff2", "h_x", "h")
        norm = Norm(nc, T, ctx, "n7", lambda t: (t % 4, 0), reuse=4, doubled=True)
        with nc.Block() as block:
            @block.tensor
            def _(pe):
                pe.wait_ge(T.loaded["a3_ff1"], 16)
                pe.wait_ge(T.loaded["a3_ff2"], 16)
                for n in range(12):
                    half, j = n // 6, n % 6
                    cols = slice(half * HALF, (half + 1) * HALF)
                    if n >= 4:
                        pe.wait_ge(s_g, n - 3)
                    pe.matmul(T.ps[:, n % 4, :], T.w["a3_ff1"][:, 0, j * P:(j + 1) * P], T.xT[:, 0, cols],
                              start=True, stop=False)
                    pe.matmul(T.ps[:, n % 4, :], T.w["a3_ff1"][0:DC, 1, j * P:(j + 1) * P], T.xT[0:DC, 1, cols],
                              start=False, stop=True).then_inc(s_f, 1)
                for t in range(NT):
                    if t % 4 == 0:
                        pe.wait_ge(s_g, 6 * (t // 4 + 1))
                    if t >= 4:
                        pe.wait_ge(s_h, t - 3)
                    for j in range(6):
                        mm = pe.matmul(T.ps[:, 4 + t % 4, 0:D], f1[:, j, t * P:(t + 1) * P], T.w["a3_ff2"][:, j, :],
                                       start=(j == 0), stop=(j == 5))
                    mm.then_inc(s_o, 1)
                    if t >= 4:
                        norm.pe(pe, t - 4)
                for t in range(NT - 4, NT):
                    norm.pe(pe, t)
                norm.pe_end(pe)

            @block.gpsimd
            def _(pool):
                for t in range(NT):
                    norm.pool(pool, t)

            @block.scalar
            def _(act):
                for n in range(12):
                    act.wait_ge(s_f, n + 1)
                    act.activation(f1[:, n % 6, (n // 6) * HALF:(n // 6 + 1) * HALF], T.ps[:, n % 4, :],
                                   ACT.Gelu_apprx_tanh).then_inc(s_g, 1)
                norm.act(act)

            @block.vector
            def _(dve):
                dve.wait_ge(T.loaded["a3_b2"], 16)
                dve.tensor_tensor(T.h[:, :, :], T.h[:, :, :], T.xn[:, :, :], ALU.add).then_inc(s_hx, 1)
                dve.wait_ge(s_hx, 1)
                dve.tensor_tensor(T.h[:, :, :], T.h[:, :, :], T.w["a3_b2"][:, :].unsqueeze(1).to_broadcast([P, NT, D]),
                                  ALU.add).then_inc(s_hx, 1)
                dve.wait_ge(s_hx, 2)
                norm.eng = dve
                for t in range(NT):
                    dve.wait_ge(s_o, t + 1)
                    dve.tensor_tensor(T.h[:, t, :], T.ps[:, 4 + t % 4, 0:D], T.h[:, t, :], ALU.add).then_inc(s_h, 1)
                    dve.wait_ge(s_h, t + 1)
                    norm.dve(t)
                norm.dve_end()


KNOTS, GRID = 16, 13.0 / 8.0
ROUNDS = KNOTS // 2


class Spline:

    AHEAD = 2

    def __init__(self, nc, ctx, name, slots, size, columns, x_of, centre_of, weights_of, products,
                 by_scalar=(), by_gpsimd=()):
        self.slots, self.x_of, self.centre_of = slots, x_of, centre_of
        self.weights_of, self.products, self.by_scalar, self.by_gpsimd = weights_of, products, by_scalar, by_gpsimd
        sb = lambda n, s: ctx.enter_context(nc.sbuf_tensor(f"{name}_{n}", s, F32))
        self.v = sb("v", [P, slots, size, HALF])
        self.both, self.both3 = sb("both", [P, slots, 2, size * HALF]), sb("both3", [P, slots, 2, size * HALF])
        self.w = sb("w", [P, slots, size, columns])
        self.s_w = sems(nc, ctx, name, *[f"w{u}" for u in range(slots)])
        (self.s_v, self.s_near, self.s_cut, self.s_sq, self.s_cube, self.s_basis, self.s_used, self.s_pool,
         self.s_waited) = sems(nc, ctx, name, "v", "near", "cut", "squares", "cubes", "basis", "used", "pool_cube",
                               "waited")

    def half(self, i):
        return i // ROUNDS if isinstance(i, int) else self.looped

    def count(self, i, u):
        return i * self.slots + u + 1

    def flat_v(self, u):
        return self.v[:, u, :, :].rearrange("p a n -> p (a n)")

    def load(self, sp, i, u):
        if not isinstance(i, int) or i:
            sp.wait_ge(self.s_used, self.count(i - 1, u))
        r = i - ROUNDS * self.half(i)
        sp.dma_start(self.w[:, u, :, :], self.weights_of(r, u).rearrange("a p n -> p a n")).then_inc(self.s_w[u], 16)

    def distance(self, act, i, u):
        if not isinstance(i, int) or i:
            wait_alone(act, self.s_cut, self.count(i - 1, u), self.s_waited)
        r = i - ROUNDS * self.half(i)
        act.activation(self.v[:, u, :, :], self.x_of(self.half(i), u), ACT.Abs, scale=GRID,
                       bias=self.centre_of(r, u)).then_inc(self.s_v, 1)

    def act_start(self, act):
        for u in range(self.AHEAD):
            self.distance(act, 0, u)

    def act(self, act, i, u):
        if u in self.by_scalar:
            act.wait_ge(self.s_near, i * len(self.by_scalar) + self.by_scalar.index(u) + 1)
        act.wait_ge(self.s_cut, self.count(i, u))
        if not isinstance(i, int) or i:
            act.wait_ge(self.s_used, self.count(i - 1, u))
        act.activation(self.both3[:, u, :, :], self.both[:, u, :, :], ACT.Square, scale=6.0 ** -0.5
                       ).then_inc(self.s_sq, 1)
        if u + 1 in self.by_scalar:
            act.wait_ge(self.s_v, self.count(i, u + 1))
            if not isinstance(i, int) or i:
                act.wait_ge(self.s_cube, self.count(i - 1, u + 1))
            act.activation(self.both[:, u + 1, 0, :], self.flat_v(u + 1), ACT.Relu, scale=-1.0, bias=2.0
                           ).then_inc(self.s_near, 1)
        if u + self.AHEAD < self.slots:
            self.distance(act, i, u + self.AHEAD)
        elif not (isinstance(i, int) and i == 2 * ROUNDS - 1):
            self.distance(act, i + 1, u + self.AHEAD - self.slots)

    def cut(self, dve, i, u):
        if not isinstance(i, int) or i:
            dve.wait_ge(self.s_cube, self.count(i - 1, u))
            if u in self.by_gpsimd:
                dve.wait_ge(self.s_pool, i)
        dve.wait_ge(self.s_v, self.count(i, u))
        if u not in self.by_scalar:
            dve.tensor_scalar(self.both[:, u, 0, :], self.flat_v(u), 2.0, -2.0, ALU.min, ALU.add)
        dve.tensor_scalar(self.both[:, u, 1, :], self.flat_v(u), 1.0, -1.0, ALU.min, ALU.add
                          ).then_inc(self.s_cut, 1)

    def dve_start(self, dve):
        for u in range(self.AHEAD):
            self.cut(dve, 0, u)

    def dve(self, dve, i, u):
        near, far = self.both[:, u, 0, :], self.both[:, u, 1, :]
        near3, far3 = self.both3[:, u, 0, :], self.both3[:, u, 1, :]
        dve.wait_ge(self.s_sq, self.count(i, u))
        if u not in self.by_gpsimd:
            dve.tensor_tensor(near3, near3, near, ALU.mult)
        dve.scalar_tensor_tensor(far3, far3, 4.0, far, ALU.mult, ALU.mult).then_inc(self.s_cube, 1)
        if u + self.AHEAD < self.slots:
            self.cut(dve, i, u + self.AHEAD)
        elif not (isinstance(i, int) and i == 2 * ROUNDS - 1):
            self.cut(dve, i + 1, u + self.AHEAD - self.slots)

    def pool(self, pool, i, u):
        near3, far3 = self.both3[:, u, 0, :], self.both3[:, u, 1, :]
        if u in self.by_gpsimd:
            pool.wait_ge(self.s_sq, self.count(i, u))
            pool.tensor_tensor(near3, near3, self.both[:, u, 0, :], ALU.mult).then_inc(self.s_pool, 1)
            pool.wait_ge(self.s_pool, i + 1)
        pool.wait_ge(self.s_cube, self.count(i, u))
        pool.tensor_tensor(near3, far3, near3, ALU.add if u in self.by_scalar else ALU.subtract
                           ).then_inc(self.s_basis, 1)

    def pe(self, pe, i, u):
        pe.wait_ge(self.s_basis, self.count(i, u))
        pe.wait_ge(self.s_w[u], 16 * (i + 1))
        starts = isinstance(i, int) and i % ROUNDS == 0 and u == 0
        stops = isinstance(i, int) and i % ROUNDS == ROUNDS - 1 and u == self.slots - 1
        self.products(pe, self.half(i), self.both3[:, u, 0, :], self.w[:, u, :, :], starts, stops
                      ).then_inc(self.s_used, 1)


def kan_stages(nc, T, a, out):
    HID, HC, HT = 512, 4, NT // 2
    with ExitStack() as ctx:
        sb = lambda n, s: ctx.enter_context(nc.sbuf_tensor(f"kan_{n}", s, F32))
        hid = sb("hid", [P, HC, N_TOK])
        with ExitStack() as inner:
            def products1(pe, half, basis, w, start, stop):
                for j in range(HC):
                    mm = pe.matmul(T.ps[:, 4 * half + j, :], w[:, 0, j * P:(j + 1) * P], basis, start=start, stop=stop)
                return mm

            def products2(pe, half, basis, w, start, stop):
                for c in range(2):
                    for t in range(HT):
                        mm = pe.matmul(T.ps[:, 4 * half + t, 0:D], basis[:, c * HALF + t * P:c * HALF + (t + 1) * P],
                                       w[:, c, :], start=start and c == 0, stop=stop and c == 1)
                return mm

            cols = lambda half: slice(half * HALF, (half + 1) * HALF)
            k1 = Spline(nc, inner, "kan1", 3, 1, HID, lambda half, u: T.x2[:, u:u + 1, cols(half)],
                        lambda r, u: T.consts[:, bass.ds(r + C_K1, 1)],
                        lambda r, u: a["kan_w1"][bass.ds(r * 3 + u, 1), :, :], products1)
            k2 = Spline(nc, inner, "kan2", 4, 2, D, lambda half, u: hid[:, 2 * (u % 2):2 * (u % 2) + 2, cols(half)],
                        lambda r, u: T.consts[:, bass.ds(r * 2 + (C_K2 + u // 2), 1)],
                        lambda r, u: a["kan_w2"][bass.ds(r * 8 + 2 * u, 2), :, :], products2,
                        by_scalar=(3,), by_gpsimd=(1,))
            s_h, s_o, s_stored = sems(nc, inner, "kanf", "hidden", "h", "stored")
            turns = sorted([((u + 0.5) / spline.slots, n, u) for n, spline in enumerate((k1, k2))
                            for u in range(spline.slots)])

            def all_rounds(eng, step1, step2, start1=None, start2=None, hidden=None, output=None):
                nothing = lambda *args: None

                def round1(i):
                    for u in range(k1.slots):
                        step1(eng, i, u)

                def round2(i):
                    for u in range(k2.slots):
                        step2(eng, i, u)

                def both(i1, i2):
                    for _, n, u in turns:
                        if n == 0:
                            step1(eng, i1, u)
                        else:
                            step2(eng, i2, u)

                (start1 or nothing)(eng)
                k1.looped = 0
                round1(0)
                with eng.Fori(1, ROUNDS - 1) as i:
                    round1(i)
                round1(ROUNDS - 1)
                round1(ROUNDS)
                (hidden or nothing)(eng, 0)
                (start2 or nothing)(eng)
                k1.looped, k2.looped = 1, 0
                both(ROUNDS + 1, 0)
                with eng.Fori(1, ROUNDS - 2) as i:
                    both(i + (ROUNDS + 1), i)
                both(2 * ROUNDS - 1, ROUNDS - 2)
                (hidden or nothing)(eng, 1)
                round2(ROUNDS - 1)
                round2(ROUNDS)
                (output or nothing)(eng, 0)
                k2.looped = 1
                with eng.Fori(ROUNDS + 1, 2 * ROUNDS - 1) as i:
                    round2(i)
                round2(2 * ROUNDS - 1)
                (output or nothing)(eng, 1)

            with nc.Block() as block:
                @block.sync
                def _(sp):
                    def output(sp, half):
                        if half == 0:
                            return
                        rows = out.rearrange("(t p) d -> p t d", p=P)
                        for first, last in ((0, HT), (HT, HT + 2), (HT + 2, NT)):
                            sp.wait_ge(s_o, last)
                            sp.dma_start(rows[:, first:last, :], T.h[:, first:last, :]).then_inc(s_stored, 16)
                        sp.wait_ge(s_stored, 3 * 16)
                        sp.wait_ge(T.s_cleared, 32)
                        for loaded in T.loaded.values():
                            sp.wait_ge(loaded, 16)
                    all_rounds(sp, k1.load, k2.load, output=output)

                @block.scalar
                def _(act):
                    def hidden(act, half):
                        act.wait_ge(k1.s_used, k1.count(ROUNDS * (half + 1) - 1, k1.slots - 1))
                        for j in range(HC):
                            act.activation(hid[:, j, cols(half)], T.ps[:, 4 * half + j, :], ACT.Copy).then_inc(s_h, 1)
                        act.wait_ge(s_h, HC * (half + 1))
                    all_rounds(act, k1.act, k2.act, k1.act_start, k2.act_start, hidden=hidden)

                @block.vector
                def _(dve):
                    def output(dve, half):
                        dve.wait_ge(k2.s_used, k2.count(ROUNDS * (half + 1) - 1, k2.slots - 1))
                        for t in range(HT):
                            dve.tensor_tensor(T.h[:, half * HT + t, :], T.ps[:, 4 * half + t, 0:D],
                                              T.h[:, half * HT + t, :], ALU.add).then_inc(s_o, 1)
                        dve.wait_ge(s_o, HT * (half + 1))
                    all_rounds(dve, k1.dve, k2.dve, k1.dve_start, k2.dve_start, output=output)

                @block.gpsimd
                def _(pool):
                    all_rounds(pool, k1.pool, k2.pool)

                @block.tensor
                def _(pe):
                    all_rounds(pe, k1.pe, k2.pe)


def tower(nc, a, out):
    with ExitStack() as ctx, ExitStack() as early:
        T = Tower()
        T.w = {}
        kept = lambda n, s: ctx.enter_context(nc.sbuf_tensor(n, s, F32))
        sb = lambda n, s, dt=F32: early.enter_context(nc.sbuf_tensor(n, s, dt))
        consts = kept("consts", [P, C_N])
        T.consts = consts
        T.ident = consts[:, C_ID:C_ID + P]
        T.block_mask = consts[:, C_BLK:C_BLK + P]
        T.causal3 = consts[:, C_CAU:C_CAU + 3 * P]
        T.h = kept("h", [P, NT, D])
        T.xn = kept("xn", [P, NT, D])
        T.x2 = kept("x2", [P, 3, N_TOK])
        T.xT = T.x2[0:DC + 1, 0:2, :]
        T.aT = sb("aT", [DC + 1, 2, N_TOK])
        T.ones = sb("ones", [P, P])
        T.zeros = sb("zeros", [P, D])
        T.power = sb("power", [P, NT])
        T.ps = ctx.enter_context(nc.psum_tensor("ps", [P, 8, HALF], F32))
        loads = {}
        for name in WEIGHTS:
            src = a[name]
            t = sb(name, list(src.shape))
            T.w[name] = t
            full = t[:, :] if len(src.shape) == 2 else t[:, :, :] if len(src.shape) == 3 else t[:, :, :, :]
            loads[name] = (full, src)
            if name == "tok_b":
                loads["consts"] = (consts[:, :], a["consts"])
        T.loaded = {n: ctx.enter_context(nc.semaphore(f"in_{n}")) for n in loads}
        T.s_cleared = ctx.enter_context(nc.semaphore("cleared"))
        T.m0, T.m1, T.m2 = Moe("m0", "e0_gate", 16, 3, shared=True), Moe("m1", "e1_gate", 16, 2), \
            Moe("m2", "e2_gate", 32, 2, logit_bank=3, renormalise=True, biased=False)
        slots = max(m.tiles for m in (T.m0, T.m1, T.m2)) * P
        T.slots_x = nc.dram_tensor("slots_x_out", (slots, D), F32, kind="Internal").ap()
        T.slots_y = nc.dram_tensor("slots_y_out", (slots, D), F32, kind="Internal").ap()
        for m in (T.m0, T.m1, T.m2):
            m.s_scattered, = sems(nc, ctx, m.name, "scattered")
            m.s_gathered = sems(nc, ctx, m.name, *[f"gathered{t}" for t in range(NT)])
            m.s_stored = sems(nc, ctx, m.name, *[f"stored{u}" for u in range(U)])
            if m.biased:
                m.gates = sb(f"{m.name}_gates", [P, NT, m.E])
            m.gate = sb(f"{m.name}_gate", [P, m.C, NT])
            m.slots = sb(f"{m.name}_slots", [P, m.C, NT], U32)
            m.expert_of = sb(f"{m.name}_expert_of", [1, m.tiles + 1], I32)
        stages = [
            lambda: tokens_stage(nc, T, a["patches"], loads),
            lambda: attention0_stage(nc, T),
            lambda: moe0(nc, T, a),
            lambda: attention1_stage(nc, T),
            lambda: moe1(nc, T, a),
            lambda: attention2_stage(nc, T, a),
            lambda: moe2(nc, T, a),
            lambda: mixer_stage(nc, T, a),
            lambda: (early.close(), kan_stages(nc, T, a, out)),
        ]
        for stage in stages:
            stage()


WEIGHTS = ["tok_w", "tok_b", "a0_w", "e0_gate", "e1_gate", "e2_gate", "a1_w", "a1_proj",
           "a2_fc1", "a2_convA", "a2_convB", "a2_qkv", "a2_proj", "a2_fc2", "a2_cols",
           "a3_in", "a3_conv", "a3_bc", "a3_skip", "a3_out", "a3_norm1", "a3_norm2", "a3_ff1", "a3_ff2", "a3_b2"]


def constants():
    import numpy as np
    c = np.zeros((P, C_N), np.float32)
    row = np.arange(P)
    c[:, C_ID:C_ID + P] = np.eye(P)
    for base, width, n in ((C_M16, 16, 6), (C_M24, 24, 4), (C_M8, 8, 6)):
        for j in range(n):
            c[:, base + j] = row // width == j
    same = row[:, None] // SEQ == row[None, :] // SEQ
    c[:, C_BLK:C_BLK + P] = np.where(same, 0.0, NEG)
    causal = np.where(same & (row[None, :] <= row[:, None]), 0.0, np.where(same, -1.0e10, NEG))
    c[:, C_CAU:C_CAU + 3 * P] = np.tile(causal, 3)
    c[:, C_LT:C_LT + P] = row[None, :] > row[:, None]
    c[:, C_IOTA:C_IOTA + P] = row[None, :]
    c[:, C_K1:C_K1 + 8] = 7.5 - (2 * np.arange(8)[None, :] + row[:, None] // 64)
    c[:, C_K2:C_K2 + 16] = 7.5 - np.arange(16)[None, :]
    return c


def neighbour_bias(rpb):
    import numpy as np
    rows, k = 16, 5
    start = lambda i, n: np.clip(i - k // 2, 0, n - k)
    out = np.full((P, 3, 4, 6, SEQ), NEG, np.float32)
    w = np.arange(SEQ)
    for kind, tile in enumerate((0, 1, NT - 1)):
        key_row0 = 2 * min(max(tile - 1, 0), NT - 3)
        for r in range(2):
            row = 2 * tile + r
            for key_row in range(start(row, rows), start(row, rows) + k):
                for b in range(k):
                    key = start(w, SEQ) + b
                    out[r * SEQ + w, kind, :, key_row - key_row0, key] = rpb[:, key_row - row + k - 1, key - w + k - 1].T
    return out.reshape(P, -1)


def lay_out(x):
    import numpy as np
    f = lambda n: np.asarray(x[n])

    def chunks(w, n):
        return np.ascontiguousarray(w.reshape(n, w.shape[0] // n, -1).transpose(1, 0, 2))

    def with_bias(w, b):
        out = np.zeros((DC + 1, 2, w.shape[1]), np.float32)
        out[0:DC] = chunks(w, 2)
        out[DC, 0] = b
        return out

    def rows(b):
        return np.ascontiguousarray(np.broadcast_to(b, (P, b.shape[0])))

    a = {"consts": constants()}
    p = f("x").reshape(16, 3, 8, 16, 8, 16).transpose(0, 1, 2, 4, 3, 5).reshape(N_TOK, 768)
    a["patches"] = chunks(p.T, 6)
    a["tok_w"] = chunks(f("L0_tok_weight").T, 6)
    a["tok_b"] = rows(f("L0_tok_bias"))
    a["a0_w"] = with_bias(f("L0_attn_W_qkv"), f("L0_attn_b_qkv"))
    a["a1_w"] = with_bias(f("L1_attn_Wqkv_w")[:D].T, f("L1_attn_Wqkv_b")[:D])
    a["a1_proj"] = with_bias(f("L1_attn_Wproj_w").T, f("L1_attn_Wproj_b"))
    a["a2_fc1"] = with_bias(f("L2_attn_fc1_w").T, f("L2_attn_fc1_b"))
    a["a2_convA"] = np.ascontiguousarray(f("L2_attn_convA_w").T)
    a["a2_convB"] = np.ascontiguousarray(f("L2_attn_convB_w").T)
    a["a2_qkv"] = np.concatenate([f("L2_attn_qkv_w").T, f("L2_attn_qkv_b")[None]])
    a["a2_proj"] = np.ascontiguousarray(f("L2_attn_proj_w").T)
    a["a2_fc2"] = np.concatenate([f("L2_attn_fc2_w").T, f("L2_attn_fc2_b")[None]])
    a["a2_cols"] = np.zeros((DC, 3), np.float32)
    a["a2_cols"][0:64, 0] = f("L2_attn_convA_b")
    a["a2_cols"][:, 1] = f("L2_attn_convB_b")
    a["a2_cols"][:, 2] = f("L2_attn_proj_b")
    a["a2_bias"] = neighbour_bias(f("L2_attn_rpb"))

    def experts_with_bias(w, b, b2=None):
        e, _, n = w.shape
        out = np.zeros((e, DC + 1, 2, n), np.float32)
        out[:, 0:DC] = w.reshape(e, 2, DC, n).transpose(0, 2, 1, 3)
        out[:, DC, 0] = b
        if b2 is not None:
            out[:, DC, 1, 0:D] = b2
        return out.reshape(e, DC + 1, 2 * n)

    def expert_chunks(w):
        e, k, n = w.shape
        return np.ascontiguousarray(w.reshape(e, k // P, P, n).transpose(0, 2, 1, 3).reshape(e, P, -1))

    a["e0_gate"] = with_bias(f("L0_ffn_gate_w"), f("L0_ffn_gate_b"))
    a["e1_gate"] = with_bias(f("L1_ffn_Wr").T, np.zeros(16, np.float32))
    a["e2_gate"] = with_bias(f("L2_ffn_gate_w").T, np.zeros(32, np.float32))
    a["e0_w1"] = experts_with_bias(f("L0_ffn_fc1_w"), f("L0_ffn_fc1_b"), f("L0_ffn_fc2_b"))
    a["e0_w2"] = np.concatenate([expert_chunks(f("L0_ffn_fc2_w")), expert_chunks(f("L0_ffn_ln_w")[:, :, None]),
                                 expert_chunks(f("L0_ffn_ln_b")[:, :, None])], axis=2)
    a["e1_w1"] = experts_with_bias(f("L1_ffn_W1"), f("L1_ffn_b1"), f("L1_ffn_b2"))
    a["e1_w2"] = expert_chunks(f("L1_ffn_W2"))
    a["e2_w1"] = experts_with_bias(f("L2_ffn_W1"), f("L2_ffn_b1"))
    a["e2_w23"] = np.concatenate([expert_chunks(f("L2_ffn_W2")), expert_chunks(f("L2_ffn_W3")),
                                  expert_chunks(f("L2_ffn_b2")[:, :, None])], axis=2)
    a["e2_wl"] = np.zeros((32, 65, D + 1), np.float32)
    a["e2_wl"][:, 0:64, 0:D] = f("L2_ffn_Wl")
    a["e2_wl"][:, 64, 0:D] = f("L2_ffn_bl")
    a["e2_wl"][:, 0:64, D] = f("L2_ffn_b3")
    a["a3_in"] = chunks(f("L3_attn_w_in"), 2)
    a["a3_conv"] = chunks(f("L3_attn_conv_w"), 3)
    w_bc = f("L3_attn_w_bc").reshape(384, 6, 2, 8).transpose(0, 2, 1, 3).reshape(384, 96)
    a["a3_bc"] = chunks(w_bc, 3)
    a["a3_skip"] = rows(np.repeat(f("L3_attn_D_skip"), 64))
    a["a3_out"] = chunks(f("L3_attn_w_out"), 3)
    a["a3_norm1"] = np.ascontiguousarray(f("L3_attn_norm1_w").reshape(2, DC).T)
    a["a3_norm2"] = np.ascontiguousarray(f("L3_attn_norm2_w").reshape(2, DC).T)
    a["a3_ff1"] = with_bias(f("L3_attn_ff_w1"), f("L3_attn_ff_b1"))
    a["a3_ff2"] = chunks(f("L3_attn_ff_w2"), 6)
    a["a3_b2"] = rows(f("L3_attn_ff_b2"))
    a["kan_w1"] = np.ascontiguousarray(f("L3_ffn_w1").reshape(512, 3, 64, 8, 2).transpose(3, 1, 4, 2, 0)
                                       .reshape(24, P, 512))
    a["kan_w2"] = np.ascontiguousarray(f("L3_ffn_w2").reshape(D, 4, P, 16).transpose(3, 1, 2, 0).reshape(64, P, D))
    return a


def kernel(**inputs):
    import numpy as np
    import concourse.bacc as bacc
    from concourse.bass_utils import run_bass_kernel_spmd

    nc = bacc.Bacc("TRN2", target_bir_lowering=False, num_devices=1)
    arrays = {f"in_{name}": np.ascontiguousarray(x) for name, x in lay_out(inputs).items()}
    args = {name[3:]: nc.dram_tensor(name, x.shape, mybir.dt.from_np(x.dtype), kind="ExternalInput").ap()
            for name, x in arrays.items()}
    out = nc.dram_tensor("out", (N_TOK, D), F32, kind="ExternalOutput").ap()
    tower(nc, args, out)
    result = run_bass_kernel_spmd(nc, [arrays], core_ids=[0]).results[0]["out"]
    return result.reshape(16, SEQ, D)
```
